# Optimizing a Trainium2 kernel written in Bass

```python
import numpy as np
import jax
import jax.numpy as jnp

def _softmax(x, axis=-1):
    return jax.nn.softmax(x, axis=axis)

def _gelu(x):
    return jax.nn.gelu(x, approximate=True)

def _silu(x):
    return jax.nn.silu(x)

def _sigmoid(x):
    return jax.nn.sigmoid(x)

def _layernorm(x, axis=-1, eps=1e-05):
    m = jnp.mean(x, axis=axis, keepdims=True)
    v = jnp.var(x, axis=axis, keepdims=True)
    return (x - m) / jnp.sqrt(v + eps)

def _scatter_add(tgt, idx, src, axis=0):
    return tgt.at[idx].add(src)

def _segment_sum(src, seg, n):
    return jax.ops.segment_sum(src, seg, n)
kernel_name = 'mk_seq_postln_d2_jaxref_r8_0c1aa6'

def setup_inputs(seed: int=0):
    np.random.seed(seed)
    _w = jnp.asarray

    def _L0_attn_setup():
        import jax, jax.numpy as jnp
        import numpy as np
        D_CONV = 4
        CHUNK = 64

        def segsum(x):
            T = x.shape[-1]
            strict = jnp.tril(jnp.ones((T, T), dtype=bool), -1)
            xr = jnp.where(strict, x[..., :, None], 0.0)
            x_segsum = jnp.cumsum(xr, axis=-2)
            return jnp.where(jnp.tril(jnp.ones((T, T), dtype=bool)), x_segsum, -jnp.inf)

        def ssd(x, A, B, C, chunk):
            b, s, h, p = x.shape
            c = s // chunk
            x = x.reshape(b, c, chunk, h, p)
            B = B.reshape(b, c, chunk, h, -1)
            C = C.reshape(b, c, chunk, h, -1)
            A = A.reshape(b, c, chunk, h).transpose(0, 3, 1, 2)
            A_cumsum = jnp.cumsum(A, axis=-1)
            L = jnp.exp(segsum(A))
            Y_diag = jnp.einsum('bclhn,bcshn,bhcls,bcshp->bclhp', C, B, L, x)
            decay_states = jnp.exp(A_cumsum[..., -1:] - A_cumsum)
            states = jnp.einsum('bclhn,bhcl,bclhp->bchpn', B, decay_states, x)
            states = jnp.concatenate([jnp.zeros_like(states[:, :1]), states], axis=1)
            A_last = jnp.pad(A_cumsum[..., -1], ((0, 0), (0, 0), (1, 0)))
            decay_chunk = jnp.exp(segsum(A_last))
            states = jnp.einsum('bhzc,bchpn->bzhpn', decay_chunk, states)[:, :-1]
            Y_off = jnp.einsum('bclhn,bchpn,bhcl->bclhp', C, states, jnp.exp(A_cumsum))
            return (Y_diag + Y_off).reshape(b, s, h, p)
        key = jax.random.key(seed)
        ks = jax.random.split(key, 6)
        d_model, d_state, d_inner, n_heads = (128, 128, 128, 16)
        d_in_proj = 2 * d_state + d_inner + n_heads
        d_conv_c = 2 * d_state + d_inner
        b, s = (4, 512)

        def xavier(k, shape):
            bnd = float(np.sqrt(6.0 / (shape[0] + shape[1])))
            return jax.random.uniform(k, shape, minval=-bnd, maxval=bnd, dtype=jnp.float32)
        return {'x': jax.random.normal(ks[0], (b, s, d_model), dtype=jnp.float32), 'W_in': xavier(ks[1], (d_in_proj, d_model)), 'conv_w': jax.random.uniform(ks[2], (d_conv_c, D_CONV), minval=-0.8, maxval=0.8, dtype=jnp.float32), 'conv_b': jnp.zeros((d_conv_c,), dtype=jnp.float32), 'A_param': jax.random.uniform(ks[3], (16,), minval=-0.01, maxval=0.01, dtype=jnp.float32), 'dt_bias': jax.random.uniform(ks[4], (16,), minval=-0.1, maxval=0.1, dtype=jnp.float32), 'W_out': xavier(ks[5], (d_model, d_inner))}
    _L0_attn_in = _L0_attn_setup()

    def _L0_ffn_setup():
        import jax, jax.numpy as jnp
        import numpy as np
        EPS = 1e-05

        def _quantize(W):
            gamma = jnp.mean(jnp.abs(W))
            return jnp.clip(jnp.round(W / (gamma + EPS)), -1.0, 1.0)
        key = jax.random.key(seed)
        k_x, k_w1, k_b1, k_w2, k_b2 = jax.random.split(key, 5)
        n_embd = 128
        d_ff = 4 * n_embd
        B, S = (4, 512)
        bound1 = 1.0 / np.sqrt(n_embd)
        bound2 = 1.0 / np.sqrt(d_ff)
        x = jax.random.normal(k_x, (B, S, n_embd), dtype=jnp.float32)
        W1 = jax.random.uniform(k_w1, (d_ff, n_embd), jnp.float32, -bound1, bound1)
        b1 = jax.random.uniform(k_b1, (d_ff,), jnp.float32, -bound1, bound1)
        W2 = jax.random.uniform(k_w2, (n_embd, d_ff), jnp.float32, -bound2, bound2)
        b2 = jax.random.uniform(k_b2, (n_embd,), jnp.float32, -bound2, bound2)
        return {'x': x, 'W1': W1, 'b1': b1, 'W2': W2, 'b2': b2}
    _L0_ffn_in = _L0_ffn_setup()

    def _L1_attn_setup():
        import jax, jax.numpy as jnp
        import numpy as np
        import math
        B, N, D, H = (8, 512, 128, 16)
        DH = D // H
        key = jax.random.key(seed)
        k1, k2, k3, k4 = jax.random.split(key, 4)
        s = 1.0 / math.sqrt(D)
        return {'x': jax.random.normal(k1, (B, N, D), dtype=jnp.float32), 'Wqk': jax.random.normal(k2, (D, D), dtype=jnp.float32) * s, 'Wv': jax.random.normal(k3, (D, D), dtype=jnp.float32) * s, 'Wo': jax.random.normal(k4, (D, D), dtype=jnp.float32) * s, 'tau': jnp.ones((H, 1, 1), dtype=jnp.float32)}
    _L1_attn_in = _L1_attn_setup()

    def _L1_ffn_setup():
        import jax, jax.numpy as jnp
        import numpy as np
        B, S, M, E, DFF = (4, 256, 128, 8, 512)
        CAPACITY_FACTOR = 1.25

        def _top1_gate(tokens, wg, capacity):
            gates = jax.nn.softmax(tokens @ wg)
            expert_idx = jnp.argmax(gates, axis=-1)
            mask1 = jax.nn.one_hot(expert_idx, gates.shape[-1], dtype=gates.dtype)
            pos = jnp.sum(jnp.cumsum(mask1, axis=0) * mask1, axis=-1).astype(jnp.int32) - 1
            keep = (pos < capacity).astype(gates.dtype)
            mask1c = mask1 * keep[:, None]
            gates1 = jnp.sum(gates * mask1c, axis=-1)
            loc_oh = jax.nn.one_hot(pos, capacity, dtype=gates.dtype)
            combine = gates1[:, None, None] * mask1c[:, :, None] * loc_oh[:, None, :]
            dispatch = (combine > 0).astype(tokens.dtype)
            return (combine, dispatch)
        key = jax.random.key(seed)
        k = jax.random.split(key, 5)
        x = jax.random.normal(k[0], (B, S, M), dtype=jnp.float32)
        wg = jax.random.normal(k[1], (M, E), dtype=jnp.float32) * 0.02
        w1 = jax.random.normal(k[2], (E, M, DFF), dtype=jnp.float32) * 0.02
        b1 = jnp.zeros((E, DFF), dtype=jnp.float32)
        w2 = jax.random.normal(k[3], (E, DFF, M), dtype=jnp.float32) * 0.02
        b2 = jnp.zeros((E, M), dtype=jnp.float32)
        return {'x': x, 'wg': wg, 'w1': w1, 'b1': b1, 'w2': w2, 'b2': b2}
    _L1_ffn_in = _L1_ffn_setup()
    _d = {'L0_attn_x': _L0_attn_in['x'], 'L0_attn_W_in': _L0_attn_in['W_in'], 'L0_attn_conv_w': _L0_attn_in['conv_w'], 'L0_attn_conv_b': _L0_attn_in['conv_b'], 'L0_attn_A_param': _L0_attn_in['A_param'], 'L0_attn_dt_bias': _L0_attn_in['dt_bias'], 'L0_attn_W_out': _L0_attn_in['W_out'], 'L0_ffn_W1': _L0_ffn_in['W1'], 'L0_ffn_b1': _L0_ffn_in['b1'], 'L0_ffn_W2': _L0_ffn_in['W2'], 'L0_ffn_b2': _L0_ffn_in['b2'], 'L1_attn_Wqk': _L1_attn_in['Wqk'], 'L1_attn_Wv': _L1_attn_in['Wv'], 'L1_attn_Wo': _L1_attn_in['Wo'], 'L1_attn_tau': _L1_attn_in['tau'], 'L1_ffn_wg': _L1_ffn_in['wg'], 'L1_ffn_w1': _L1_ffn_in['w1'], 'L1_ffn_b1': _L1_ffn_in['b1'], 'L1_ffn_w2': _L1_ffn_in['w2'], 'L1_ffn_b2': _L1_ffn_in['b2']}
    _x0 = _d['L0_attn_x']
    _d['L0_attn_x'] = jax.random.normal(jax.random.fold_in(jax.random.key(seed), 1), (4, 1024, 128), dtype=_x0.dtype)
    del _x0
    return _d

def reference(L0_attn_x, L0_attn_W_in, L0_attn_conv_w, L0_attn_conv_b, L0_attn_A_param, L0_attn_dt_bias, L0_attn_W_out, L0_ffn_W1, L0_ffn_b1, L0_ffn_W2, L0_ffn_b2, L1_attn_Wqk, L1_attn_Wv, L1_attn_Wo, L1_attn_tau, L1_ffn_wg, L1_ffn_w1, L1_ffn_b1, L1_ffn_w2, L1_ffn_b2):

    def _L0_attn_ref(x, W_in, conv_w, conv_b, A_param, dt_bias, W_out):
        import jax, jax.numpy as jnp
        import numpy as np
        D_CONV = 4
        CHUNK = 64

        def segsum(x):
            T = x.shape[-1]
            strict = jnp.tril(jnp.ones((T, T), dtype=bool), -1)
            xr = jnp.where(strict, x[..., :, None], 0.0)
            x_segsum = jnp.cumsum(xr, axis=-2)
            return jnp.where(jnp.tril(jnp.ones((T, T), dtype=bool)), x_segsum, -jnp.inf)

        def ssd(x, A, B, C, chunk):
            b, s, h, p = x.shape
            c = s // chunk
            x = x.reshape(b, c, chunk, h, p)
            B = B.reshape(b, c, chunk, h, -1)
            C = C.reshape(b, c, chunk, h, -1)
            A = A.reshape(b, c, chunk, h).transpose(0, 3, 1, 2)
            A_cumsum = jnp.cumsum(A, axis=-1)
            L = jnp.exp(segsum(A))
            Y_diag = jnp.einsum('bclhn,bcshn,bhcls,bcshp->bclhp', C, B, L, x)
            decay_states = jnp.exp(A_cumsum[..., -1:] - A_cumsum)
            states = jnp.einsum('bclhn,bhcl,bclhp->bchpn', B, decay_states, x)
            states = jnp.concatenate([jnp.zeros_like(states[:, :1]), states], axis=1)
            A_last = jnp.pad(A_cumsum[..., -1], ((0, 0), (0, 0), (1, 0)))
            decay_chunk = jnp.exp(segsum(A_last))
            states = jnp.einsum('bhzc,bchpn->bzhpn', decay_chunk, states)[:, :-1]
            Y_off = jnp.einsum('bclhn,bchpn,bhcl->bclhp', C, states, jnp.exp(A_cumsum))
            return (Y_diag + Y_off).reshape(b, s, h, p)
        b, src_len, d_model = x.shape
        n_heads = A_param.shape[0]
        d_conv_c = conv_w.shape[0]
        d_inner = W_out.shape[1]
        d_state = (d_conv_c - d_inner) // 2
        pad = -src_len % CHUNK
        xs = jnp.pad(x, ((0, 0), (0, pad), (0, 0)))
        s = xs.shape[1]
        proj = xs @ W_in.T
        xBC, dt = (proj[..., :d_conv_c], proj[..., d_conv_c:])
        xp = jnp.pad(xBC, ((0, 0), (D_CONV - 1, 0), (0, 0)))
        conv_out = sum((xp[:, k:k + s, :] * conv_w[:, k] for k in range(D_CONV))) + conv_b
        C_ = conv_out[..., :d_state]
        B_ = conv_out[..., d_state:2 * d_state]
        xin = conv_out[..., 2 * d_state:]
        dt = jax.nn.softplus(dt + dt_bias)
        Ch = C_.reshape(b, s, n_heads, -1)
        Bh = B_.reshape(b, s, n_heads, -1)
        xh = xin.reshape(b, s, n_heads, -1)
        A = A_param * dt
        cumA = jnp.cumsum(A, axis=1)
        norm = (jnp.exp(cumA) * jnp.cumsum(jnp.exp(-cumA), axis=1))[..., None]
        Y = ssd(xh, A, Bh, Ch, CHUNK)
        out = Y[0] / norm
        out = out.reshape(b, s, -1) @ W_out.T
        return out[:, :src_len]

    def _L0_ffn_ref(x, W1, b1, W2, b2):
        import jax, jax.numpy as jnp
        import numpy as np
        EPS = 1e-05

        def _quantize(W):
            gamma = jnp.mean(jnp.abs(W))
            return jnp.clip(jnp.round(W / (gamma + EPS)), -1.0, 1.0)
        Wq1 = _quantize(W1)
        Wq2 = _quantize(W2)
        h = jax.nn.relu(jnp.einsum('bsd,fd->bsf', x, Wq1) + b1)
        out = jnp.einsum('bsf,df->bsd', h, Wq2) + b2
        return out

    def _L1_attn_ref(x, Wqk, Wv, Wo, tau):
        import jax, jax.numpy as jnp
        import numpy as np
        import math
        B, N, D, H = (8, 512, 128, 16)
        DH = D // H
        Bb, Nn, Dd = x.shape
        qk = x @ Wqk
        v = x @ Wv
        qk = jnp.transpose(qk, (0, 2, 1)).reshape(Bb, H, DH, Nn)
        v = jnp.transpose(v, (0, 2, 1)).reshape(Bb, H, DH, Nn)
        dot = jnp.einsum('bhdn,bhen->bhde', qk, qk)
        q2 = jnp.sum(qk * qk, axis=-1)
        logits = 2.0 * dot - q2[..., :, None] - q2[..., None, :]
        logits = logits / jnp.sqrt(jnp.asarray(Nn, dtype=x.dtype))
        logits = logits * tau
        attn = jax.nn.softmax(logits, axis=-1)
        w = jnp.einsum('bhde,bhen->bhdn', attn, v)
        out = jnp.transpose(w.reshape(Bb, Dd, Nn), (0, 2, 1))
        return out @ Wo

    def _L1_ffn_ref(x, wg, w1, b1, w2, b2):
        import jax, jax.numpy as jnp
        import numpy as np
        B, S, M, E, DFF = (4, 256, 128, 8, 512)
        CAPACITY_FACTOR = 1.25

        def _top1_gate(tokens, wg, capacity):
            gates = jax.nn.softmax(tokens @ wg)
            expert_idx = jnp.argmax(gates, axis=-1)
            mask1 = jax.nn.one_hot(expert_idx, gates.shape[-1], dtype=gates.dtype)
            pos = jnp.sum(jnp.cumsum(mask1, axis=0) * mask1, axis=-1).astype(jnp.int32) - 1
            keep = (pos < capacity).astype(gates.dtype)
            mask1c = mask1 * keep[:, None]
            gates1 = jnp.sum(gates * mask1c, axis=-1)
            loc_oh = jax.nn.one_hot(pos, capacity, dtype=gates.dtype)
            combine = gates1[:, None, None] * mask1c[:, :, None] * loc_oh[:, None, :]
            dispatch = (combine > 0).astype(tokens.dtype)
            return (combine, dispatch)
        d_model = x.shape[-1]
        tokens = x.reshape(-1, d_model)
        T = tokens.shape[0]
        num_experts = wg.shape[1]
        capacity = int(CAPACITY_FACTOR * T / num_experts)
        combine, dispatch = _top1_gate(tokens, wg, capacity)
        dispatched = jnp.einsum('sec,sm->ecm', dispatch, tokens)
        h = jax.nn.relu(jnp.einsum('ecm,emf->ecf', dispatched, w1) + b1[:, None, :])
        expert_out = jnp.einsum('ecf,efm->ecm', h, w2) + b2[:, None, :]
        combined = jnp.einsum('sec,ecm->sm', combine, expert_out)
        return combined.reshape(x.shape)
    x = L0_attn_x
    x = _layernorm(x + _L0_attn_ref(x, L0_attn_W_in, L0_attn_conv_w, L0_attn_conv_b, L0_attn_A_param, L0_attn_dt_bias, L0_attn_W_out), axis=-1)
    x = _layernorm(x + _L0_ffn_ref(x, L0_ffn_W1, L0_ffn_b1, L0_ffn_W2, L0_ffn_b2), axis=-1)
    x = _layernorm(x + _L1_attn_ref(x, L1_attn_Wqk, L1_attn_Wv, L1_attn_Wo, L1_attn_tau), axis=-1)
    x = _layernorm(x + _L1_ffn_ref(x, L1_ffn_wg, L1_ffn_w1, L1_ffn_b1, L1_ffn_w2, L1_ffn_b2), axis=-1)
    return x

_drawn_inputs = setup_inputs


def setup_inputs(seed=0):
    import zlib

    import numpy as np

    out = dict(_drawn_inputs(seed))
    spreads = {'L0_attn_conv_b': (0.0, 0.292),
     'L1_attn_tau': (1.0, 0.2),
     'L1_ffn_b1': (0.0, 0.8),
     'L1_ffn_b2': (0.0, 0.575)}
    factors = {'L0_attn_dt_bias': 8.0,
     'L0_ffn_b1': 8.0,
     'L0_ffn_b2': 59.946,
     'L1_ffn_wg': 3.275,
     'L1_ffn_w1': 6.683,
     'L1_ffn_w2': 5.145}
    for name, (base, spread) in spreads.items():
        noise = np.random.default_rng([zlib.crc32(name.encode()), seed]).standard_normal(out[name].shape)
        drawn = base * np.exp(spread * noise) if base else spread * noise
        out[name] = jnp.asarray(drawn.astype(out[name].dtype))
    for name, factor in factors.items():
        out[name] = (out[name] * factor).astype(out[name].dtype)
    return out
```

```python
from contextlib import ExitStack

import concourse.bass as bass
from concourse import mybir

F32 = mybir.dt.float32
F16 = mybir.dt.float16
I32 = mybir.dt.int32
U32 = mybir.dt.uint32
ACT = mybir.ActivationFunctionType
ALU = mybir.AluOpType
AX = mybir.AxisListType.X

P = 128
B, S, D = 4, 1024, 128
H, HD = 16, 8
TAPS = 4
F = 512
FB = F // P
E = 8
TOK = B * S
CAP = int(1.25 * TOK / E)
CT = CAP // P
NT = TOK // P
TPB = S // P
SUP = 4
NS = NT // SUP
ROW = D + 2
EPS = 1e-5
DROP = 8192.0


def build_program(nc, x, W_in, conv_w, conv_b, A_param, dt_bias, W_out, W1, b1, W2, b2,
                  Wqk, Wv, Wo, tau, wg, w1, eb1, w2, eb2, out):
    ctx = ExitStack()
    with ctx:
        def sb(name, shape, dt=F32):
            return ctx.enter_context(nc.sbuf_tensor(name, shape, dt))

        def sem(name):
            return ctx.enter_context(nc.semaphore(name))

        def wait_free(eng, semaphore, count):
            if not isinstance(count, int) or count > 0:
                eng.wait_ge(semaphore, count)

        PS = ctx.enter_context(nc.psum_tensor("PS", [P, 8, 512], F32))

        def bank(n):
            return PS[:, n, :]

        def part(tensor, first, *dims):
            size, names = 1, "abcd"[:len(dims)]
            for d in dims:
                size *= d
            flat = tensor[:, first:first + size]
            if len(dims) == 1:
                return flat
            return flat.rearrange(f"p ({' '.join(names)}) -> p {' '.join(names)}", **dict(zip(names, dims)))

        def pair(n):
            return PS[:, n:n + 2, :].rearrange("p a f -> p (a f)")

        slots = nc.dram_tensor("slots", (E * CAP, ROW), F32, kind="Internal").ap()

        ones = sb("ones", [P, P])
        ident = sb("ident", [P, P])
        upper = sb("upper", [P, P])
        block = sb("block", [P, P])
        ones16 = sb("ones16", [P, 512], F16)
        ident16 = sb("ident16", [P, P], F16)
        upper16 = sb("upper16", [P, P], F16)
        diag8 = sb("diag8", [P, HD])
        selA = sb("selA", [H, B, 2, H])
        selB = sb("selB", [H, B, 2, H])
        tokid = sb("tokid", [P, NT], I32)
        rev8 = sb("rev8", [P, E])
        base8 = sb("base8", [P, E])
        drop8 = sb("drop8", [P, SUP, E])
        sign2 = sb("sign2", [P, SUP + 1, 2])
        eps2 = sb("eps2", [P, SUP + 1, 2])
        epsT = sb("epsT", [P, SUP])
        mhalf = sb("mhalf", [P, SUP + 1])
        empty = sb("empty", [P, ROW])

        xt = sb("xt", [P, NT, D])
        win = sb("win", [P, 3, D])
        windt = sb("windt", [H, D])
        convw = sb("convw", [P, 3, TAPS])
        convb = sb("convb", [P, 3])
        ab = sb("ab", [H, 2])
        wout = sb("wout", [P, D])
        wn = sb("wn", [P, 2, F])
        w1n = part(wn[:, 0, :], 0, FB, D)
        w2n = wn[:, 1, :]
        wqk = sb("wqk", [P, D])
        wv = sb("wv", [P, D])
        wo = sb("wo", [P, D])
        tauc = sb("tauc", [P, 1])
        wgs = sb("wgs", [P, E])
        eb1n = sb("eb1n", [E * FB, P])
        b1r = sb("b1r", [1, F])
        b2r = sb("b2r", [1, D])
        eb2r = sb("eb2r", [1, E * D])

        winT = sb("winT", [P, 3 * D])
        wdtT = sb("wdtT", [P, 2 * H])
        acol = sb("acol", [P, 2])
        nega = sb("nega", [P, 1])
        woutT = sb("woutT", [P, D])
        wvT = sb("wvT", [P, D])
        eb1T = sb("eb1T", [P, E * FB])
        wabs = sb("wabs", [P, 2])
        cut = sb("cut", [P, 2])
        ncut = sb("ncut", [P, 2])
        qpos = sb("qpos", [P, F])
        qneg = sb("qneg", [P, F])
        q16 = sb("q16", [P, 2, F], F16)
        qT = sb("qT", [P, 2, FB, P], F16)
        b1s = sb("b1s", [P, F], F16)
        b2s = sb("b2s", [P, D], F16)
        eb2s = sb("eb2s", [P, E * D], F16)
        tau32 = sb("tau32", [P, 1])

        xT = sb("xT", [P, TOK])
        first = sb("first", [P, 3 * (TAPS - 1 + S) + 3 * S])
        craw = part(first, 0, 3, TAPS - 1 + S)
        conv = part(first, 3 * (TAPS - 1 + S), 3, S)
        work = sb("work", [P, 5, S])
        s1, s2, s3, s4, s5 = (work[:, n, :] for n in range(5))
        cum = sb("cum", [P, S])
        onesS = sb("onesS", [P, S])
        expn = sb("expn", [P, S])
        rT = sb("rT", [P, TPB, P])
        eT = sb("eT", [P, TPB, 2 * H])
        bcx = sb("bcx", [P, 2, 3 * D])
        xp = sb("xp", [P, 2, D])
        zz = sb("zz", [P, 2, 1024])
        cz = sb("cz", [P, 1024])
        yi = sb("yi", [P, D])
        ys = sb("ys", [P, D])
        st = sb("st", [P, D])
        stn = sb("stn", [P, D])
        y0 = sb("y0", [P, TPB, D])

        ld_x = [sem(f"ld_x{b}") for b in range(B)]
        ld_win = sem("ld_win")
        ld_small = sem("ld_small")
        ld_w = sem("ld_w")
        ld_l1 = sem("ld_l1")
        ld_bias = sem("ld_bias")
        k_ones = sem("k_ones")
        k_pool = sem("k_pool")
        k_sel = sem("k_sel")
        k_const = sem("k_const")
        k_empty = sem("k_empty")
        slots_init = sem("slots_init")
        slf_ok = sem("slf_ok")
        slp_ok = sem("slp_ok")
        win_ps = sem("win_ps")
        win_sb = sem("win_sb")
        nega_ok = sem("nega_ok")
        pad_ok = sem("pad_ok")
        xT_ps = sem("xT_ps")
        xT_sb = sem("xT_sb")
        proj_ps = sem("proj_ps")
        proj_sb = sem("proj_sb")
        dt_ps = sem("dt_ps")
        dt_abs = sem("dt_abs")
        dt_ln = sem("dt_ln")
        dve1 = sem("dve1")
        act1 = sem("act1")
        dt_pos = sem("dt_pos")
        cum_ok = sem("cum_ok")
        exp_ok = sem("exp_ok")
        cs_ok = sem("cs_ok")
        lncs_ok = sem("lncs_ok")
        lr_ok = sem("lr_ok")
        r_ok = sem("r_ok")
        e_ps = sem("e_ps")
        e_sb = sem("e_sb")
        r_ps = sem("r_ps")
        r_sb = sem("r_sb")
        conv_ok = sem("conv_ok")
        wabs_ok = sem("wabs_ok")
        wsum_ps = sem("wsum_ps")
        q_ok = sem("q_ok")
        cut_ok = sem("cut_ok")
        cmp_ok = sem("cmp_ok")
        q_ps = sem("q_ps")
        q_sb = sem("q_sb")
        wT_ps = sem("wT_ps")
        wT_sb = sem("wT_sb")
        bias_ok = sem("bias_ok")
        tr_ps = sem("tr_ps")
        tr_sb = sem("tr_sb")
        xp_ok = sem("xp_ok")
        z_ok = sem("z_ok")
        cum_ps = sem("cum_ps")
        cz_ok = sem("cz_ok")
        off_ps = sem("off_ps")
        st_ps = sem("st_ps")
        stn_ok = sem("stn_ok")
        st_ok = sem("st_ok")
        yi_ok = sem("yi_ok")
        ys_ok = sem("ys_ok")
        y0_ok = sem("y0_ok")

        yr = sb("yr", [P, 2, SUP, D])
        yrT = sb("yrT", [P, 512])
        r1 = sb("r1", [P, 512])
        st1 = sb("st1", [P, SUP, 6])
        mv1 = sb("mv1", [P, SUP, 2])
        ln1 = [sb(f"ln1_{n}", [P, SUP, 2]) for n in range(2)]
        rs1 = sb("rs1", [P, SUP])
        nm1 = sb("nm1", [P, SUP])
        x1 = sb("x1", [P, 2, 512])
        x1h = sb("x1h", [P, 2, 512], F16)
        x1l = sb("x1l", [P, 2, 512], F16)
        hh = sb("hh", [P, 2, FB, 512], F16)
        hl = sb("hl", [P, 2, FB, 512], F16)
        r2 = sb("r2", [P, 512])
        st2 = sb("st2", [P, SUP, 6])
        mv2 = sb("mv2", [P, SUP, 2])
        ln2 = [sb(f"ln2_{n}", [P, SUP, 2]) for n in range(2)]
        rs2 = sb("rs2", [P, SUP])
        nm2 = sb("nm2", [P, SUP])
        x2s = sb("x2s", [P, 2, 512])
        x2k = xt[:, :, :].rearrange("p t d -> p (t d)")
        x2T = xT
        gram = sb("gram", [P, B, D])
        yr_ok = sem("yr_ok")
        yrT_ps = sem("yrT_ps")
        yrT_sb = sem("yrT_sb")
        ao_ps = sem("ao_ps")
        r1_ok = sem("r1_ok")
        st1_ok = sem("st1_ok")
        mv1_ok = sem("mv1_ok")
        ln1_step = sem("ln1_step")
        x1_ok = sem("x1_ok")
        x1T_ps = sem("x1T_ps")
        x1h_ok = sem("x1h_ok")
        x1l_ok = sem("x1l_ok")
        h_ps = sem("h_ps")
        hh_ok = sem("hh_ok")
        hl_ok = sem("hl_ok")
        ff_ps = sem("ff_ps")
        r2_ok = sem("r2_ok")
        st2_ok = sem("st2_ok")
        mv2_ok = sem("mv2_ok")
        ln2_step = sem("ln2_step")
        x2_ok = sem("x2_ok")
        x2_kept = [sem("x2_kept0"), sem("x2_kept1")]
        x2T_ps = sem("x2T_ps")
        x2T_sb = sem("x2T_sb")
        gram_sb = sem("gram_sb")

        gq = part(expn, 0, 512)
        dm = sb("dm", [P, B, D])
        dc = sb("dc", [P, B, HD])
        dq = sb("dq", [P, B, HD])
        qc = sb("qc", [P, B])
        lg = sb("lg", [P, B, HD])
        mx = sb("mx", [P, B])
        ea = sb("ea", [P, B, HD])
        ad = sb("ad", [P, B, D])
        p1 = part(expn, 512, 512)
        mix = sb("mix", [P, 512])
        m1_ps = sem("m1_ps")
        m1_sb = sem("m1_sb")
        m2_ps = sem("m2_ps")
        mixs = sem("mixs")
        dq_ok = sem("dq_ok")
        m3_ps = sem("m3_ps")
        lg_ok = sem("lg_ok")
        ea_ok = sem("ea_ok")
        ad_ok = sem("ad_ok")
        m4_ps = sem("m4_ps")
        m4_sb = sem("m4_sb")
        m5_ps = sem("m5_ps")
        mix_ok = sem("mix_ok")

        x2Ts = part(onesS, 0, 2, 512)
        r3 = sb("r3", [P, 512])
        st3 = sb("st3", [P, SUP, 6])
        mv3 = sb("mv3", [P, SUP, 2])
        ln3 = [sb(f"ln3_{n}", [P, SUP, 2]) for n in range(2)]
        rs3 = sb("rs3", [P, SUP])
        nm3 = sb("nm3", [P, SUP])
        sq3 = sb("sq3", [P, SUP])
        lv3 = sb("lv3", [P, SUP])
        s43 = sb("s43", [P, SUP])
        onep = sb("onep", [P, 1])
        zz1 = zz[:, :, :].rearrange("p a f -> p (a f)")
        rows = part(zz1, 0, 2, SUP, ROW)
        x3T = part(zz1, 2 * SUP * ROW, 512)
        x4 = part(cz, 0, 2, 512)
        gmax = sb("gmax", [P, SUP])
        gl = sb("gl", [P, SUP, E])
        ge = sb("ge", [P, SUP, E])
        gs = sb("gs", [P, SUP])
        eqv = sb("eqv", [P, SUP, E])
        vmax = sb("vmax", [P, SUP])
        oh = sb("oh", [P, SUP, E], F16)
        ohs = sb("ohs", [P, E])
        carry = sb("carry", [P, E], F16)
        sl1 = sb("sl1", [P, SUP, E])
        sl2 = sb("sl2", [P, SUP, E])
        slf = sb("slf", [P, SUP])
        slp = sb("slp", [P, SUP])
        slot = sb("slot", [P, 2, SUP], U32)
        staged = [sem("staged0"), sem("staged1")]
        o3_ps = sem("o3_ps")
        r3_ok = sem("r3_ok")
        st3_ok = sem("st3_ok")
        mv3_ok = sem("mv3_ok")
        ln3_step = sem("ln3_step")
        x3_ok = sem("x3_ok")
        x3T_ps = sem("x3T_ps")
        x3T_sb = sem("x3T_sb")
        gate_ps = sem("gate_ps")
        gate_step = sem("gate_step")
        gl_ok = sem("gl_ok")
        ge_ok = sem("ge_ok")
        oh_ok = sem("oh_ok")
        pos_ps = sem("pos_ps")
        slot_ok = sem("slot_ok")
        sl_ok = sem("sl_ok")
        s4_step = sem("s4_step")
        x4_ok = sem("x4_ok")
        stored = [sem("stored0"), sem("stored1")]
        scat = [sem("scat0"), sem("scat1")]
        carry_ok = sem("carry_ok")

        work1 = work[:, :, :].rearrange("p a f -> p (a f)")
        xs = part(first, 0, 2, CT, ROW)
        xr = part(first, 2 * CT * ROW, 2, CT, ROW)
        w1s = part(cum, 0, 2, F)
        w2s = part(wn[:, :, :].rearrange("p a f -> p (a f)"), 0, 2, FB, D)
        xeT = part(xT, 0, 2, CAP)
        eh = part(work1, 0, FB, CAP)
        xr_ok = sem("xr_ok")
        r4 = part(work1, FB * CAP, CT, D)
        st4 = sb("st4", [P, CT, 6])
        mv4 = sb("mv4", [P, CT, 2])
        ln4 = [sb(f"ln4_{n}", [P, CT, 2]) for n in range(2)]
        rs4 = sb("rs4", [P, CT])
        nm4 = sb("nm4", [P, CT])
        y4 = part(work1, (FB + 1) * CAP, 2, CT, D)
        ldw = [sem("ldw0"), sem("ldw1")]
        lds = [sem("lds0"), sem("lds1")]
        xeT_ps = sem("xeT_ps")
        xeT_sb = sem("xeT_sb")
        eh_ps = sem("eh_ps")
        eh_ok = sem("eh_ok")
        ey_ps = sem("ey_ps")
        r4_ok = sem("r4_ok")
        st4_ok = sem("st4_ok")
        mv4_ok = sem("mv4_ok")
        ln4_step = sem("ln4_step")
        y4_ok = sem("y4_ok")
        put = [sem("put0"), sem("put1")]

        block_ = ctx.enter_context(nc.Block())

        @block_.sync
        def _(sp):
            sp.dma_start(win[:, :, :], W_in[0:3 * D, :].rearrange("(g p) d -> p g d", p=P)).then_inc(ld_win, 16)
            sp.dma_start(windt[:, :], W_in[3 * D:3 * D + H, :]).then_inc(ld_win, 16)
            for b in range(B):
                sp.dma_start(xt[:, b * TPB:(b + 1) * TPB, :],
                             x[b].rearrange("(t p) d -> p t d", p=P)).then_inc(ld_x[b], 16)
            sp.dma_start(w1n[:, :, :], W1.rearrange("(k p) d -> p k d", p=P)).then_inc(ld_w, 16)
            sp.dma_start(w2n[:, :], W2).then_inc(ld_w, 16)
            sp.dma_start(wout[:, :], W_out).then_inc(ld_w, 16)
            sp.dma_start(wv[:, :], Wv).then_inc(ld_w, 16)
            sp.dma_start(eb1n[:, :], eb1.rearrange("e (k p) -> (e k) p", p=P)).then_inc(ld_w, 16)
            sp.dma_start(b1r[:, :], b1.rearrange("(o f) -> o f", o=1)).then_inc(ld_bias, 16)
            sp.dma_start(b2r[:, :], b2.rearrange("(o f) -> o f", o=1)).then_inc(ld_bias, 16)
            sp.dma_start(eb2r[:, :], eb2.rearrange("(o e) d -> o (e d)", o=1)).then_inc(ld_bias, 16)
            sp.dma_start(wqk[:, :], Wqk).then_inc(ld_l1, 16)
            sp.dma_start(wo[:, :], Wo).then_inc(ld_l1, 16)
            sp.dma_start(tauc[:, :], tau.rearrange("h a b -> h (a b)").unsqueeze(1).to_broadcast([H, HD, 1])).then_inc(ld_l1, 16)
            sp.dma_start(wgs[:, :], wg).then_inc(ld_l1, 16)
            sp.wait_ge(k_empty, 2)
            sp.dma_start(slots.rearrange("(p t) r -> p t r", p=P),
                         empty[:, :].unsqueeze(1).to_broadcast([P, E * CT, ROW])).then_inc(slots_init, 16)

            def keep_x2(b, c):
                sp.wait_ge(x2_ok, 2 * b + c + 1)
                sp.dma_start(x2k[:, bass.ds(b * 1024 + c * 512, 512)], x2s[:, c, :]).then_inc(x2_kept[c], 16)

            with sp.Fori(0, B) as b:
                keep_x2(b, 0)
                keep_x2(b, 1)

            def load_weights(k, c):
                sp.dma_start(w1s[:, c, :], w1[bass.ds(2 * k + c, 1)].rearrange("e d f -> d (e f)")).then_inc(ldw[c], 16)
                sp.dma_start(w2s[:, c, :, :], w2[bass.ds(2 * k + c, 1)].rearrange("e (k p) d -> p (e k) d", p=P)).then_inc(ldw[c], 16)

            def stage_x2T(b, c):
                sp.dma_start(x2Ts[:, c, :], x2T[:, bass.ds(b * 1024 + c * 512, 512)]).then_inc(staged[c], 16)

            def store_x4(b, c):
                sp.wait_ge(x4_ok, 2 * b + c + 1)
                sp.dma_start(out[bass.ds(b, 1), c * 512:(c + 1) * 512, :].rearrange("b (t p) d -> p (b t) d", p=P),
                             x4[:, c, :].rearrange("p (t d) -> p t d", t=SUP)).then_inc(stored[c], 16)

            load_weights(0, 0)
            load_weights(0, 1)
            sp.wait_ge(x2T_sb, NS)
            stage_x2T(0, 0)
            stage_x2T(0, 1)
            with sp.Fori(0, B - 1) as b:
                sp.wait_ge(o3_ps, 2 * b + 1)
                stage_x2T(b + 1, 0)
                store_x4(b, 0)
                sp.wait_ge(o3_ps, 2 * b + 2)
                stage_x2T(b + 1, 1)
                store_x4(b, 1)
            store_x4(B - 1, 0)
            store_x4(B - 1, 1)

            def load_slots(k, c):
                sp.dma_start(xs[:, c, :, :],
                             slots[bass.ds((2 * k + c) * CAP, CAP), :].rearrange("(t p) r -> p t r", p=P)).then_inc(lds[c], 16)

            for c in range(2):
                sp.wait_ge(scat[c], 16 * SUP * B)
            load_slots(0, 0)
            load_slots(0, 1)
            with sp.Fori(0, E // 2 - 1) as k:
                for c in range(2):
                    sp.wait_ge(xeT_ps, 2 * k + c + 1)
                    sp.wait_ge(xr_ok, 2 * k + c + 1)
                    load_slots(k + 1, c)
                for c in range(2):
                    sp.wait_ge(ey_ps, 2 * k + c + 1)
                    load_weights(k + 1, c)
            for c in range(2):
                sp.wait_ge(put[c], 16 * CT * (E // 2))
                sp.wait_ge(stored[c], 16 * B)

        @block_.gpsimd
        def _(pool):
            pool.memset(ones[:, :], 1.0).then_inc(k_ones, 1)
            pool.wait_ge(k_ones, 1)
            pool.affine_select(out=ident[:, :], in_=ones[:, :], compare_op=ALU.is_equal, fill=0.0, base=0,
                               pattern=[[-1, P]], channel_multiplier=1).then_inc(k_pool, 1)
            pool.affine_select(out=upper[:, :], in_=ones[:, :], compare_op=ALU.is_ge, fill=0.0, base=0,
                               pattern=[[1, P]], channel_multiplier=-1).then_inc(k_pool, 1)
            pool.affine_select(out=block[:, :], in_=ones[:, :], compare_op=ALU.is_ge, fill=0.0, base=0,
                               pattern=[[-HD, H], [0, HD]], channel_multiplier=1).then_inc(k_pool, 1)
            pool.wait_ge(k_pool, 3)
            pool.affine_select(out=block[:, :], in_=block[:, :], compare_op=ALU.is_ge, fill=0.0, base=HD - 1,
                               pattern=[[HD, H], [0, HD]], channel_multiplier=-1).then_inc(k_pool, 1)
            pool.iota(tokid[:, :], pattern=[[P, NT]], base=0, channel_multiplier=1).then_inc(k_pool, 1)
            pool.iota(rev8[:, :], pattern=[[-1, E]], base=E, channel_multiplier=0,
                      allow_small_or_imprecise_dtypes=True).then_inc(k_pool, 1)
            pool.iota(base8[:, :], pattern=[[CAP, E]], base=0, channel_multiplier=0,
                      allow_small_or_imprecise_dtypes=True).then_inc(k_pool, 1)
            pool.memset(ones16[:, :], 1.0).then_inc(k_ones, 1)
            pool.memset(onesS[:, :], 1.0).then_inc(k_ones, 1)
            pool.wait_ge(ld_w, 80)
            pool.wait_ge(cut_ok, 2)
            for n, src in enumerate((w1n[:, :, :].rearrange("p k d -> p (k d)"), w2n[:, :])):
                pool.tensor_scalar(qneg[:, :], src, ncut[:, n:n + 1], None, ALU.is_lt).then_inc(cmp_ok, 1)
                pool.tensor_scalar(qpos[:, :], src, cut[:, n:n + 1], None, ALU.is_gt).then_inc(cmp_ok, 1)
                pool.wait_ge(cmp_ok, 2 * n + 2)
                pool.tensor_tensor(q16[:, n, :], qpos[:, :], qneg[:, :], ALU.subtract).then_inc(q_ok, 1)
                pool.wait_ge(q_ok, n + 1)
            for t in range(TPB):
                c = t % 2
                pool.wait_ge(tr_sb, t + 1)
                if t == 0:
                    pool.wait_ge(e_sb, 1)
                wait_free(pool, st_ps, t - 1)
                pool.tensor_tensor(xp[:, c, :].rearrange("p (h d) -> p h d", h=H),
                                   bcx[:, c, 2 * D:].rearrange("p (h d) -> p h d", h=H),
                                   eT[:, t, 0:H].unsqueeze(2).to_broadcast([P, H, HD]), ALU.mult).then_inc(xp_ok, 1)
                pool.wait_ge(xp_ok, t + 1)
                wait_free(pool, cum_ps, t - 1)
                pool.tensor_tensor(zz[:, c, :].rearrange("p (h d n) -> p h d n", h=H, d=HD),
                                   bcx[:, c, D:2 * D].rearrange("p (h n) -> p h n", h=H).unsqueeze(2).to_broadcast([P, H, HD, HD]),
                                   xp[:, c, :].rearrange("p (h d) -> p h d", h=H).unsqueeze(3).to_broadcast([P, H, HD, HD]),
                                   ALU.mult).then_inc(z_ok, 1)

            def norm_out(b, c):
                if isinstance(b, int) and b == 0:
                    pool.wait_ge(y0_ok, SUP * (c + 1))
                    pool.wait_ge(r_sb, 1)
                wait_free(pool, yrT_ps, 2 * b + c - 1)
                pool.tensor_tensor(yr[:, c, :, :].rearrange("p t (h d) -> p t h d", h=H),
                                   y0[:, SUP * c:SUP * (c + 1), :].rearrange("p t (h d) -> p t h d", h=H),
                                   rT[:, SUP * c:SUP * (c + 1), bass.ds(b * 2 * H, H)].unsqueeze(3).to_broadcast([P, SUP, H, HD]),
                                   ALU.mult).then_inc(yr_ok, 1)

            def rstd(i, mv, mv_ok, ln, ln_step, rs, nm, free):
                pool.wait_ge(mv_ok, i + 1)
                wait_free(pool, free, i)
                pool.tensor_tensor(ln[0][:, :, :], mv[:, :, :], sign2[:, 0:SUP, :], ALU.mult).then_inc(ln_step, 1)
                pool.wait_ge(ln_step, 4 * i + 1)
                pool.tensor_tensor(ln[1][:, :, :], ln[0][:, :, :], eps2[:, 0:SUP, :], ALU.add).then_inc(ln_step, 1)
                pool.wait_ge(ln_step, 4 * i + 2)
                pool.tensor_tensor(rs[:, :], ln[1][:, :, 1], mhalf[:, 0:SUP], ALU.pow).then_inc(ln_step, 1)
                pool.wait_ge(ln_step, 4 * i + 3)
                pool.tensor_tensor(nm[:, :], ln[1][:, :, 0], rs[:, :], ALU.mult).then_inc(ln_step, 1)

            def rstd1(b, c):
                rstd(2 * b + c, mv1, mv1_ok, ln1, ln1_step, rs1, nm1, x1_ok)

            def rstd2(b, c):
                rstd(2 * b + c, mv2, mv2_ok, ln2, ln2_step, rs2, nm2, x2_ok)

            norm_out(0, 0)
            norm_out(0, 1)
            rstd1(0, 0)

            def both(b):
                norm_out(b + 1, 0)
                rstd1(b, 1)
                rstd2(b, 0)
                norm_out(b + 1, 1)
                rstd1(b + 1, 0)
                rstd2(b, 1)

            both(0)
            with pool.Fori(1, B - 1) as b:
                both(b)
            rstd1(B - 1, 1)
            rstd2(B - 1, 0)
            rstd2(B - 1, 1)

            def rstd3(b, c):
                i = 2 * b + c
                pool.wait_ge(mv3_ok, i + 1)
                wait_free(pool, x4_ok, i)
                pool.tensor_tensor(ln3[0][:, :, :], mv3[:, :, :], sign2[:, 0:SUP, :], ALU.mult).then_inc(ln3_step, 1)
                pool.wait_ge(ln3_step, 5 * i + 1)
                pool.tensor_tensor(ln3[1][:, :, :], ln3[0][:, :, :], eps2[:, 0:SUP, :], ALU.add).then_inc(ln3_step, 1)
                pool.wait_ge(ln3_step, 5 * i + 2)
                pool.tensor_tensor(rs3[:, :], ln3[1][:, :, 1], mhalf[:, 0:SUP], ALU.pow).then_inc(ln3_step, 1)
                pool.wait_ge(ln3_step, 5 * i + 3)
                pool.tensor_tensor(nm3[:, :], ln3[1][:, :, 0], rs3[:, :], ALU.mult).then_inc(ln3_step, 1)
                pool.tensor_tensor(sq3[:, :], rs3[:, :], rs3[:, :], ALU.mult).then_inc(ln3_step, 1)

            def scatter(b, c):
                i = 2 * b + c
                wait_free(pool, scat[c], 16 * SUP * b)
                pool.wait_ge(slf_ok, i + 1)
                pool.tensor_tensor(slp[:, :], slf[:, :], ones[:, 0:SUP], ALU.subtract).then_inc(slp_ok, 1)
                pool.wait_ge(k_ones, 3)
                pool.wait_ge(slp_ok, i + 1)
                pool.tensor_copy(slot[:, c, :], slp[:, :]).then_inc(slot_ok, 1)
                pool.wait_ge(slots_init, 16)
                pool.wait_ge(slot_ok, i + 1)
                for j in range(SUP):
                    pool.indirect_dma_start(out=slots, out_offset=bass.IndirectOffsetOnAxis(ap=slot[:, c, j:j + 1], axis=0),
                                            in_=rows[:, c, j, :], in_offset=None,
                                            bounds_check=E * CAP - 1, oob_is_err=False).then_inc(scat[c], 16)

            rstd3(0, 0)
            rstd3(0, 1)
            scatter(0, 0)

            def both(b):
                rstd3(b + 1, 0)
                scatter(b, 1)
                rstd3(b + 1, 1)
                scatter(b + 1, 0)

            both(0)
            with pool.Fori(1, B - 1) as b:
                both(b)
            scatter(B - 1, 1)

            def rstd4(k, c):
                e = 2 * k + c
                pool.wait_ge(mv4_ok, e + 1)
                wait_free(pool, y4_ok, e)
                pool.tensor_tensor(ln4[0][:, :, :], mv4[:, :, :], sign2[:, :, :], ALU.mult).then_inc(ln4_step, 1)
                pool.wait_ge(ln4_step, 4 * e + 1)
                pool.tensor_tensor(ln4[1][:, :, :], ln4[0][:, :, :], eps2[:, :, :], ALU.add).then_inc(ln4_step, 1)
                pool.wait_ge(ln4_step, 4 * e + 2)
                pool.tensor_tensor(rs4[:, :], ln4[1][:, :, 1], mhalf[:, :], ALU.pow).then_inc(ln4_step, 1)
                pool.wait_ge(ln4_step, 4 * e + 3)
                pool.tensor_tensor(nm4[:, :], ln4[1][:, :, 0], rs4[:, :], ALU.mult).then_inc(ln4_step, 1)

            def put_rows(k, c):
                for n in range(2):
                    pool.wait_ge(stored[n], 16 * B)
                pool.wait_ge(y4_ok, 2 * k + c + 1)
                for j in range(CT):
                    pool.indirect_dma_start(out=out.rearrange("b s d -> (b s) d"),
                                            out_offset=bass.IndirectOffsetOnAxis(ap=xr[:, c, j, D + 1:D + 2].bitcast(U32), axis=0),
                                            in_=y4[:, c, j, :], in_offset=None,
                                            bounds_check=TOK - 1, oob_is_err=False).then_inc(put[c], 16)

            rstd4(0, 0)
            with pool.Fori(0, E // 2 - 1) as k:
                rstd4(k, 1)
                put_rows(k, 0)
                rstd4(k + 1, 0)
                put_rows(k, 1)
            rstd4(E // 2 - 1, 1)
            put_rows(E // 2 - 1, 0)
            put_rows(E // 2 - 1, 1)

        @block_.scalar
        def _(act):
            act.dma_start(convw[:, :, :], conv_w.rearrange("(g p) k -> p g k", p=P)).then_inc(ld_small, 16)
            act.dma_start(convb[:, :], conv_b.rearrange("(g p) -> p g", p=P), allow_slow_non_contiguous=True).then_inc(ld_small, 16)
            act.dma_start(ab[:, 0:1], A_param.rearrange("(h o) -> h o", o=1)).then_inc(ld_small, 16)
            act.dma_start(ab[:, 1:2], dt_bias.rearrange("(h o) -> h o", o=1)).then_inc(ld_small, 16)
            nc.scalar.preload_act_table_set("natural_log_exp_and_others")
            act.wait_ge(win_ps, 1)
            nc.scalar.copy(winT[:, :], bank(0)[:, 0:3 * D]).then_inc(win_sb, 1)
            nc.scalar.copy(wdtT[:, :].rearrange("p (a h) -> p a h", a=2),
                           bank(0)[:, 3 * D:3 * D + H].unsqueeze(1).to_broadcast([P, 2, H])).then_inc(win_sb, 1)
            nc.scalar.copy(acol[:, :], bank(0)[:, 3 * D + H:3 * D + H + 2]).then_inc(win_sb, 1)

            def x_out(n):
                act.wait_ge(xT_ps, n + 1)
                nc.scalar.copy(xT[:, n * 512:(n + 1) * 512], bank(1 + n % 2)).then_inc(xT_sb, 1)

            x_out(0)
            x_out(1)
            act.wait_ge(wsum_ps, 1)
            nc.scalar.activation(cut[:, :], bank(7)[:, 0:2], ACT.Copy, scale=0.5 / (F * D), bias=0.5 * EPS).then_inc(cut_ok, 1)
            nc.scalar.activation(ncut[:, :], bank(7)[:, 0:2], ACT.Copy, scale=-0.5 / (F * D), bias=-0.5 * EPS).then_inc(cut_ok, 1)
            for n in range(6):
                act.wait_ge(proj_ps, n + 1)
                if n == 0:
                    act.wait_ge(ld_small, 64)
                nc.scalar.activation(conv[:, n // 2, 512 * (n % 2):512 * (n % 2) + 512], bank(3 + n % 3), ACT.Identity,
                                     scale=convw[:, n // 2, TAPS - 1:TAPS], bias=convb[:, n // 2:n // 2 + 1])
                nc.scalar.copy(craw[:, n // 2, TAPS - 1 + 512 * (n % 2):TAPS - 1 + 512 * (n % 2) + 512],
                               bank(3 + n % 3)).then_inc(proj_sb, 1)
                x_out(2 + n)
            act.wait_ge(dt_ps, NS)
            act.wait_ge(win_sb, 3)
            nc.scalar.activation(s1[:, :], pair(6), ACT.Abs, bias=acol[:, 1:2]).then_inc(dt_abs, 1)
            act.wait_ge(dt_abs, 1)
            nc.scalar.activation(s2[:, :], s1[:, :], ACT.Exp, scale=-1.0).then_inc(act1, 1)
            act.wait_ge(act1, 1)
            nc.scalar.activation(s3[:, :], s2[:, :], ACT.Ln, bias=1.0).then_inc(dt_ln, 1)
            act.wait_ge(wT_ps, 1)
            nc.scalar.copy(woutT[:, :], bank(5)[:, 0:D]).then_inc(wT_sb, 1)
            nc.scalar.copy(wvT[:, :], bank(5)[:, D:2 * D]).then_inc(wT_sb, 1)
            nc.scalar.copy(eb1T[:, :], bank(5)[:, 2 * D:2 * D + E * FB]).then_inc(wT_sb, 1)
            act.wait_ge(cum_ok, 1)
            act.wait_ge(nega_ok, 1)
            nc.scalar.activation(expn[:, :], cum[:, :], ACT.Exp, scale=nega[:, 0:1]).then_inc(exp_ok, 1)
            act.wait_ge(e_ps, 1)
            nc.scalar.copy(eT[:, :, :], bank(3)[:, 0:TPB * 2 * H].rearrange("p (t k) -> p t k", t=TPB)).then_inc(e_sb, 1)

            def chunk_out(t):
                act.wait_ge(tr_ps, t + 1)
                wait_free(act, st_ps, t - 1)
                wait_free(act, z_ok, t - 1)
                wait_free(act, cz_ok, t - 1)
                nc.scalar.copy(bcx[:, t % 2, :], bank(t % 2)[:, 0:3 * D]).then_inc(tr_sb, 1)

            chunk_out(0)
            act.wait_ge(cs_ok, 1)
            nc.scalar.activation(s4[:, :], s5[:, :], ACT.Ln).then_inc(lncs_ok, 1)
            chunk_out(1)
            act.wait_ge(lr_ok, 1)
            nc.scalar.activation(s1[:, :], s2[:, :], ACT.Exp).then_inc(r_ok, 1)
            for t in range(2, TPB):
                chunk_out(t)
            act.wait_ge(q_ps, 1)
            nc.scalar.copy(qT[:, :, :, :].rearrange("p a k f -> p (a k f)"), bank(6).bitcast(F16)).then_inc(q_sb, 1)
            act.wait_ge(r_ps, 1)
            nc.scalar.copy(rT[:, :, :].rearrange("p t k -> p (t k)"), pair(0)).then_inc(r_sb, 1)

            def yrT_out(b, c):
                i = 2 * b + c
                act.wait_ge(yrT_ps, i + 1)
                wait_free(act, ao_ps, i)
                nc.scalar.copy(yrT[:, :], bank(0)).then_inc(yrT_sb, 1)

            def x1_norm(b, c):
                i = 2 * b + c
                act.wait_ge(ln1_step, 4 * i + 4)
                wait_free(act, r2_ok, i - 1)
                for j in range(SUP):
                    last = nc.scalar.activation(x1[:, c, j * P:(j + 1) * P], r1[:, j * P:(j + 1) * P], ACT.Identity,
                                                scale=rs1[:, j:j + 1], bias=nm1[:, j:j + 1])
                last.then_inc(x1_ok, 1)

            def x1_high(b, c):
                i = 2 * b + c
                act.wait_ge(x1T_ps, i + 1)
                wait_free(act, h_ps, FB * (i - 1))
                nc.scalar.copy(x1h[:, c, :], bank(2)).then_inc(x1h_ok, 1)

            def hidden_high(b, c, f):
                i = 2 * b + c
                act.wait_ge(h_ps, FB * i + f + 1)
                if f == 0:
                    wait_free(act, ff_ps, i - 1)
                nc.scalar.activation(hh[:, c, f, :], bank(3 + f % 2), ACT.Relu).then_inc(hh_ok, 1)

            def x2_norm(b, c):
                i = 2 * b + c
                act.wait_ge(ln2_step, 4 * i + 4)
                for j in range(SUP):
                    last = nc.scalar.activation(x2s[:, c, j * P:(j + 1) * P], r2[:, j * P:(j + 1) * P], ACT.Identity,
                                                scale=rs2[:, j:j + 1], bias=nm2[:, j:j + 1])
                last.then_inc(x2_ok, 1)

            def x2T_out(b, c):
                i = 2 * b + c
                act.wait_ge(x2T_ps, i + 1)
                nc.scalar.copy(x2T[:, bass.ds(b * 1024 + c * 512, 512)], bank(6)).then_inc(x2T_sb, 1)
                if c == 1:
                    nc.scalar.copy(gram[:, bass.ds(b, 1), :], bank(7)[:, 0:D].unsqueeze(1)).then_inc(gram_sb, 1)

            def body(b, c, nxt, prev):
                if nxt is not None:
                    yrT_out(*nxt)
                hidden_high(b, c, 0)
                hidden_high(b, c, 1)
                if prev is not None:
                    x2_norm(*prev)
                hidden_high(b, c, 2)
                hidden_high(b, c, 3)
                if nxt is not None:
                    x1_norm(*nxt)
                if prev is not None:
                    x2T_out(*prev)
                    act.wait_ge(x2_kept[prev[1]], 16 * (prev[0] + 1))
                if nxt is not None:
                    x1_high(*nxt)

            yrT_out(0, 0)
            x1_norm(0, 0)
            x1_high(0, 0)
            body(0, 0, (0, 1), None)
            body(0, 1, (1, 0), (0, 0))
            body(1, 0, (1, 1), (0, 1))
            with act.Fori(1, B - 1) as b:
                body(b, 1, (b + 1, 0), (b, 0))
                body(b + 1, 0, (b + 1, 1), (b, 1))
            body(B - 1, 1, None, (B - 1, 0))
            x2_norm(B - 1, 1)
            x2T_out(B - 1, 1)

            act.wait_ge(m1_ps, 1)
            nc.scalar.copy(gq[:, :], bank(1)).then_inc(m1_sb, 1)
            act.wait_ge(lg_ok, 1)
            nc.scalar.activation(ea[:, :, :], lg[:, :, :], ACT.Exp).then_inc(ea_ok, 1)
            act.wait_ge(m4_ps, 1)
            nc.scalar.copy(p1[:, :], bank(4)).then_inc(m4_sb, 1)
            act.wait_ge(m5_ps, 1)
            nc.scalar.copy(mix[:, :], bank(5)).then_inc(mix_ok, 1)

            def x3_norm(b, c):
                i = 2 * b + c
                act.wait_ge(ln3_step, 5 * i + 5)
                wait_free(act, scat[c], 16 * SUP * b)
                for j in range(SUP):
                    last = nc.scalar.activation(rows[:, c, j, 0:D], r3[:, j * P:(j + 1) * P], ACT.Identity,
                                                scale=rs3[:, j:j + 1], bias=nm3[:, j:j + 1])
                last.then_inc(x3_ok, 1)

            def x4_norm(b, c):
                i = 2 * b + c
                nc.scalar.activation(lv3[:, :], sq3[:, :], ACT.Ln, scale=-EPS, bias=onep[:, 0:1]).then_inc(s4_step, 1)
                act.wait_ge(s4_step, 2 * i + 1)
                nc.scalar.activation(s43[:, :], lv3[:, :], ACT.Exp, scale=-0.5).then_inc(s4_step, 1)
                act.wait_ge(s4_step, 2 * i + 2)
                act.wait_ge(x3_ok, i + 1)
                wait_free(act, stored[c], 16 * b)
                for j in range(SUP):
                    last = nc.scalar.activation(x4[:, c, j * P:(j + 1) * P], rows[:, c, j, 0:D], ACT.Copy, scale=s43[:, j:j + 1])
                last.then_inc(x4_ok, 1)

            def x3T_out(b, c):
                i = 2 * b + c
                act.wait_ge(x3T_ps, i + 1)
                wait_free(act, gate_ps, i)
                nc.scalar.copy(x3T[:, :], bank(2)).then_inc(x3T_sb, 1)

            def gate_exp(b, c):
                i = 2 * b + c
                act.wait_ge(gl_ok, i + 1)
                nc.scalar.activation(ge[:, :, :], gl[:, :, :], ACT.Exp).then_inc(ge_ok, 1)

            def body(b, c, nxt):
                x3T_out(b, c)
                gate_exp(b, c)
                if nxt is not None:
                    x3_norm(*nxt)
                    x4_norm(*nxt)

            act.wait_ge(carry_ok, 1)
            x3_norm(0, 0)
            x4_norm(0, 0)
            body(0, 0, (0, 1))
            with act.Fori(0, B - 1) as b:
                body(b, 1, (b + 1, 0))
                body(b + 1, 0, (b + 1, 1))
            body(B - 1, 1, None)

            def xeT_out(k, c):
                e = 2 * k + c
                act.wait_ge(xeT_ps, e + 1)
                wait_free(act, eh_ps, FB * (e - 1))
                nc.scalar.copy(xeT[:, c, :], pair(0)[:, 0:CAP]).then_inc(xeT_sb, 1)

            def expert_hidden(k, c, f):
                e = 2 * k + c
                act.wait_ge(eh_ps, FB * e + f + 1)
                if f == 0:
                    wait_free(act, ey_ps, e)
                n = 2 + 2 * (f % 2)
                nc.scalar.activation(eh[:, f, :].rearrange("p (a n) -> p a n", a=2), PS[:, n:n + 2, 0:CAP // 2], ACT.Relu,
                                     bias=eb1T[:, bass.ds(FB * e + f, 1)]).then_inc(eh_ok, 1)

            def y4_norm(k, c):
                e = 2 * k + c
                act.wait_ge(ln4_step, 4 * e + 4)
                wait_free(act, put[c], 16 * CT * k)
                for j in range(CT):
                    last = nc.scalar.activation(y4[:, c, j, :], r4[:, j, :], ACT.Identity,
                                                scale=rs4[:, j:j + 1], bias=nm4[:, j:j + 1])
                last.then_inc(y4_ok, 1)

            def expert(k, c, nxt, prev):
                if nxt is not None:
                    xeT_out(*nxt)
                expert_hidden(k, c, 0)
                expert_hidden(k, c, 1)
                if prev is not None:
                    y4_norm(*prev)
                expert_hidden(k, c, 2)
                expert_hidden(k, c, 3)

            xeT_out(0, 0)
            expert(0, 0, (0, 1), None)
            expert(0, 1, (1, 0), (0, 0))
            expert(1, 0, (1, 1), (0, 1))
            with act.Fori(1, E // 2 - 1) as k:
                expert(k, 1, (k + 1, 0), (k, 0))
                expert(k + 1, 0, (k + 1, 1), (k, 1))
            expert(E // 2 - 1, 1, None, (E // 2 - 1, 0))
            y4_norm(E // 2 - 1, 1)

        @block_.vector
        def _(dve):
            V = nc.vector
            step = [0]

            def link(ins):
                step[0] += 1
                ins.then_inc(dve1, 1)
                dve.wait_ge(dve1, step[0])

            V.memset(craw[:, :, 0:TAPS - 1], 0.0).then_inc(pad_ok, 1)
            V.memset(selA[:, :, :, :], 0.0)
            V.memset(empty[:, :], 0.0).then_inc(k_empty, 1)
            dve.wait_ge(k_empty, 1)
            V.memset(empty[:, D + 1:D + 2].bitcast(I32), TOK).then_inc(k_empty, 1)
            dve.wait_ge(k_pool, 1)
            for a in range(2):
                V.tensor_scalar(selA[:, :, a, :], ident[0:H, 0:H].unsqueeze(1).to_broadcast([H, B, H]),
                                1.0 - 2.0 * a, None, ALU.mult)
                last = V.tensor_copy(selB[:, :, a, :], ident[0:H, 0:H].unsqueeze(1).to_broadcast([H, B, H]))
            last.then_inc(k_sel, 1)
            V.memset(sign2[:, :, 0], -1.0)
            V.memset(sign2[:, :, 1], 1.0)
            V.memset(eps2[:, :, 0], 0.0)
            V.memset(eps2[:, :, 1], EPS)
            V.memset(epsT[:, :], EPS)
            V.memset(mhalf[:, :], -0.5)
            V.memset(drop8[:, :, :], DROP)
            V.memset(b1s[:, :], 0.0)
            V.memset(b2s[:, :], 0.0)
            link(V.memset(eb2s[:, :], 0.0))
            dve.wait_ge(k_pool, 7)
            V.tensor_reduce(diag8[:, :], ident[:, :].rearrange("p (h d) -> p d h", h=H), axis=AX, op=ALU.add)
            V.tensor_copy(ident16[:, :], ident[:, :])
            V.tensor_copy(upper16[:, :], upper[:, :]).then_inc(k_const, 1)
            dve.wait_ge(ld_w, 80)
            V.tensor_reduce(wabs[:, 0:1], w1n[:, :, :].rearrange("p k d -> p (k d)"), axis=AX, op=ALU.add,
                            apply_absolute_value=True)
            V.tensor_reduce(wabs[:, 1:2], w2n[:, :], axis=AX, op=ALU.add,
                            apply_absolute_value=True).then_inc(wabs_ok, 1)
            dve.wait_ge(win_sb, 3)
            V.tensor_scalar(nega[:, :], acol[:, 0:1], -1.0, None, ALU.mult).then_inc(nega_ok, 1)
            dve.wait_ge(ld_small, 64)
            dve.wait_ge(pad_ok, 1)

            def convolve(n):
                dve.wait_ge(proj_sb, 2 * n + 2)
                for k in range(TAPS - 1):
                    ins = V.scalar_tensor_tensor(out=conv[:, n, :], in0=craw[:, n, k:k + S],
                                                 scalar=convw[:, n, k:k + 1], in1=conv[:, n, :],
                                                 op0=ALU.mult, op1=ALU.add)
                    if k < TAPS - 2:
                        link(ins)
                    else:
                        ins.then_inc(conv_ok, 1)

            convolve(0)
            convolve(1)
            dve.wait_ge(dt_abs, 1)
            V.tensor_scalar(s4[:, :], pair(6), acol[:, 1:2], 0.0, ALU.add, ALU.max).then_inc(dt_pos, 1)
            dve.wait_ge(dt_ln, 1)
            dve.wait_ge(dt_pos, 1)
            link(V.tensor_tensor(s3[:, :], s3[:, :], s4[:, :], ALU.add))
            dve.wait_ge(k_ones, 3)
            V.tensor_tensor_scan(cum[:, :], onesS[:, :], s3[:, :], 0.0, ALU.mult, ALU.add).then_inc(cum_ok, 1)
            convolve(2)
            dve.wait_ge(exp_ok, 1)
            V.tensor_tensor_scan(s5[:, :], onesS[:, :], expn[:, :], 0.0, ALU.mult, ALU.add).then_inc(cs_ok, 1)
            dve.wait_ge(lncs_ok, 1)
            V.scalar_tensor_tensor(out=s2[:, :], in0=cum[:, :], scalar=nega[:, 0:1], in1=s4[:, :],
                                   op0=ALU.mult, op1=ALU.subtract).then_inc(lr_ok, 1)
            dve.wait_ge(ld_bias, 48)
            for src, dst in ((b1r, b1s), (b2r, b2s), (eb2r, eb2s)):
                link(V.tensor_copy(dst[0:1, :], src[0:1, :]))
                last = V.tensor_tensor(dst[32:33, :], src[0:1, :], dst[0:1, :], ALU.subtract)
            last.then_inc(bias_ok, 1)
            for t in range(TPB):
                c = t % 2
                if t < TPB - 1:
                    dve.wait_ge(st_ps, t + 1)
                    if t == 0:
                        V.tensor_tensor(st[:, :], bank(7)[:, 0:D], block[:, :], ALU.mult).then_inc(st_ok, 1)
                    else:
                        V.tensor_tensor(stn[:, :], bank(7)[:, 0:D], block[:, :], ALU.mult).then_inc(stn_ok, 1)
                        dve.wait_ge(stn_ok, t)
                        dve.wait_ge(off_ps, t)
                        V.tensor_tensor(st[:, :], st[:, :], stn[:, :], ALU.add).then_inc(st_ok, 1)
                dve.wait_ge(cum_ps, t + 1)
                V.tensor_tensor(cz[:, :].rearrange("p (h d n) -> p h d n", h=H, d=HD),
                                pair(2 + 2 * c).rearrange("p (h d n) -> p h d n", h=H, d=HD),
                                bcx[:, c, 0:D].rearrange("p (h n) -> p h n", h=H).unsqueeze(2).to_broadcast([P, H, HD, HD]),
                                ALU.mult).then_inc(cz_ok, 1)
                dve.wait_ge(cz_ok, t + 1)
                V.tensor_reduce(yi[:, :], cz[:, :].rearrange("p (k n) -> p k n", n=HD), axis=AX, op=ALU.add).then_inc(yi_ok, 1)
                dve.wait_ge(yi_ok, t + 1)
                src = yi
                if t > 0:
                    dve.wait_ge(off_ps, t)
                    V.tensor_tensor(ys[:, :], bank(6)[:, 0:D], yi[:, :], ALU.add).then_inc(ys_ok, 1)
                    dve.wait_ge(ys_ok, t)
                    src = ys
                V.tensor_tensor(y0[:, t, :].rearrange("p (h d) -> p h d", h=H),
                                src[:, :].rearrange("p (h d) -> p h d", h=H),
                                eT[:, t, H:2 * H].unsqueeze(2).to_broadcast([P, H, HD]), ALU.mult).then_inc(y0_ok, 1)

            def moments(i, r, r_ok, st, st_ok, mv, mv_ok):
                dve.wait_ge(r_ok, i + 1)
                for j in range(SUP):
                    last = V.bn_stats(st[:, j, :], r[:, j * P:(j + 1) * P])
                last.then_inc(st_ok, 1)
                dve.wait_ge(k_const, 1)
                dve.wait_ge(st_ok, i + 1)
                for j in range(SUP):
                    last = V.bn_aggr(mv[:, j, :], st[:, j, :])
                last.then_inc(mv_ok, 1)

            def add1(b, c):
                i = 2 * b + c
                dve.wait_ge(ao_ps, i + 1)
                wait_free(dve, x1_ok, i)
                V.tensor_tensor(r1[:, :], bank(1), xt[:, :, :].rearrange("p t d -> p (t d)")[:, bass.ds(b * 1024 + c * 512, 512)],
                                ALU.add).then_inc(r1_ok, 1)

            def moments1(b, c):
                i = 2 * b + c
                moments(i, r1, r1_ok, st1, st1_ok, mv1, mv1_ok)

            def x1_low(b, c):
                i = 2 * b + c
                dve.wait_ge(x1h_ok, i + 1)
                V.tensor_tensor(x1l[:, c, :], bank(2), x1h[:, c, :], ALU.subtract).then_inc(x1l_ok, 1)

            def hidden_low(b, c, f):
                i = 2 * b + c
                dve.wait_ge(hh_ok, FB * i + f + 1)
                V.scalar_tensor_tensor(out=hl[:, c, f, :], in0=bank(3 + f % 2), scalar=0.0, in1=hh[:, c, f, :],
                                       op0=ALU.max, op1=ALU.subtract).then_inc(hl_ok, 1)

            def add2(b, c):
                i = 2 * b + c
                dve.wait_ge(ff_ps, i + 1)
                wait_free(dve, x2_ok, i)
                V.tensor_tensor(r2[:, :], bank(5), x1[:, c, :], ALU.add).then_inc(r2_ok, 1)

            def moments2(b, c):
                i = 2 * b + c
                moments(i, r2, r2_ok, st2, st2_ok, mv2, mv2_ok)

            def body(b, c, nxt):
                if nxt is not None:
                    add1(*nxt)
                hidden_low(b, c, 0)
                if nxt is not None:
                    moments1(*nxt)
                for f in range(1, FB):
                    hidden_low(b, c, f)
                if nxt is not None:
                    x1_low(*nxt)
                add2(b, c)
                moments2(b, c)

            add1(0, 0)
            moments1(0, 0)
            x1_low(0, 0)
            body(0, 0, (0, 1))
            with dve.Fori(0, B - 1) as b:
                body(b, 1, (b + 1, 0))
                body(b + 1, 0, (b + 1, 1))
            body(B - 1, 1, None)

            dve.wait_ge(ld_l1, 64)
            V.tensor_scalar(tau32[:, :], tauc[:, :], float(S) ** -0.5, None, ALU.mult)
            step = [0]

            def link2(ins):
                step[0] += 1
                ins.then_inc(mixs, 1)
                dve.wait_ge(mixs, step[0])

            dve.wait_ge(m2_ps, 1)
            link2(V.tensor_tensor(dm[:, :, :], bank(2).rearrange("p (b f) -> p b f", b=B),
                                  block[:, :].unsqueeze(1).to_broadcast([P, B, D]), ALU.mult))
            link2(V.tensor_reduce(dc[:, :, :], dm[:, :, :].rearrange("p b (h d) -> p b d h", h=H), axis=AX, op=ALU.add))
            V.tensor_tensor(dq[:, :, :], dc[:, :, :], diag8[:, :].unsqueeze(1).to_broadcast([P, B, HD]),
                            ALU.mult).then_inc(dq_ok, 1)
            dve.wait_ge(dq_ok, 1)
            link2(V.tensor_reduce(qc[:, :], dq[:, :, :], axis=AX, op=ALU.add))
            dve.wait_ge(m3_ps, 1)
            link2(V.scalar_tensor_tensor(out=lg[:, :, :], in0=dc[:, :, :], scalar=2.0,
                                         in1=bank(3)[:, 0:B * HD].rearrange("p (b d) -> p b d", b=B),
                                         op0=ALU.mult, op1=ALU.subtract))
            link2(V.tensor_tensor(lg[:, :, :], lg[:, :, :], qc[:, :].unsqueeze(2).to_broadcast([P, B, HD]), ALU.subtract))
            link2(V.tensor_scalar(lg[:, :, :], lg[:, :, :], tau32[:, 0:1], None, ALU.mult))
            link2(V.tensor_reduce(mx[:, :], lg[:, :, :], axis=AX, op=ALU.max))
            V.tensor_tensor(lg[:, :, :], lg[:, :, :], mx[:, :].unsqueeze(2).to_broadcast([P, B, HD]),
                            ALU.subtract).then_inc(lg_ok, 1)
            dve.wait_ge(ea_ok, 1)
            link2(V.tensor_reduce(mx[:, :], ea[:, :, :], axis=AX, op=ALU.add))
            link2(V.reciprocal(mx[:, :], mx[:, :]))
            link2(V.tensor_tensor(ea[:, :, :], ea[:, :, :], mx[:, :].unsqueeze(2).to_broadcast([P, B, HD]), ALU.mult))
            V.tensor_tensor(ad[:, :, :].rearrange("p b (h d) -> p b h d", h=H),
                            ea[:, :, :].unsqueeze(2).to_broadcast([P, B, H, HD]),
                            block[:, :].rearrange("p (h d) -> p h d", h=H).unsqueeze(1).to_broadcast([P, B, H, HD]),
                            ALU.mult).then_inc(ad_ok, 1)

            V.memset(carry[:, :], 0.0)
            V.memset(onep[:, :], 1.0 + EPS).then_inc(carry_ok, 1)

            def add3(b, c):
                i = 2 * b + c
                dve.wait_ge(o3_ps, i + 1)
                wait_free(dve, x3_ok, i)
                V.tensor_tensor(r3[:, :], bank(0), x2k[:, bass.ds(b * 1024 + c * 512, 512)], ALU.add).then_inc(r3_ok, 1)

            def moments3(b, c):
                i = 2 * b + c
                moments(i, r3, r3_ok, st3, st3_ok, mv3, mv3_ok)

            G_STEPS = 8

            def gate_link(i, n, ins):
                ins.then_inc(gate_step, 1)
                dve.wait_ge(gate_step, G_STEPS * i + n)

            def gate(b, c):
                i = 2 * b + c
                lgt = bank(3)[:, 0:SUP * E].rearrange("p (t e) -> p t e", t=SUP)
                dve.wait_ge(gate_ps, i + 1)
                gate_link(i, 1, V.tensor_reduce(gmax[:, :], lgt, axis=AX, op=ALU.max))
                V.tensor_tensor(gl[:, :, :], lgt, gmax[:, :].unsqueeze(2).to_broadcast([P, SUP, E]), ALU.subtract).then_inc(gl_ok, 1)
                gate_link(i, 2, V.tensor_tensor(eqv[:, :, :], lgt, gmax[:, :].unsqueeze(2).to_broadcast([P, SUP, E]), ALU.is_ge))
                gate_link(i, 3, V.tensor_tensor(eqv[:, :, :], eqv[:, :, :], rev8[:, :].unsqueeze(1).to_broadcast([P, SUP, E]), ALU.mult))
                gate_link(i, 4, V.tensor_reduce(vmax[:, :], eqv[:, :, :], axis=AX, op=ALU.max))
                V.tensor_tensor(oh[:, :, :], eqv[:, :, :], vmax[:, :].unsqueeze(2).to_broadcast([P, SUP, E]), ALU.is_equal).then_inc(oh_ok, 1)
                dve.wait_ge(ge_ok, i + 1)
                gate_link(i, 5, V.tensor_reduce(gs[:, :], ge[:, :, :], axis=AX, op=ALU.add))

            def route(b, c):
                i = 2 * b + c
                pos = bank(4)[:, 0:SUP * E].rearrange("p (t e) -> p t e", t=SUP)
                wait_free(dve, scat[c], 16 * SUP * b)
                V.reciprocal(rows[:, c, :, D], gs[:, :])
                V.tensor_copy(rows[:, c, :, D + 1].bitcast(I32), tokid[:, bass.ds(SUP * i, SUP)])
                dve.wait_ge(oh_ok, i + 1)
                V.tensor_reduce(ohs[:, :], oh[:, :, :].rearrange("p t e -> p e t"), axis=AX, op=ALU.add)
                dve.wait_ge(pos_ps, i + 1)
                gate_link(i, 6, V.scalar_tensor_tensor(out=sl1[:, :, :], in0=pos, scalar=float(CAP), in1=drop8[:, :, :],
                                                       op0=ALU.is_gt, op1=ALU.mult))
                V.tensor_tensor(carry[:, :], carry[:, :], ohs[:, :], ALU.add).then_inc(carry_ok, 1)
                gate_link(i, 7, V.tensor_tensor(sl2[:, :, :], pos, sl1[:, :, :], ALU.add))
                gate_link(i, 8, V.tensor_tensor(sl1[:, :, :], sl2[:, :, :], base8[:, :].unsqueeze(1).to_broadcast([P, SUP, E]), ALU.add))
                V.tensor_tensor(sl2[:, :, :], sl1[:, :, :], oh[:, :, :], ALU.mult).then_inc(sl_ok, 1)
                dve.wait_ge(sl_ok, i + 1)
                wait_free(dve, slot_ok, i)
                V.tensor_reduce(slf[:, :], sl2[:, :, :], axis=AX, op=ALU.add).then_inc(slf_ok, 1)

            def body(b, c, nxt):
                if nxt is not None:
                    add3(*nxt)
                gate(b, c)
                if nxt is not None:
                    moments3(*nxt)
                route(b, c)

            add3(0, 0)
            moments3(0, 0)
            body(0, 0, (0, 1))
            body(0, 1, (1, 0))
            body(1, 0, (1, 1))
            with dve.Fori(1, B - 1) as b:
                body(b, 1, (b + 1, 0))
                body(b + 1, 0, (b + 1, 1))
            body(B - 1, 1, None)

            def expert(k, c):
                e = 2 * k + c
                dve.wait_ge(lds[c], 16 * (k + 1))
                wait_free(dve, put[c], 16 * CT * k)
                V.tensor_copy(xr[:, c, :, :], xs[:, c, :, :]).then_inc(xr_ok, 1)
                dve.wait_ge(xr_ok, e + 1)
                dve.wait_ge(ey_ps, e + 1)
                wait_free(dve, y4_ok, e)
                for j in range(CT):
                    last = V.scalar_tensor_tensor(out=r4[:, j, :], in0=pair(6)[:, j * D:(j + 1) * D],
                                                  scalar=xr[:, c, j, D:D + 1], in1=xr[:, c, j, 0:D],
                                                  op0=ALU.mult, op1=ALU.add)
                last.then_inc(r4_ok, 1)
                dve.wait_ge(r4_ok, e + 1)
                for j in range(CT):
                    last = V.bn_stats(st4[:, j, :], r4[:, j, :])
                last.then_inc(st4_ok, 1)
                dve.wait_ge(k_const, 1)
                dve.wait_ge(st4_ok, e + 1)
                for j in range(CT):
                    last = V.bn_aggr(mv4[:, j, :], st4[:, j, :])
                last.then_inc(mv4_ok, 1)

            expert(0, 0)
            expert(0, 1)
            expert(1, 0)
            with dve.Fori(1, E // 2 - 1) as k:
                expert(k, 1)
                expert(k + 1, 0)
            expert(E // 2 - 1, 1)

        @block_.tensor
        def _(pe):
            T = nc.tensor
            pe.wait_ge(k_pool, 1)
            pe.wait_ge(ld_win, 32)
            for n in range(3):
                T.transpose(bank(0)[:, n * D:(n + 1) * D], win[:, n, :], ident[:, :])
            T.transpose(bank(0)[:, 3 * D:3 * D + H], windt[:, :], ident[0:H, 0:H])
            pe.wait_ge(k_sel, 1)
            pe.wait_ge(ld_small, 64)
            T.matmul(bank(0)[:, 400:401], selA[:, :, :, :].rearrange("p b a h -> p (b a h)"), ab[:, 0:1], start=True, stop=True)
            T.matmul(bank(0)[:, 401:402], selB[:, :, :, :].rearrange("p b a h -> p (b a h)"), ab[:, 1:2], start=True, stop=True).then_inc(win_ps, 1)

            def x_in(n):
                pe.wait_ge(ld_x[n // 2], 16)
                wait_free(pe, xT_sb, n - 1)
                for j in range(SUP):
                    last = T.transpose(bank(1 + n % 2)[:, j * P:(j + 1) * P], xt[:, n * SUP + j, :], ident[:, :])
                last.then_inc(xT_ps, 1)

            def dt_in(n):
                pe.wait_ge(xT_sb, n + 1)
                T.matmul(PS[32 * (n // 2):32 * (n // 2) + 32, 6 + n % 2, :], wdtT[:, :], xT[:, n * 512:(n + 1) * 512],
                         start=True, stop=True).then_inc(dt_ps, 1)

            x_in(0)
            x_in(1)
            pe.wait_ge(wabs_ok, 1)
            T.matmul(bank(7)[:, 0:2], ones[:, :], wabs[:, :], start=True, stop=True).then_inc(wsum_ps, 1)
            pe.wait_ge(win_sb, 3)
            pe.wait_ge(xT_sb, 2)
            pe.wait_ge(cut_ok, 2)
            for n in range(6):
                wait_free(pe, proj_sb, n - 2)
                T.matmul(bank(3 + n % 3), winT[:, (n // 2) * D:(n // 2 + 1) * D], xT[:, (n % 2) * 512:(n % 2 + 1) * 512],
                         start=True, stop=True).then_inc(proj_ps, 1)
                x_in(2 + n)
                dt_in(n)
            dt_in(6)
            dt_in(7)
            pe.wait_ge(proj_sb, 6)
            pe.wait_ge(ld_w, 80)
            T.transpose(bank(5)[:, 0:D], wout[:, :], ident[:, :])
            T.transpose(bank(5)[:, D:2 * D], wv[:, :], ident[:, :])
            T.transpose(bank(5)[:, 2 * D:2 * D + E * FB], eb1n[:, :], ident[0:E * FB, 0:E * FB]).then_inc(wT_ps, 1)

            def chunk_in(t):
                pe.wait_ge(conv_ok, 3)
                if t == 0:
                    pe.wait_ge(xT_sb, NS)
                wait_free(pe, tr_sb, t - 1)
                for n in range(3):
                    last = T.transpose(bank(t % 2)[:, n * D:(n + 1) * D], conv[:, n, t * P:(t + 1) * P], ident[:, :])
                last.then_inc(tr_ps, 1)

            pe.wait_ge(exp_ok, 1)
            for t in range(TPB):
                last = T.transpose(bank(3)[:, t * 2 * H:(t + 1) * 2 * H], expn[0:2 * H, t * P:(t + 1) * P], ident[0:2 * H, 0:2 * H])
            last.then_inc(e_ps, 1)
            chunk_in(0)
            chunk_in(1)
            pe.wait_ge(dt_pos, 1)
            pe.wait_ge(e_sb, 1)
            pe.wait_ge(wT_sb, 3)
            for t in range(TPB):
                c = t % 2
                pe.wait_ge(xp_ok, t + 1)
                if t < TPB - 1:
                    wait_free(pe, stn_ok, t - 1)
                    if t == 1:
                        pe.wait_ge(st_ok, 1)
                    T.matmul(bank(7)[:, 0:D], bcx[:, c, D:2 * D], xp[:, c, :], start=True, stop=True).then_inc(st_ps, 1)
                pe.wait_ge(z_ok, t + 1)
                wait_free(pe, cz_ok, t - 1)
                for a in range(2):
                    last = T.matmul(bank(2 + 2 * c + a), upper[:, :], zz[:, c, a * 512:(a + 1) * 512], start=True, stop=True)
                last.then_inc(cum_ps, 1)
                if t > 0:
                    pe.wait_ge(st_ok, t)
                    wait_free(pe, ys_ok, t - 1)
                    T.matmul(bank(6)[:, 0:D], conv[:, 0, t * P:(t + 1) * P], st[:, :], start=True, stop=True).then_inc(off_ps, 1)
                if t + 2 < TPB:
                    chunk_in(t + 2)
            pe.wait_ge(ys_ok, TPB - 1)
            pe.wait_ge(k_const, 1)
            pe.wait_ge(q_ok, 2)
            for a in range(2):
                for k in range(FB):
                    src = q16[:, a, k * P:(k + 1) * P]
                    last = T.transpose(bank(6).bitcast(F16)[:, (a * FB + k) * P:(a * FB + k + 1) * P], src, ident16[:, :])
            last.then_inc(q_ps, 1)
            pe.wait_ge(r_ok, 1)
            pe.wait_ge(tr_sb, TPB)
            for t in range(TPB):
                last = T.transpose(bank(t // 4)[:, (t % 4) * P:(t % 4 + 1) * P], s1[:, t * P:(t + 1) * P], ident[:, :])
            last.then_inc(r_ps, 1)

            def yr_transpose(b, c):
                i = 2 * b + c
                pe.wait_ge(yr_ok, i + 1)
                wait_free(pe, yrT_sb, i)
                for j in range(SUP):
                    last = T.transpose(bank(0)[:, j * P:(j + 1) * P], yr[:, c, j, :], ident[:, :])
                last.then_inc(yrT_ps, 1)

            def attn_out(b, c):
                i = 2 * b + c
                pe.wait_ge(yrT_sb, i + 1)
                wait_free(pe, r1_ok, i)
                for j in range(SUP):
                    last = T.matmul(bank(1)[:, j * P:(j + 1) * P], yrT[:, j * P:(j + 1) * P], woutT[:, :], start=True, stop=True)
                last.then_inc(ao_ps, 1)

            def x1_transpose(b, c):
                i = 2 * b + c
                pe.wait_ge(x1_ok, i + 1)
                wait_free(pe, x1l_ok, i)
                for j in range(SUP):
                    last = T.transpose(bank(2)[:, j * P:(j + 1) * P], x1[:, c, j * P:(j + 1) * P], ident[:, :])
                last.then_inc(x1T_ps, 1)

            def hidden(b, c, f):
                i = 2 * b + c
                if f == 0:
                    pe.wait_ge(x1l_ok, i + 1)
                wait_free(pe, hl_ok, FB * i + f - 1)
                T.matmul(bank(3 + f % 2), qT[:, 0, f, :], x1h[:, c, :], start=True, stop=False)
                T.matmul(bank(3 + f % 2), qT[:, 0, f, :], x1l[:, c, :], start=False, stop=False)
                T.matmul(bank(3 + f % 2), b1s[:, f * P:(f + 1) * P], ones16[:, :], start=False, stop=True).then_inc(h_ps, 1)

            def feed_out(b, c):
                i = 2 * b + c
                pe.wait_ge(hl_ok, FB * (i + 1))
                wait_free(pe, r2_ok, i)
                for j in range(SUP):
                    o = bank(5)[:, j * P:(j + 1) * P]
                    T.matmul(o, ones16[:, 0:P], b2s[:, :], start=True, stop=False)
                    for f in range(FB):
                        T.matmul(o, hh[:, c, f, j * P:(j + 1) * P], qT[:, 1, f, :], start=False, stop=False)
                        last = T.matmul(o, hl[:, c, f, j * P:(j + 1) * P], qT[:, 1, f, :], start=False, stop=f == FB - 1)
                last.then_inc(ff_ps, 1)

            def x2_products(b, c):
                i = 2 * b + c
                pe.wait_ge(x2_ok, i + 1)
                wait_free(pe, x2T_sb, i)
                if c == 0:
                    wait_free(pe, gram_sb, b)
                for j in range(SUP):
                    T.matmul(bank(7)[:, 0:D], x2s[:, c, j * P:(j + 1) * P], x2s[:, c, j * P:(j + 1) * P],
                             start=c == 0 and j == 0, stop=c == 1 and j == SUP - 1)
                for j in range(SUP):
                    last = T.transpose(bank(6)[:, j * P:(j + 1) * P], x2s[:, c, j * P:(j + 1) * P], ident[:, :])
                last.then_inc(x2T_ps, 1)

            def body(b, c, nxt, prev):
                if nxt is not None:
                    yr_transpose(*nxt)
                hidden(b, c, 0)
                if nxt is not None:
                    attn_out(*nxt)
                for f in range(1, FB):
                    hidden(b, c, f)
                if prev is not None:
                    x2_products(*prev)
                if nxt is not None:
                    x1_transpose(*nxt)
                feed_out(b, c)

            pe.wait_ge(r_sb, 1)
            pe.wait_ge(q_sb, 1)
            pe.wait_ge(bias_ok, 1)
            pe.wait_ge(k_ones, 3)
            yr_transpose(0, 0)
            attn_out(0, 0)
            x1_transpose(0, 0)
            body(0, 0, (0, 1), None)
            body(0, 1, (1, 0), (0, 0))
            body(1, 0, (1, 1), (0, 1))
            with pe.Fori(1, B - 1) as b:
                body(b, 1, (b + 1, 0), (b, 0))
                body(b + 1, 0, (b + 1, 1), (b, 1))
            body(B - 1, 1, None, (B - 1, 0))
            x2_products(B - 1, 1)

            pe.wait_ge(gram_sb, B)
            pe.wait_ge(ld_l1, 64)
            for b in range(B):
                last = T.matmul(bank(1)[:, b * D:(b + 1) * D], gram[:, b, :], wqk[:, :], start=True, stop=True)
            last.then_inc(m1_ps, 1)
            pe.wait_ge(m1_sb, 1)
            T.matmul(bank(2), wqk[:, :], gq[:, :], start=True, stop=True).then_inc(m2_ps, 1)
            pe.wait_ge(dq_ok, 1)
            T.matmul(bank(3)[:, 0:B * HD], block[:, :], dq[:, :, :].rearrange("p b d -> p (b d)"), start=True, stop=True).then_inc(m3_ps, 1)
            pe.wait_ge(ad_ok, 1)
            for b in range(B):
                last = T.matmul(bank(4)[:, b * D:(b + 1) * D], ad[:, b, :], wo[:, :], start=True, stop=True)
            last.then_inc(m4_ps, 1)
            pe.wait_ge(m4_sb, 1)
            T.matmul(bank(5), wvT[:, :], p1[:, :], start=True, stop=True).then_inc(m5_ps, 1)

            def attn2_out(b, c):
                i = 2 * b + c
                pe.wait_ge(staged[c], 16 * (b + 1))
                wait_free(pe, r3_ok, i)
                for j in range(SUP):
                    last = T.matmul(bank(0)[:, j * P:(j + 1) * P], x2Ts[:, c, j * P:(j + 1) * P],
                                    mix[:, bass.ds(b * D, D)], start=True, stop=True)
                last.then_inc(o3_ps, 1)

            def gate(b, c):
                i = 2 * b + c
                pe.wait_ge(x3_ok, i + 1)
                wait_free(pe, x3T_sb, i)
                for j in range(SUP):
                    last = T.transpose(bank(2)[:, j * P:(j + 1) * P], rows[:, c, j, 0:D], ident[:, :])
                last.then_inc(x3T_ps, 1)
                pe.wait_ge(x3T_sb, i + 1)
                wait_free(pe, oh_ok, i)
                for j in range(SUP):
                    last = T.matmul(bank(3)[:, j * E:(j + 1) * E], x3T[:, j * P:(j + 1) * P], wgs[:, :], start=True, stop=True)
                last.then_inc(gate_ps, 1)
                pe.wait_ge(oh_ok, i + 1)
                pe.wait_ge(carry_ok, i + 1)
                wait_free(pe, slf_ok, i)
                flat = oh[:, :, :].rearrange("p t e -> p (t e)")
                T.matmul(bank(4)[:, 0:SUP * E], upper16[:, :], flat, start=True, stop=False)
                for n in range(1, SUP):
                    T.matmul(bank(4)[:, n * E:SUP * E], ones16[:, 0:P], flat[:, 0:(SUP - n) * E], start=False, stop=False)
                T.matmul(bank(4)[:, 0:SUP * E].rearrange("p (t e) -> p t e", t=SUP), ones16[:, 0:P],
                         carry[:, :].unsqueeze(1).to_broadcast([P, SUP, E]), start=False, stop=True).then_inc(pos_ps, 1)

            def body(b, c, nxt):
                if nxt is not None:
                    attn2_out(*nxt)
                gate(b, c)

            pe.wait_ge(mix_ok, 1)
            attn2_out(0, 0)
            body(0, 0, (0, 1))
            with pe.Fori(0, B - 1) as b:
                body(b, 1, (b + 1, 0))
                body(b + 1, 0, (b + 1, 1))
            body(B - 1, 1, None)

            def expert_in(k, c):
                e = 2 * k + c
                pe.wait_ge(lds[c], 16 * (k + 1))
                wait_free(pe, xeT_sb, e)
                for j in range(CT):
                    last = T.transpose(pair(0)[:, j * P:(j + 1) * P], xs[:, c, j, 0:D], ident[:, :])
                last.then_inc(xeT_ps, 1)

            def expert_hidden(k, c, f):
                e = 2 * k + c
                if f == 0:
                    pe.wait_ge(xeT_sb, e + 1)
                    pe.wait_ge(ldw[c], 32 * (k + 1))
                wait_free(pe, eh_ok, FB * e + f - 1)
                for a in range(2):
                    last = T.matmul(PS[:, 2 + 2 * (f % 2) + a, 0:CAP // 2], w1s[:, c, f * P:(f + 1) * P],
                                    xeT[:, c, a * (CAP // 2):(a + 1) * (CAP // 2)], start=True, stop=True)
                last.then_inc(eh_ps, 1)

            def expert_out(k, c):
                e = 2 * k + c
                pe.wait_ge(eh_ok, FB * (e + 1))
                wait_free(pe, r4_ok, e)
                for j in range(CT):
                    o = pair(6)[:, j * D:(j + 1) * D]
                    T.matmul(o, ones16[:, 0:P], eb2s[:, bass.ds(e * D, D)], start=True, stop=False)
                    for f in range(FB):
                        last = T.matmul(o, eh[:, f, j * P:(j + 1) * P], w2s[:, c, f, :], start=False, stop=f == FB - 1)
                last.then_inc(ey_ps, 1)

            def expert(k, c, nxt):
                if nxt is not None:
                    expert_in(*nxt)
                for f in range(FB):
                    expert_hidden(k, c, f)
                expert_out(k, c)

            pe.wait_ge(slot_ok, NS)
            expert_in(0, 0)
            expert(0, 0, (0, 1))
            with pe.Fori(0, E // 2 - 1) as k:
                expert(k, 1, (k + 1, 0))
                expert(k + 1, 0, (k + 1, 1))
            expert(E // 2 - 1, 1, None)


_INS = ['L0_attn_x', 'L0_attn_W_in', 'L0_attn_conv_w', 'L0_attn_conv_b', 'L0_attn_A_param', 'L0_attn_dt_bias',
        'L0_attn_W_out', 'L0_ffn_W1', 'L0_ffn_b1', 'L0_ffn_W2', 'L0_ffn_b2', 'L1_attn_Wqk', 'L1_attn_Wv',
        'L1_attn_Wo', 'L1_attn_tau', 'L1_ffn_wg', 'L1_ffn_w1', 'L1_ffn_b1', 'L1_ffn_w2', 'L1_ffn_b2']


def kernel(**inputs):
    import numpy as np
    import concourse.bacc as bacc
    from concourse.bass_utils import run_bass_kernel_spmd

    nc = bacc.Bacc("TRN2", target_bir_lowering=False, num_devices=1)
    arrays, args = {}, []
    for name in _INS:
        a = np.ascontiguousarray(inputs[name])
        arrays[f"in_{name}"] = a
        args.append(nc.dram_tensor(f"in_{name}", a.shape, mybir.dt.from_np(a.dtype), kind="ExternalInput").ap())
    args.append(nc.dram_tensor("out", (B, S, D), F32, kind="ExternalOutput").ap())
    build_program(nc, *args)
    return run_bass_kernel_spmd(nc, [arrays], core_ids=[0]).results[0]["out"]
```

```python
from contextlib import ExitStack

import concourse.bass as bass
from concourse import mybir

F32 = mybir.dt.float32
F16 = mybir.dt.float16
I32 = mybir.dt.int32
U32 = mybir.dt.uint32
ACT = mybir.ActivationFunctionType
ALU = mybir.AluOpType
AX = mybir.AxisListType.X

P = 128
B, S, D = 4, 1024, 128
H, HD = 16, 8
TAPS = 4
F = 512
FB = F // P
E = 8
TOK = B * S
CAP = int(1.25 * TOK / E)
CT = CAP // P
NT = TOK // P
TPB = S // P
SUP = 4
NS = NT // SUP
ME = D + E
ROW = D + 2
EPS = 1e-5
DROP = 8192.0


def build_program(nc, x, W_in, conv_w, conv_b, A_param, dt_bias, W_out, W1, b1, W2, b2,
                  Wqk, Wv, Wo, tau, wg, w1, eb1, w2, eb2, out):
    ctx = ExitStack()
    with ctx:
        def sb(name, shape, dt=F32):
            return ctx.enter_context(nc.sbuf_tensor(name, shape, dt))

        def sem(name):
            return ctx.enter_context(nc.semaphore(name))

        def wait_free(eng, semaphore, count):
            if not isinstance(count, int) or count > 0:
                eng.wait_ge(semaphore, count)

        PS = ctx.enter_context(nc.psum_tensor("PS", [P, 8, 512], F32))

        def bank(n):
            return PS[:, n, :]

        def part(tensor, first, *dims):
            size, names = 1, "abcd"[:len(dims)]
            for d in dims:
                size *= d
            flat = tensor[:, first:first + size]
            if len(dims) == 1:
                return flat
            return flat.rearrange(f"p ({' '.join(names)}) -> p {' '.join(names)}", **dict(zip(names, dims)))

        def pair(n):
            return PS[:, n:n + 2, :].rearrange("p a f -> p (a f)")

        slots = nc.dram_tensor("slots", (E * CAP, ROW), F32, kind="Internal").ap()

        ones = sb("ones", [P, P])
        ident = sb("ident", [P, P])
        upper = sb("upper", [P, P])
        block = sb("block", [P, P])
        ones16 = sb("ones16", [P, 512], F16)
        ident16 = sb("ident16", [P, P], F16)
        upper16 = sb("upper16", [P, P], F16)
        diag8 = sb("diag8", [P, HD])
        selA = sb("selA", [H, B, 2, H])
        selB = sb("selB", [H, B, 2, H])
        tokid = sb("tokid", [P, NT], I32)
        rev8 = sb("rev8", [P, E])
        base8 = sb("base8", [P, E])
        lim8 = sb("lim8", [P, E])
        base16 = sb("base16", [P, E], F16)
        sign2 = sb("sign2", [P, SUP + 1, 2])
        eps2 = sb("eps2", [P, SUP + 1, 2])
        epsT = sb("epsT", [P, SUP])
        mhalf = sb("mhalf", [P, SUP])
        empty = sb("empty", [P, ROW])

        xt = sb("xt", [P, NT, D])
        win = sb("win", [P, 3, D])
        windt = sb("windt", [H, D])
        convw = sb("convw", [P, 3, TAPS])
        convb = sb("convb", [P, 3])
        ab = sb("ab", [H, 2])
        wout = sb("wout", [P, D])
        wn = sb("wn", [P, 2, F])
        w1n = part(wn[:, 0, :], 0, FB, D)
        w2n = wn[:, 1, :]
        wqk = sb("wqk", [P, D])
        wv = sb("wv", [P, D])
        wog = sb("wog", [P, ME])
        wo = wog[:, 0:D]
        tauc = sb("tauc", [P, 1])
        wgs = sb("wgs", [P, E])
        eb1n = sb("eb1n", [E * FB, P])
        b1r = sb("b1r", [1, F])
        b2r = sb("b2r", [1, D])
        eb2r = sb("eb2r", [1, E * D])

        winT = sb("winT", [P, 3 * D])
        wdtT = sb("wdtT", [P, 2 * H])
        acol = sb("acol", [P, 2])
        nega = sb("nega", [P, 1])
        woutT = sb("woutT", [P, D])
        wvT = sb("wvT", [P, D])
        woT = sb("woT", [P, D])
        wgsum = sb("wgsum", [P, E])
        eb1T = sb("eb1T", [P, E * FB])
        wabs = sb("wabs", [P, 2])
        cut = sb("cut", [P, 2])
        ncut = sb("ncut", [P, 2])
        q16 = sb("q16", [P, 2, F], F16)
        qT = sb("qT", [P, 2, FB, P], F16)
        b1s = sb("b1s", [P, F], F16)
        b2s = sb("b2s", [P, D], F16)
        eb2s = sb("eb2s", [P, E * D], F16)
        tau32 = sb("tau32", [P, 1])

        xT = sb("xT", [P, TOK])
        first = sb("first", [P, 3 * (TAPS - 1 + S) + 3 * S])
        craw = part(first, 0, 3, TAPS - 1 + S)
        conv = part(first, 3 * (TAPS - 1 + S), 3, S)
        work = sb("work", [P, 5, S])
        s1, s2, s3, s4, s5 = (work[:, n, :] for n in range(5))
        qpos = part(s5, 0, F)
        qneg = part(s5, F, F)
        cum = sb("cum", [P, S])
        onesS = sb("onesS", [P, S])
        expn = sb("expn", [P, S])
        rT = sb("rT", [P, TPB, P])
        eT = sb("eT", [P, TPB, 2 * H])
        bcx = sb("bcx", [P, 3, 3 * D])
        xp = sb("xp", [P, 2, D])
        zz = sb("zz", [P, 2, 1024])
        cz = sb("cz", [P, 2, 1024])
        taps = [zz[:, 0, :], zz[:, 1, :], cz[:, 0, :]]
        yi = sb("yi", [P, 2, D])
        ys = sb("ys", [P, 4, D])
        st = sb("st", [P, 2, D])
        y0 = sb("y0", [P, TPB, D])

        ld_x = [sem(f"ld_x{b}") for b in range(B)]
        ld_win = sem("ld_win")
        ld_small = sem("ld_small")
        ld_w = sem("ld_w")
        ld_l1 = sem("ld_l1")
        ld_bias = sem("ld_bias")
        k_ones = sem("k_ones")
        k_pool = sem("k_pool")
        k_sel = sem("k_sel")
        k_const = sem("k_const")
        k_empty = sem("k_empty")
        slots_init = sem("slots_init")
        slf_ok = sem("slf_ok")
        slp_ok = sem("slp_ok")
        win_ps = sem("win_ps")
        win_sb = sem("win_sb")
        nega_ok = sem("nega_ok")
        pad_ok = sem("pad_ok")
        xT_ps = sem("xT_ps")
        xT_sb = [sem("xT_sb0"), sem("xT_sb1")]
        proj_ps = sem("proj_ps")
        proj_sb = sem("proj_sb")
        dt_ps = sem("dt_ps")
        dt_abs = sem("dt_abs")
        dt_ln = sem("dt_ln")
        dve1 = sem("dve1")
        act1 = sem("act1")
        dt_pos = sem("dt_pos")
        cum_ok = sem("cum_ok")
        exp_ok = sem("exp_ok")
        cs_ok = sem("cs_ok")
        lncs_ok = sem("lncs_ok")
        lr_ok = sem("lr_ok")
        r_ok = sem("r_ok")
        e_ps = sem("e_ps")
        e_sb = sem("e_sb")
        r_ps = sem("r_ps")
        r_sb = sem("r_sb")
        tap_ok = sem("tap_ok")
        tap_sum = sem("tap_sum")
        conv_ok = sem("conv_ok")
        wabs_ok = sem("wabs_ok")
        wsum_ps = sem("wsum_ps")
        q_ok = sem("q_ok")
        cut_ok = sem("cut_ok")
        cmp_ok = sem("cmp_ok")
        q_ps = sem("q_ps")
        q_sb = sem("q_sb")
        wT_ps = sem("wT_ps")
        wT_sb = sem("wT_sb")
        wg_ps = sem("wg_ps")
        wg_sb = sem("wg_sb")
        bias_ok = sem("bias_ok")
        tr_ps = sem("tr_ps")
        tr_sb = sem("tr_sb")
        xp_ok = sem("xp_ok")
        z_ok = sem("z_ok")
        cum_ps = sem("cum_ps")
        cz_ok = sem("cz_ok")
        off_ps = sem("off_ps")
        st_ps = sem("st_ps")
        st_ok = sem("st_ok")
        yi_ok = sem("yi_ok")
        ys_ok = sem("ys_ok")
        y0_ok = sem("y0_ok")

        yr = sb("yr", [P, 2, SUP, D])
        yrT = sb("yrT", [P, 512])
        r1 = sb("r1", [P, 512])
        st1 = sb("st1", [P, SUP, 6])
        mv1 = sb("mv1", [P, SUP, 2])
        neg1 = sb("neg1", [P, SUP])
        ve1 = sb("ve1", [P, SUP])
        neg1_ok = sem("neg1_ok")
        rs1 = sb("rs1", [P, SUP])
        nm1 = sb("nm1", [P, SUP])
        x1 = sb("x1", [P, 2, 512])
        x1h = sb("x1h", [P, 2, 512], F16)
        x1l = sb("x1l", [P, 2, 512], F16)
        hh = sb("hh", [P, 2, FB, 512], F16)
        hl = sb("hl", [P, 2, FB, 512], F16)
        r2 = sb("r2", [P, 512])
        st2 = sb("st2", [P, SUP, 6])
        mv2 = sb("mv2", [P, SUP, 2])
        neg2 = sb("neg2", [P, SUP])
        ve2 = sb("ve2", [P, SUP])
        neg2_ok = sem("neg2_ok")
        rs2 = sb("rs2", [P, SUP])
        nm2 = sb("nm2", [P, SUP])
        x2s = sb("x2s", [P, 2, 512])
        x2k = xt[:, :, :].rearrange("p t d -> p (t d)")
        x2T = xT
        gram = sb("gram", [P, B, D])
        yr_ok = sem("yr_ok")
        yrT_ps = sem("yrT_ps")
        yrT_sb = sem("yrT_sb")
        ao_ps = sem("ao_ps")
        r1_ok = sem("r1_ok")
        st1_ok = sem("st1_ok")
        mv1_ok = sem("mv1_ok")
        ln1_step = sem("ln1_step")
        x1_ok = sem("x1_ok")
        x1T_ps = sem("x1T_ps")
        x1h_ok = sem("x1h_ok")
        x1l_ok = sem("x1l_ok")
        h_ps = sem("h_ps")
        hh_ok = sem("hh_ok")
        hl_ok = sem("hl_ok")
        ff_ps = sem("ff_ps")
        r2_ok = sem("r2_ok")
        st2_ok = sem("st2_ok")
        mv2_ok = sem("mv2_ok")
        ln2_step = sem("ln2_step")
        x2_ok = sem("x2_ok")
        x2_kept = [sem("x2_kept0"), sem("x2_kept1")]
        x2T_ps = sem("x2T_ps")
        x2T_sb = sem("x2T_sb")
        gram_sb = sem("gram_sb")

        gq = part(expn, 0, 512)
        dm = sb("dm", [P, B, D])
        dc = sb("dc", [P, B, HD])
        dq = sb("dq", [P, B, HD])
        qc = sb("qc", [P, B])
        lg = sb("lg", [P, B, HD])
        mx = sb("mx", [P, B])
        ea = sb("ea", [P, B, HD])
        ad = sb("ad", [P, B, D])
        p1 = sb("p1", [P, B * ME])
        mix = sb("mix", [P, B * ME])
        m1_ps = sem("m1_ps")
        m1_sb = sem("m1_sb")
        m2_ps = sem("m2_ps")
        mixs = sem("mixs")
        dq_ok = sem("dq_ok")
        m3_ps = sem("m3_ps")
        lg_ok = sem("lg_ok")
        ea_ok = sem("ea_ok")
        ad_ok = sem("ad_ok")
        m4_ps = sem("m4_ps")
        m4_sb = sem("m4_sb")
        m5_ps = sem("m5_ps")
        mix_ok = sem("mix_ok")

        x2Ts = part(onesS, 0, 2, 512)
        r3 = part(expn, 512, 512)
        st3 = sb("st3", [P, SUP, 6])
        mv3 = sb("mv3", [P, SUP, 2])
        rs3 = sb("rs3", [P, SUP])
        nm3 = sb("nm3", [P, SUP])
        lv3 = sb("lv3", [P, SUP])
        sq3 = sb("sq3", [P, SUP])
        lq3 = sb("lq3", [P, SUP])
        s43 = sb("s43", [P, SUP])
        onep = sb("onep", [P, 1])
        zz1 = zz[:, :, :].rearrange("p a f -> p (a f)")
        rows = part(zz1, 0, 2, SUP, ROW)
        x4 = part(cz[:, 0, :], 0, 2, 512)
        gmax = sb("gmax", [P, SUP])
        l1 = sb("l1", [P, SUP, E])
        l2 = sb("l2", [P, SUP, E])
        gl = sb("gl", [P, SUP, E])
        ge = sb("ge", [P, SUP, E])
        gs = sb("gs", [P, SUP])
        eqv = sb("eqv", [P, SUP, E])
        vmax = sb("vmax", [P, SUP])
        oh = sb("oh", [P, 2, SUP, E], F16)
        ohs = sb("ohs", [P, E])
        carry = sb("carry", [P, E], F16)
        sl1 = sb("sl1", [P, SUP, E])
        sl2 = sb("sl2", [P, SUP, E])
        slf = sb("slf", [P, SUP])
        slp = sb("slp", [P, SUP])
        slot = sb("slot", [P, 2, SUP], U32)
        staged = [sem("staged0"), sem("staged1")]
        o3_ps = sem("o3_ps")
        r3_ok = sem("r3_ok")
        st3_ok = sem("st3_ok")
        mv3_ok = sem("mv3_ok")
        lv3_ok = sem("lv3_ok")
        rs3_ok = sem("rs3_ok")
        nm3_ok = sem("nm3_ok")
        x3_ok = sem("x3_ok")
        gate_step = sem("gate_step")
        gl_ok = sem("gl_ok")
        ge_ok = sem("ge_ok")
        oh_ok = sem("oh_ok")
        pos_ps = sem("pos_ps")
        slot_ok = sem("slot_ok")
        sl_ok = sem("sl_ok")
        s4_step = sem("s4_step")
        x4_ok = sem("x4_ok")
        stored = [sem("stored0"), sem("stored1")]
        scat = [sem("scat0"), sem("scat1")]
        carry_ok = sem("carry_ok")

        work1 = work[:, :, :].rearrange("p a f -> p (a f)")
        xs = part(first, 0, 2, CT, ROW)
        xr = part(first, 2 * CT * ROW, 2, CT, ROW)
        w1s = part(cum, 0, 2, F)
        w2s = part(wn[:, :, :].rearrange("p a f -> p (a f)"), 0, 2, FB, D)
        xeT = part(xT, 0, 2, CAP)
        eh = part(work1, 0, FB, CAP)
        xr_ok = sem("xr_ok")
        r4 = part(work1, FB * CAP, CT, D)
        st4 = sb("st4", [P, CT, 6])
        mv4 = sb("mv4", [P, CT, 2])
        ln4 = [sb(f"ln4_{n}", [P, CT, 2]) for n in range(2)]
        neg4 = sb("neg4", [P, CT])
        lv4 = sb("lv4", [P, CT])
        rs4 = sb("rs4", [P, CT])
        nm4 = sb("nm4", [P, CT])
        y4 = part(work1, (FB + 1) * CAP, 2, CT, D)
        ldw = [sem("ldw0"), sem("ldw1")]
        lds = [sem("lds0"), sem("lds1")]
        xeT_ps = sem("xeT_ps")
        xeT_sb = sem("xeT_sb")
        eh_ps = sem("eh_ps")
        eh_ok = sem("eh_ok")
        ey_ps = sem("ey_ps")
        r4_ok = sem("r4_ok")
        st4_ok = sem("st4_ok")
        mv4_ok = sem("mv4_ok")
        rs4_ok = sem("rs4_ok")
        neg4_ok = sem("neg4_ok")
        lv4_ok = sem("lv4_ok")
        ln4_step = sem("ln4_step")
        y4_ok = sem("y4_ok")
        put = [sem("put0"), sem("put1")]

        block_ = ctx.enter_context(nc.Block())

        @block_.sync
        def _(sp):
            sp.dma_start(win[:, :, :], W_in[0:3 * D, :].rearrange("(g p) d -> p g d", p=P)).then_inc(ld_win, 16)
            sp.dma_start(windt[:, :], W_in[3 * D:3 * D + H, :]).then_inc(ld_win, 16)
            for b in range(B):
                sp.dma_start(xt[:, b * TPB:(b + 1) * TPB, :],
                             x[b].rearrange("(t p) d -> p t d", p=P)).then_inc(ld_x[b], 16)
            sp.dma_start(w1n[:, :, :], W1.rearrange("(k p) d -> p k d", p=P)).then_inc(ld_w, 16)
            sp.dma_start(w2n[:, :], W2).then_inc(ld_w, 16)
            sp.dma_start(wout[:, :], W_out).then_inc(ld_w, 16)
            sp.dma_start(wv[:, :], Wv).then_inc(ld_w, 16)
            sp.dma_start(eb1n[:, :], eb1.rearrange("e (k p) -> (e k) p", p=P)).then_inc(ld_w, 16)
            sp.dma_start(b1r[:, :], b1.rearrange("(o f) -> o f", o=1)).then_inc(ld_bias, 16)
            sp.dma_start(b2r[:, :], b2.rearrange("(o f) -> o f", o=1)).then_inc(ld_bias, 16)
            sp.dma_start(eb2r[:, :], eb2.rearrange("(o e) d -> o (e d)", o=1)).then_inc(ld_bias, 16)
            sp.dma_start(wqk[:, :], Wqk).then_inc(ld_l1, 16)
            sp.dma_start(wo, Wo).then_inc(ld_l1, 16)
            sp.dma_start(tauc[:, :], tau.rearrange("h a b -> h (a b)").unsqueeze(1).to_broadcast([H, HD, 1])).then_inc(ld_l1, 16)
            sp.dma_start(wgs[:, :], wg).then_inc(ld_l1, 16)
            sp.wait_ge(k_empty, 2)
            sp.dma_start(slots.rearrange("(p t) r -> p t r", p=P),
                         empty[:, :].unsqueeze(1).to_broadcast([P, E * CT, ROW])).then_inc(slots_init, 16)

            def keep_x2(b, c):
                sp.wait_ge(x2_ok, 2 * b + c + 1)
                sp.dma_start(x2k[:, bass.ds(b * 1024 + c * 512, 512)], x2s[:, c, :]).then_inc(x2_kept[c], 16)

            with sp.Fori(0, B) as b:
                keep_x2(b, 0)
                keep_x2(b, 1)

            def load_weights(k, c):
                sp.dma_start(w1s[:, c, :], w1[bass.ds(2 * k + c, 1)].rearrange("e d f -> d (e f)")).then_inc(ldw[c], 16)
                sp.dma_start(w2s[:, c, :, :], w2[bass.ds(2 * k + c, 1)].rearrange("e (k p) d -> p (e k) d", p=P)).then_inc(ldw[c], 16)

            def stage_x2T(b, c):
                sp.dma_start(x2Ts[:, c, :], x2T[:, bass.ds(b * 1024 + c * 512, 512)]).then_inc(staged[c], 16)

            def store_x4(b, c):
                sp.wait_ge(x4_ok, 2 * b + c + 1)
                sp.dma_start(out[bass.ds(b, 1), c * 512:(c + 1) * 512, :].rearrange("b (t p) d -> p (b t) d", p=P),
                             x4[:, c, :].rearrange("p (t d) -> p t d", t=SUP)).then_inc(stored[c], 16)

            load_weights(0, 0)
            load_weights(0, 1)
            sp.wait_ge(x2T_sb, NS)
            stage_x2T(0, 0)
            stage_x2T(0, 1)
            with sp.Fori(0, B - 1) as b:
                sp.wait_ge(o3_ps, 2 * b + 1)
                stage_x2T(b + 1, 0)
                store_x4(b, 0)
                sp.wait_ge(o3_ps, 2 * b + 2)
                stage_x2T(b + 1, 1)
                store_x4(b, 1)
            store_x4(B - 1, 0)
            store_x4(B - 1, 1)

            def load_slots(k, c):
                sp.dma_start(xs[:, c, :, :],
                             slots[bass.ds((2 * k + c) * CAP, CAP), :].rearrange("(t p) r -> p t r", p=P)).then_inc(lds[c], 16)

            for c in range(2):
                sp.wait_ge(scat[c], 16 * SUP * B)
            load_slots(0, 0)
            load_slots(0, 1)
            with sp.Fori(0, E // 2 - 1) as k:
                for c in range(2):
                    sp.wait_ge(xeT_ps, 2 * k + c + 1)
                    sp.wait_ge(xr_ok, 2 * k + c + 1)
                    load_slots(k + 1, c)
                for c in range(2):
                    sp.wait_ge(ey_ps, 2 * k + c + 1)
                    load_weights(k + 1, c)
            for c in range(2):
                sp.wait_ge(put[c], 16 * CT * (E // 2))
                sp.wait_ge(stored[c], 16 * B)

        @block_.gpsimd
        def _(pool):
            pool.memset(ones[:, :], 1.0).then_inc(k_ones, 1)
            pool.wait_ge(k_ones, 1)
            pool.affine_select(out=ident[:, :], in_=ones[:, :], compare_op=ALU.is_equal, fill=0.0, base=0,
                               pattern=[[-1, P]], channel_multiplier=1).then_inc(k_pool, 1)
            pool.affine_select(out=upper[:, :], in_=ones[:, :], compare_op=ALU.is_ge, fill=0.0, base=0,
                               pattern=[[1, P]], channel_multiplier=-1).then_inc(k_pool, 1)
            pool.affine_select(out=block[:, :], in_=ones[:, :], compare_op=ALU.is_ge, fill=0.0, base=0,
                               pattern=[[-HD, H], [0, HD]], channel_multiplier=1).then_inc(k_pool, 1)
            pool.wait_ge(k_pool, 3)
            pool.affine_select(out=block[:, :], in_=block[:, :], compare_op=ALU.is_ge, fill=0.0, base=HD - 1,
                               pattern=[[HD, H], [0, HD]], channel_multiplier=-1).then_inc(k_pool, 1)
            pool.iota(tokid[:, :], pattern=[[P, NT]], base=0, channel_multiplier=1).then_inc(k_pool, 1)
            pool.iota(rev8[:, :], pattern=[[-1, E]], base=E, channel_multiplier=0,
                      allow_small_or_imprecise_dtypes=True).then_inc(k_pool, 1)
            pool.iota(base8[:, :], pattern=[[CAP, E]], base=0, channel_multiplier=0,
                      allow_small_or_imprecise_dtypes=True).then_inc(k_pool, 1)
            pool.memset(ones16[:, :], 1.0).then_inc(k_ones, 1)
            pool.memset(onesS[:, :], 1.0).then_inc(k_ones, 1)
            pool.wait_ge(ld_w, 80)
            pool.wait_ge(cut_ok, 2)
            for n, src in enumerate((w1n[:, :, :].rearrange("p k d -> p (k d)"), w2n[:, :])):
                pool.tensor_scalar(qneg[:, :], src, ncut[:, n:n + 1], None, ALU.is_lt).then_inc(cmp_ok, 1)
                pool.tensor_scalar(qpos[:, :], src, cut[:, n:n + 1], None, ALU.is_gt).then_inc(cmp_ok, 1)
                pool.wait_ge(cmp_ok, 2 * n + 2)
                pool.tensor_tensor(q16[:, n, :], qpos[:, :], qneg[:, :], ALU.subtract).then_inc(q_ok, 1)
                pool.wait_ge(q_ok, n + 1)
            pool.wait_ge(tap_ok, 1)
            pool.tensor_tensor(conv[:, 2, :], conv[:, 2, :], taps[0], ALU.add).then_inc(tap_sum, 1)

            def scale_out(t):
                if t == 0:
                    pool.wait_ge(yi_ok, 1)
                else:
                    pool.wait_ge(ys_ok, t)
                pool.tensor_tensor(y0[:, t, :].rearrange("p (h d) -> p h d", h=H),
                                   ys[:, t % 4, :].rearrange("p (h d) -> p h d", h=H),
                                   eT[:, t, H:2 * H].unsqueeze(2).to_broadcast([P, H, HD]), ALU.mult).then_inc(y0_ok, 1)

            def norm_out(b, c):
                if isinstance(b, int) and b == 0:
                    pool.wait_ge(y0_ok, SUP * (c + 1))
                    if c == 0:
                        pool.wait_ge(tr_sb, TPB - 2)
                    else:
                        pool.wait_ge(r_sb, 1)
                wait_free(pool, yrT_ps, 2 * b + c - 1)
                pool.tensor_tensor(yr[:, c, :, :].rearrange("p t (h d) -> p t h d", h=H),
                                   y0[:, SUP * c:SUP * (c + 1), :].rearrange("p t (h d) -> p t h d", h=H),
                                   rT[:, SUP * c:SUP * (c + 1), bass.ds(b * 2 * H, H)].unsqueeze(3).to_broadcast([P, SUP, H, HD]),
                                   ALU.mult).then_inc(yr_ok, 1)

            for t in range(TPB):
                c = t % 2
                pool.wait_ge(tr_sb, t + 1)
                if t == 0:
                    pool.wait_ge(e_sb, 1)
                wait_free(pool, st_ps, t - 1)
                pool.tensor_tensor(xp[:, c, :].rearrange("p (h d) -> p h d", h=H),
                                   bcx[:, t % 3, 2 * D:].rearrange("p (h d) -> p h d", h=H),
                                   eT[:, t, 0:H].unsqueeze(2).to_broadcast([P, H, HD]), ALU.mult).then_inc(xp_ok, 1)
                pool.wait_ge(xp_ok, t + 1)
                wait_free(pool, cum_ps, t - 1)
                pool.tensor_tensor(zz[:, c, :].rearrange("p (h d n) -> p h d n", h=H, d=HD),
                                   bcx[:, t % 3, D:2 * D].rearrange("p (h n) -> p h n", h=H).unsqueeze(2).to_broadcast([P, H, HD, HD]),
                                   xp[:, c, :].rearrange("p (h d) -> p h d", h=H).unsqueeze(3).to_broadcast([P, H, HD, HD]),
                                   ALU.mult).then_inc(z_ok, 1)

                if t > 1:
                    scale_out(t - 2)
            norm_out(0, 0)
            scale_out(TPB - 2)
            scale_out(TPB - 1)

            def rstd(i, mv, neg, neg_ok, ve, ln_step, rs, nm, free):
                pool.wait_ge(neg_ok, i + 1)
                wait_free(pool, free, i)
                pool.tensor_tensor(ve[:, :], mv[:, :, 1], epsT[:, :], ALU.add).then_inc(ln_step, 1)
                pool.wait_ge(ln_step, 3 * i + 1)
                pool.tensor_tensor(rs[:, :], ve[:, :], mhalf[:, :], ALU.pow).then_inc(ln_step, 1)
                pool.wait_ge(ln_step, 3 * i + 2)
                pool.tensor_tensor(nm[:, :], neg[:, :], rs[:, :], ALU.mult).then_inc(ln_step, 1)

            def rstd1(b, c):
                rstd(2 * b + c, mv1, neg1, neg1_ok, ve1, ln1_step, rs1, nm1, x1_ok)

            def rstd2(b, c):
                rstd(2 * b + c, mv2, neg2, neg2_ok, ve2, ln2_step, rs2, nm2, x2_ok)

            def body(b, c, prev=None, nxt=None, then=None, before=None):
                if then is not None:
                    norm_out(*then)
                if prev is not None:
                    rstd2(*prev)
                if then is not None:
                    rstd1(*then)

            norm_out(0, 1)
            rstd1(0, 0)
            rstd1(0, 1)
            body(0, 0, nxt=(0, 1), then=(1, 0))
            body(0, 1, (0, 0), (1, 0), (1, 1))
            with pool.Fori(1, B - 1) as b:
                body(b, 0, (b - 1, 1), (b, 1), (b + 1, 0), (b - 1, 0))
                body(b, 1, (b, 0), (b + 1, 0), (b + 1, 1), (b - 1, 1))
            body(B - 1, 0, (B - 2, 1), (B - 1, 1), before=(B - 2, 0))
            body(B - 1, 1, (B - 1, 0), before=(B - 2, 1))
            rstd2(B - 1, 1)

            def scatter(b, c):
                i = 2 * b + c
                wait_free(pool, scat[c], 16 * SUP * b)
                pool.wait_ge(slf_ok, i + 1)
                pool.tensor_tensor(slp[:, :], slf[:, :], ones[:, 0:SUP], ALU.subtract).then_inc(slp_ok, 1)
                pool.wait_ge(k_ones, 3)
                pool.wait_ge(slp_ok, i + 1)
                pool.tensor_copy(slot[:, c, :], slp[:, :]).then_inc(slot_ok, 1)
                pool.wait_ge(slots_init, 16)
                pool.wait_ge(slot_ok, i + 1)
                for j in range(SUP):
                    pool.indirect_dma_start(out=slots, out_offset=bass.IndirectOffsetOnAxis(ap=slot[:, c, j:j + 1], axis=0),
                                            in_=rows[:, c, j, :], in_offset=None,
                                            bounds_check=E * CAP - 1, oob_is_err=False).then_inc(scat[c], 16)

            scatter(0, 0)
            scatter(0, 1)
            with pool.Fori(1, B) as b:
                scatter(b, 0)
                scatter(b, 1)

            def scaled_mean(k, c):
                e = 2 * k + c
                pool.wait_ge(neg4_ok, e + 1)
                pool.wait_ge(rs4_ok, e + 1)
                pool.tensor_tensor(nm4[:, :], neg4[:, :], rs4[:, :], ALU.mult).then_inc(ln4_step, 1)

            def put_rows(k, c):
                for n in range(2):
                    pool.wait_ge(stored[n], 16 * B)
                pool.wait_ge(y4_ok, 2 * k + c + 1)
                for j in range(CT):
                    pool.indirect_dma_start(out=out.rearrange("b s d -> (b s) d"),
                                            out_offset=bass.IndirectOffsetOnAxis(ap=xr[:, c, j, D + 1:D + 2].bitcast(U32), axis=0),
                                            in_=y4[:, c, j, :], in_offset=None,
                                            bounds_check=TOK - 1, oob_is_err=False).then_inc(put[c], 16)

            with pool.Fori(0, E // 2) as k:
                scaled_mean(k, 0)
                put_rows(k, 0)
                scaled_mean(k, 1)
                put_rows(k, 1)

        @block_.scalar
        def _(act):
            act.dma_start(convw[:, :, :], conv_w.rearrange("(g p) k -> p g k", p=P)).then_inc(ld_small, 16)
            act.dma_start(convb[:, :], conv_b.rearrange("(g p) -> p g", p=P), allow_slow_non_contiguous=True).then_inc(ld_small, 16)
            act.dma_start(ab[:, 0:1], A_param.rearrange("(h o) -> h o", o=1)).then_inc(ld_small, 16)
            act.dma_start(ab[:, 1:2], dt_bias.rearrange("(h o) -> h o", o=1)).then_inc(ld_small, 16)
            nc.scalar.preload_act_table_set("natural_log_exp_and_others")
            act.wait_ge(win_ps, 1)
            nc.scalar.copy(winT[:, :], bank(0)[:, 0:3 * D]).then_inc(win_sb, 1)
            nc.scalar.copy(wdtT[:, :].rearrange("p (a h) -> p a h", a=2),
                           bank(0)[:, 3 * D:3 * D + H].unsqueeze(1).to_broadcast([P, 2, H])).then_inc(win_sb, 1)
            nc.scalar.copy(acol[:, :], bank(0)[:, 3 * D + H:3 * D + H + 2]).then_inc(win_sb, 1)

            def x_out(n):
                act.wait_ge(xT_ps, n + 1)
                nc.scalar.copy(xT[:, n * 512:(n + 1) * 512], bank(1)).then_inc(xT_sb[0], 1)

            x_out(0)
            for n in range(6):
                act.wait_ge(proj_ps, n + 1)
                if n == 0:
                    act.wait_ge(ld_small, 64)
                if n == 3:
                    act.wait_ge(wsum_ps, 1)
                    nc.scalar.activation(cut[:, :], bank(0)[:, 0:2], ACT.Copy, scale=0.5 / (F * D), bias=0.5 * EPS).then_inc(cut_ok, 1)
                    nc.scalar.activation(ncut[:, :], bank(0)[:, 0:2], ACT.Copy, scale=-0.5 / (F * D), bias=-0.5 * EPS).then_inc(cut_ok, 1)
                nc.scalar.activation(conv[:, n // 2, 512 * (n % 2):512 * (n % 2) + 512], bank(3 + n % 3), ACT.Identity,
                                     scale=convw[:, n // 2, TAPS - 1:TAPS], bias=convb[:, n // 2:n // 2 + 1])
                nc.scalar.copy(craw[:, n // 2, TAPS - 1 + 512 * (n % 2):TAPS - 1 + 512 * (n % 2) + 512],
                               bank(3 + n % 3)).then_inc(proj_sb, 1)
                if n % 2 == 0:
                    x_out(2 + n)
            act.wait_ge(dt_ps, NS)
            act.wait_ge(win_sb, 3)
            nc.scalar.activation(s1[:, :], pair(6), ACT.Abs, bias=acol[:, 1:2]).then_inc(dt_abs, 1)
            act.wait_ge(dt_abs, 1)
            nc.scalar.activation(s2[:, :], s1[:, :], ACT.Exp, scale=-1.0).then_inc(act1, 1)
            act.wait_ge(act1, 1)
            nc.scalar.activation(s3[:, :], s2[:, :], ACT.Ln, bias=1.0).then_inc(dt_ln, 1)
            for k, tap in enumerate(taps):
                nc.scalar.activation(tap, craw[:, 2, k:k + S], ACT.Copy, scale=convw[:, 2, k:k + 1]).then_inc(tap_ok, 1)
            act.wait_ge(cum_ok, 1)
            act.wait_ge(nega_ok, 1)
            nc.scalar.activation(expn[:, :], cum[:, :], ACT.Exp, scale=nega[:, 0:1]).then_inc(exp_ok, 1)
            act.wait_ge(e_ps, 1)
            nc.scalar.copy(eT[:, :, :], bank(3)[:, 0:TPB * 2 * H].rearrange("p (t k) -> p t k", t=TPB)).then_inc(e_sb, 1)

            act.wait_ge(wT_ps, 1)
            nc.scalar.copy(woutT[:, :], bank(5)[:, 0:D]).then_inc(wT_sb, 1)
            nc.scalar.copy(wvT[:, :], bank(5)[:, D:2 * D]).then_inc(wT_sb, 1)
            nc.scalar.copy(eb1T[:, :], bank(5)[:, 2 * D:2 * D + E * FB]).then_inc(wT_sb, 1)
            nc.scalar.copy(woT[:, :], bank(5)[:, 3 * D:4 * D]).then_inc(wT_sb, 1)
            def chunk_out(t):
                act.wait_ge(tr_ps, t + 1)
                wait_free(act, st_ps, t - 2)
                wait_free(act, z_ok, t - 2)
                wait_free(act, cz_ok, t - 2)
                last = nc.scalar.copy(bcx[:, t % 3, :], bank(t % 2)[:, 0:3 * D])
                if t >= 2:
                    last = nc.scalar.copy(rT[:, t - 2, :], bank(t % 2)[:, 3 * D:4 * D])
                last.then_inc(tr_sb, 1)

            chunk_out(0)
            act.wait_ge(cs_ok, 1)
            nc.scalar.activation(s4[:, :], s5[:, :], ACT.Ln).then_inc(lncs_ok, 1)
            chunk_out(1)
            act.wait_ge(q_ps, 1)
            nc.scalar.copy(qT[:, :, :, :].rearrange("p a k f -> p (a k f)"), bank(4).bitcast(F16)).then_inc(q_sb, 1)
            act.wait_ge(wg_ps, 1)
            nc.scalar.copy(wog[:, D:ME], bank(5)[:, 0:E])
            nc.scalar.copy(wgsum[:, :], bank(5)[:, E:2 * E]).then_inc(wg_sb, 1)
            act.wait_ge(lr_ok, 1)
            nc.scalar.activation(s1[:, :], s2[:, :], ACT.Exp).then_inc(r_ok, 1)
            for t in range(2, TPB):
                chunk_out(t)
            def yrT_out(b, c):
                i = 2 * b + c
                act.wait_ge(yrT_ps, i + 1)
                wait_free(act, ao_ps, i)
                nc.scalar.copy(yrT[:, :], bank(0)).then_inc(yrT_sb, 1)

            yrT_out(0, 0)
            act.wait_ge(r_ps, 1)
            nc.scalar.copy(rT[:, TPB - 2:TPB, :].rearrange("p t k -> p (t k)"), bank(6)[:, 0:2 * P]).then_inc(r_sb, 1)

            def x1_norm(b, c):
                i = 2 * b + c
                act.wait_ge(ln1_step, 3 * i + 3)
                wait_free(act, r2_ok, i - 1)
                for j in range(SUP):
                    last = nc.scalar.activation(x1[:, c, j * P:(j + 1) * P], r1[:, j * P:(j + 1) * P], ACT.Identity,
                                                scale=rs1[:, j:j + 1], bias=nm1[:, j:j + 1])
                last.then_inc(x1_ok, 1)

            def x1_high(b, c):
                i = 2 * b + c
                act.wait_ge(x1T_ps, i + 1)
                wait_free(act, h_ps, FB * (i - 1))
                nc.scalar.copy(x1h[:, c, :], bank(2)).then_inc(x1h_ok, 1)

            def hidden_high(b, c, f):
                i = 2 * b + c
                act.wait_ge(h_ps, FB * i + f + 1)
                if f == 0:
                    wait_free(act, ff_ps, i - 1)
                nc.scalar.activation(hh[:, c, f, :], bank(3 + f % 2), ACT.Relu).then_inc(hh_ok, 1)

            def x2_norm(b, c):
                i = 2 * b + c
                act.wait_ge(ln2_step, 3 * i + 3)
                for j in range(SUP):
                    last = nc.scalar.activation(x2s[:, c, j * P:(j + 1) * P], r2[:, j * P:(j + 1) * P], ACT.Identity,
                                                scale=rs2[:, j:j + 1], bias=nm2[:, j:j + 1])
                last.then_inc(x2_ok, 1)

            def x2T_out(b, c):
                i = 2 * b + c
                act.wait_ge(x2T_ps, i + 1)
                nc.scalar.copy(x2T[:, bass.ds(b * 1024 + c * 512, 512)], bank(6)).then_inc(x2T_sb, 1)
                if c == 1:
                    nc.scalar.copy(gram[:, bass.ds(b, 1), :], bank(7)[:, 0:D].unsqueeze(1)).then_inc(gram_sb, 1)

            def body(b, c, prev=None, nxt=None, then=None, before=None):
                hidden_high(b, c, 0)
                hidden_high(b, c, 1)
                if nxt is not None:
                    x1_norm(*nxt)
                if before is not None:
                    x2T_out(*before)
                    act.wait_ge(x2_kept[c], 16 * (before[0] + 1))
                hidden_high(b, c, 2)
                if nxt is not None:
                    x1_high(*nxt)
                if then is not None:
                    yrT_out(*then)
                hidden_high(b, c, 3)
                if prev is not None:
                    x2_norm(*prev)

            yrT_out(0, 1)
            x1_norm(0, 0)
            x1_high(0, 0)
            body(0, 0, nxt=(0, 1), then=(1, 0))
            body(0, 1, (0, 0), (1, 0), (1, 1))
            with act.Fori(1, B - 1) as b:
                body(b, 0, (b - 1, 1), (b, 1), (b + 1, 0), (b - 1, 0))
                body(b, 1, (b, 0), (b + 1, 0), (b + 1, 1), (b - 1, 1))
            body(B - 1, 0, (B - 2, 1), (B - 1, 1), before=(B - 2, 0))
            body(B - 1, 1, (B - 1, 0), before=(B - 2, 1))
            x2T_out(B - 1, 0)
            x2_norm(B - 1, 1)
            x2T_out(B - 1, 1)

            act.wait_ge(m1_ps, 1)
            nc.scalar.copy(gq[:, :], bank(1)).then_inc(m1_sb, 1)
            act.wait_ge(lg_ok, 1)
            nc.scalar.activation(ea[:, :, :], lg[:, :, :], ACT.Exp).then_inc(ea_ok, 1)
            act.wait_ge(m4_ps, 1)
            nc.scalar.copy(p1[:, :].rearrange("p (a n) -> p a n", a=2), PS[:, 4:6, 0:2 * ME]).then_inc(m4_sb, 1)
            act.wait_ge(m5_ps, 1)
            nc.scalar.copy(mix[:, :].rearrange("p (a n) -> p a n", a=2), PS[:, 1:3, 0:2 * ME]).then_inc(mix_ok, 1)

            def x3_norm(b, c):
                i = 2 * b + c
                act.wait_ge(mv3_ok, i + 1)
                nc.scalar.activation(lv3[:, :], mv3[:, :, 1], ACT.Ln, bias=epsT[:, 0:1]).then_inc(lv3_ok, 1)
                wait_free(act, oh_ok, i)
                act.wait_ge(lv3_ok, i + 1)
                nc.scalar.activation(rs3[:, :], lv3[:, :], ACT.Exp, scale=-0.5).then_inc(rs3_ok, 1)
                nc.scalar.activation(sq3[:, :], lv3[:, :], ACT.Exp, scale=-1.0).then_inc(s4_step, 1)
                act.wait_ge(s4_step, 3 * i + 1)
                nc.scalar.activation(lq3[:, :], sq3[:, :], ACT.Ln, scale=-EPS, bias=onep[:, 0:1]).then_inc(s4_step, 1)
                act.wait_ge(s4_step, 3 * i + 2)
                nc.scalar.activation(s43[:, :], lq3[:, :], ACT.Exp, scale=-0.5).then_inc(s4_step, 1)
                act.wait_ge(nm3_ok, i + 1)
                wait_free(act, scat[c], 16 * SUP * b)
                for j in range(SUP):
                    last = nc.scalar.activation(rows[:, c, j, 0:D], r3[:, j * P:(j + 1) * P], ACT.Identity,
                                                scale=rs3[:, j:j + 1], bias=nm3[:, j:j + 1])
                last.then_inc(x3_ok, 1)

            def x4_norm(b, c):
                i = 2 * b + c
                act.wait_ge(s4_step, 3 * i + 3)
                act.wait_ge(x3_ok, i + 1)
                wait_free(act, stored[c], 16 * b)
                for j in range(SUP):
                    last = nc.scalar.activation(x4[:, c, j * P:(j + 1) * P], rows[:, c, j, 0:D], ACT.Copy, scale=s43[:, j:j + 1])
                last.then_inc(x4_ok, 1)

            def gate_exp(b, c):
                i = 2 * b + c
                act.wait_ge(gl_ok, i + 1)
                nc.scalar.activation(ge[:, :, :], gl[:, :, :], ACT.Exp).then_inc(ge_ok, 1)

            def body(b, c, nxt):
                gate_exp(b, c)
                if nxt is not None:
                    x3_norm(*nxt)
                    x4_norm(*nxt)

            act.wait_ge(carry_ok, 1)
            x3_norm(0, 0)
            x4_norm(0, 0)
            body(0, 0, (0, 1))
            with act.Fori(0, B - 1) as b:
                body(b, 1, (b + 1, 0))
                body(b + 1, 0, (b + 1, 1))
            body(B - 1, 1, None)

            def xeT_out(k, c):
                e = 2 * k + c
                act.wait_ge(xeT_ps, e + 1)
                wait_free(act, eh_ps, FB * (e - 1))
                nc.scalar.copy(xeT[:, c, :], pair(0)[:, 0:CAP]).then_inc(xeT_sb, 1)

            def expert_hidden(k, c, f):
                e = 2 * k + c
                act.wait_ge(eh_ps, FB * e + f + 1)
                if f == 0:
                    wait_free(act, ey_ps, e)
                n = 2 + 2 * (f % 2)
                nc.scalar.activation(eh[:, f, :].rearrange("p (a n) -> p a n", a=2), PS[:, n:n + 2, 0:CAP // 2], ACT.Relu,
                                     bias=eb1T[:, bass.ds(FB * e + f, 1)]).then_inc(eh_ok, 1)

            def y4_norm(k, c):
                e = 2 * k + c
                act.wait_ge(mv4_ok, e + 1)
                nc.scalar.activation(lv4[:, :], mv4[:, :, 1], ACT.Ln, bias=epsT[:, 0:1]).then_inc(lv4_ok, 1)
                act.wait_ge(lv4_ok, e + 1)
                nc.scalar.activation(rs4[:, :], lv4[:, :], ACT.Exp, scale=-0.5).then_inc(rs4_ok, 1)
                act.wait_ge(ln4_step, e + 1)
                act.wait_ge(rs4_ok, e + 1)
                wait_free(act, put[c], 16 * CT * k)
                for j in range(CT):
                    last = nc.scalar.activation(y4[:, c, j, :], r4[:, j, :], ACT.Identity,
                                                scale=rs4[:, j:j + 1], bias=nm4[:, j:j + 1])
                last.then_inc(y4_ok, 1)

            def expert(k, c, nxt, prev):
                for f in range(FB):
                    expert_hidden(k, c, f)
                if nxt is not None:
                    xeT_out(*nxt)
                if prev is not None:
                    y4_norm(*prev)

            xeT_out(0, 0)
            expert(0, 0, (0, 1), None)
            expert(0, 1, (1, 0), (0, 0))
            expert(1, 0, (1, 1), (0, 1))
            with act.Fori(1, E // 2 - 1) as k:
                expert(k, 1, (k + 1, 0), (k, 0))
                expert(k + 1, 0, (k + 1, 1), (k, 1))
            expert(E // 2 - 1, 1, None, (E // 2 - 1, 0))
            y4_norm(E // 2 - 1, 1)

        @block_.vector
        def _(dve):
            V = nc.vector
            step = [0]

            def link(ins):
                step[0] += 1
                ins.then_inc(dve1, 1)
                dve.wait_ge(dve1, step[0])

            V.memset(craw[:, :, 0:TAPS - 1], 0.0).then_inc(pad_ok, 1)
            V.memset(selA[:, :, :, :], 0.0)
            V.memset(empty[:, :], 0.0).then_inc(k_empty, 1)
            dve.wait_ge(k_empty, 1)
            V.memset(empty[:, D + 1:D + 2].bitcast(I32), TOK).then_inc(k_empty, 1)
            dve.wait_ge(k_pool, 1)
            for a in range(2):
                V.tensor_scalar(selA[:, :, a, :], ident[0:H, 0:H].unsqueeze(1).to_broadcast([H, B, H]),
                                1.0 - 2.0 * a, None, ALU.mult)
                last = V.tensor_copy(selB[:, :, a, :], ident[0:H, 0:H].unsqueeze(1).to_broadcast([H, B, H]))
            last.then_inc(k_sel, 1)
            V.memset(sign2[:, :, 0], -1.0)
            V.memset(sign2[:, :, 1], 1.0)
            V.memset(eps2[:, :, 0], 0.0)
            V.memset(eps2[:, :, 1], EPS)
            V.memset(epsT[:, :], EPS)
            V.memset(mhalf[:, :], -0.5)
            V.memset(base16[:, :], 0.0)
            V.memset(b1s[:, :], 0.0)
            V.memset(b2s[:, :], 0.0)
            link(V.memset(eb2s[:, :], 0.0))
            dve.wait_ge(k_pool, 7)
            V.tensor_scalar(lim8[:, :], base8[:, :], float(CAP), None, ALU.add)
            V.tensor_copy(base16[0:1, :], base8[0:1, :])
            V.tensor_reduce(diag8[:, :], ident[:, :].rearrange("p (h d) -> p d h", h=H), axis=AX, op=ALU.add)
            V.tensor_copy(ident16[:, :], ident[:, :])
            V.tensor_copy(upper16[:, :], upper[:, :]).then_inc(k_const, 1)
            def x_out(n):
                dve.wait_ge(xT_ps, n + 1)
                V.tensor_copy(xT[:, n * 512:(n + 1) * 512], bank(2)).then_inc(xT_sb[1], 1)

            x_out(1)
            dve.wait_ge(ld_w, 80)
            V.tensor_reduce(wabs[:, 0:1], w1n[:, :, :].rearrange("p k d -> p (k d)"), axis=AX, op=ALU.add,
                            apply_absolute_value=True)
            V.tensor_reduce(wabs[:, 1:2], w2n[:, :], axis=AX, op=ALU.add,
                            apply_absolute_value=True).then_inc(wabs_ok, 1)
            dve.wait_ge(win_sb, 3)
            V.tensor_scalar(nega[:, :], acol[:, 0:1], -1.0, None, ALU.mult).then_inc(nega_ok, 1)
            dve.wait_ge(ld_small, 64)
            dve.wait_ge(pad_ok, 1)

            def convolve(n, k):
                if k == 0:
                    dve.wait_ge(proj_sb, 2 * n + 2)
                ins = V.scalar_tensor_tensor(out=conv[:, n, :], in0=craw[:, n, k:k + S],
                                             scalar=convw[:, n, k:k + 1], in1=conv[:, n, :],
                                             op0=ALU.mult, op1=ALU.add)
                if k < TAPS - 2:
                    link(ins)
                else:
                    ins.then_inc(conv_ok, 1)

            x_out(3)
            convolve(0, 0)
            convolve(0, 1)
            x_out(5)
            convolve(0, 2)
            x_out(7)
            for k in range(TAPS - 1):
                convolve(1, k)
            dve.wait_ge(dt_abs, 1)
            V.tensor_scalar(s4[:, :], pair(6), acol[:, 1:2], 0.0, ALU.add, ALU.max).then_inc(dt_pos, 1)
            dve.wait_ge(dt_ln, 1)
            dve.wait_ge(dt_pos, 1)
            link(V.tensor_tensor(s3[:, :], s3[:, :], s4[:, :], ALU.add))
            dve.wait_ge(k_ones, 3)
            V.tensor_tensor_scan(cum[:, :], onesS[:, :], s3[:, :], 0.0, ALU.mult, ALU.add).then_inc(cum_ok, 1)
            dve.wait_ge(tap_ok, 3)
            link(V.tensor_tensor(taps[1], taps[1], taps[2], ALU.add))
            dve.wait_ge(tap_sum, 1)
            V.tensor_tensor(conv[:, 2, :], conv[:, 2, :], taps[1], ALU.add).then_inc(conv_ok, 1)
            dve.wait_ge(exp_ok, 1)
            V.tensor_tensor_scan(s5[:, :], onesS[:, :], expn[:, :], 0.0, ALU.mult, ALU.add).then_inc(cs_ok, 1)
            dve.wait_ge(lncs_ok, 1)
            V.scalar_tensor_tensor(out=s2[:, :], in0=cum[:, :], scalar=nega[:, 0:1], in1=s4[:, :],
                                   op0=ALU.mult, op1=ALU.subtract).then_inc(lr_ok, 1)
            dve.wait_ge(ld_bias, 48)
            for src, dst in ((b1r, b1s), (b2r, b2s), (eb2r, eb2s)):
                link(V.tensor_copy(dst[0:1, :], src[0:1, :]))
                last = V.tensor_tensor(dst[32:33, :], src[0:1, :], dst[0:1, :], ALU.subtract)
            last.then_inc(bias_ok, 1)

            def add_state(t):
                dve.wait_ge(off_ps, t)
                dve.wait_ge(yi_ok, t + 1)
                wait_free(dve, y0_ok, t - 3)
                V.tensor_tensor(ys[:, t % 4, :], bank(6)[:, 0:D], yi[:, t % 2, :], ALU.add).then_inc(ys_ok, 1)

            for t in range(TPB):
                c = t % 2
                wait_free(dve, yi_ok, t - 1)
                dve.wait_ge(cum_ps, t + 1)
                V.tensor_tensor(cz[:, c, :].rearrange("p (h d n) -> p h d n", h=H, d=HD),
                                pair(2 + 2 * c).rearrange("p (h d n) -> p h d n", h=H, d=HD),
                                bcx[:, t % 3, 0:D].rearrange("p (h n) -> p h n", h=H).unsqueeze(2).to_broadcast([P, H, HD, HD]),
                                ALU.mult).then_inc(cz_ok, 1)
                if t < TPB - 1:
                    dve.wait_ge(st_ps, t + 1)
                    wait_free(dve, off_ps, t - 1)
                    V.tensor_tensor(st[:, c, :], bank(7)[:, 0:D], block[:, :], ALU.mult).then_inc(st_ok, 1)
                dve.wait_ge(cz_ok, t + 1)
                wait_free(dve, ys_ok, t - 2)
                if t == 0:
                    V.tensor_reduce(ys[:, 0, :], cz[:, c, :].rearrange("p (k n) -> p k n", n=HD), axis=AX, op=ALU.add).then_inc(yi_ok, 1)
                else:
                    V.tensor_reduce(yi[:, t % 2, :], cz[:, c, :].rearrange("p (k n) -> p k n", n=HD), axis=AX, op=ALU.add).then_inc(yi_ok, 1)
                    add_state(t)
            def moments(i, r, r_ok, st, st_ok, mv, mv_ok):
                dve.wait_ge(r_ok, i + 1)
                for j in range(SUP):
                    last = V.bn_stats(st[:, j, :], r[:, j * P:(j + 1) * P])
                last.then_inc(st_ok, 1)
                dve.wait_ge(k_const, 1)
                dve.wait_ge(st_ok, i + 1)
                for j in range(SUP):
                    last = V.bn_aggr(mv[:, j, :], st[:, j, :])
                last.then_inc(mv_ok, 1)

            def add1(b, c):
                i = 2 * b + c
                dve.wait_ge(ao_ps, i + 1)
                wait_free(dve, x1_ok, i)
                V.tensor_tensor(r1[:, :], bank(1), xt[:, :, :].rearrange("p t d -> p (t d)")[:, bass.ds(b * 1024 + c * 512, 512)],
                                ALU.add).then_inc(r1_ok, 1)

            def moments1(b, c):
                i = 2 * b + c
                moments(i, r1, r1_ok, st1, st1_ok, mv1, mv1_ok)
                dve.wait_ge(mv1_ok, i + 1)
                V.tensor_scalar(neg1[:, :], mv1[:, :, 0], -1.0, None, ALU.mult).then_inc(neg1_ok, 1)

            def x1_low(b, c):
                i = 2 * b + c
                dve.wait_ge(x1h_ok, i + 1)
                V.tensor_tensor(x1l[:, c, :], bank(2), x1h[:, c, :], ALU.subtract).then_inc(x1l_ok, 1)

            def hidden_low(b, c, f):
                i = 2 * b + c
                dve.wait_ge(hh_ok, FB * i + f + 1)
                V.scalar_tensor_tensor(out=hl[:, c, f, :], in0=bank(3 + f % 2), scalar=0.0, in1=hh[:, c, f, :],
                                       op0=ALU.max, op1=ALU.subtract).then_inc(hl_ok, 1)

            def add2(b, c):
                i = 2 * b + c
                dve.wait_ge(ff_ps, i + 1)
                wait_free(dve, x2_ok, i)
                V.tensor_tensor(r2[:, :], bank(5), x1[:, c, :], ALU.add).then_inc(r2_ok, 1)

            def moments2(b, c):
                i = 2 * b + c
                moments(i, r2, r2_ok, st2, st2_ok, mv2, mv2_ok)
                dve.wait_ge(mv2_ok, i + 1)
                V.tensor_scalar(neg2[:, :], mv2[:, :, 0], -1.0, None, ALU.mult).then_inc(neg2_ok, 1)

            def body(b, c, prev=None, nxt=None, then=None, before=None):
                hidden_low(b, c, 0)
                hidden_low(b, c, 1)
                if prev is not None:
                    add2(*prev)
                    moments2(*prev)
                hidden_low(b, c, 2)
                if nxt is not None:
                    x1_low(*nxt)
                if then is not None:
                    add1(*then)
                hidden_low(b, c, 3)
                if then is not None:
                    moments1(*then)

            add1(0, 0)
            moments1(0, 0)
            add1(0, 1)
            x1_low(0, 0)
            moments1(0, 1)
            body(0, 0, nxt=(0, 1), then=(1, 0))
            body(0, 1, (0, 0), (1, 0), (1, 1))
            with dve.Fori(1, B - 1) as b:
                body(b, 0, (b - 1, 1), (b, 1), (b + 1, 0), (b - 1, 0))
                body(b, 1, (b, 0), (b + 1, 0), (b + 1, 1), (b - 1, 1))
            body(B - 1, 0, (B - 2, 1), (B - 1, 1), before=(B - 2, 0))
            body(B - 1, 1, (B - 1, 0), before=(B - 2, 1))
            add2(B - 1, 1)
            moments2(B - 1, 1)

            dve.wait_ge(ld_l1, 64)
            V.tensor_scalar(tau32[:, :], tauc[:, :], float(S) ** -0.5, None, ALU.mult)
            step = [0]

            def link2(ins):
                step[0] += 1
                ins.then_inc(mixs, 1)
                dve.wait_ge(mixs, step[0])

            dve.wait_ge(m2_ps, 1)
            link2(V.tensor_tensor(dm[:, :, :], bank(2).rearrange("p (b f) -> p b f", b=B),
                                  block[:, :].unsqueeze(1).to_broadcast([P, B, D]), ALU.mult))
            link2(V.tensor_reduce(dc[:, :, :], dm[:, :, :].rearrange("p b (h d) -> p b d h", h=H), axis=AX, op=ALU.add))
            V.tensor_tensor(dq[:, :, :], dc[:, :, :], diag8[:, :].unsqueeze(1).to_broadcast([P, B, HD]),
                            ALU.mult).then_inc(dq_ok, 1)
            dve.wait_ge(dq_ok, 1)
            link2(V.tensor_reduce(qc[:, :], dq[:, :, :], axis=AX, op=ALU.add))
            dve.wait_ge(m3_ps, 1)
            link2(V.scalar_tensor_tensor(out=lg[:, :, :], in0=dc[:, :, :], scalar=2.0,
                                         in1=bank(3)[:, 0:B * HD].rearrange("p (b d) -> p b d", b=B),
                                         op0=ALU.mult, op1=ALU.subtract))
            link2(V.tensor_tensor(lg[:, :, :], lg[:, :, :], qc[:, :].unsqueeze(2).to_broadcast([P, B, HD]), ALU.subtract))
            link2(V.tensor_scalar(lg[:, :, :], lg[:, :, :], tau32[:, 0:1], None, ALU.mult))
            link2(V.tensor_reduce(mx[:, :], lg[:, :, :], axis=AX, op=ALU.max))
            V.tensor_tensor(lg[:, :, :], lg[:, :, :], mx[:, :].unsqueeze(2).to_broadcast([P, B, HD]),
                            ALU.subtract).then_inc(lg_ok, 1)
            dve.wait_ge(ea_ok, 1)
            link2(V.tensor_reduce(mx[:, :], ea[:, :, :], axis=AX, op=ALU.add))
            link2(V.reciprocal(mx[:, :], mx[:, :]))
            link2(V.tensor_tensor(ea[:, :, :], ea[:, :, :], mx[:, :].unsqueeze(2).to_broadcast([P, B, HD]), ALU.mult))
            V.tensor_tensor(ad[:, :, :].rearrange("p b (h d) -> p b h d", h=H),
                            ea[:, :, :].unsqueeze(2).to_broadcast([P, B, H, HD]),
                            block[:, :].rearrange("p (h d) -> p h d", h=H).unsqueeze(1).to_broadcast([P, B, H, HD]),
                            ALU.mult).then_inc(ad_ok, 1)

            V.memset(carry[:, :], 0.0)
            V.memset(onep[:, :], 1.0 + EPS).then_inc(carry_ok, 1)

            def attended(c, first, last):
                return PS[:, 2 * c:2 * c + 2, 0:2 * ME].rearrange("p a (t k) -> p a t k", k=ME)[:, :, :, first:last]

            def add3(b, c):
                i = 2 * b + c
                dve.wait_ge(o3_ps, i + 1)
                wait_free(dve, x3_ok, i)
                V.tensor_tensor(r3[:, :].rearrange("p (a t d) -> p a t d", a=2, t=2), attended(c, 0, D),
                                x2k[:, bass.ds(b * 1024 + c * 512, 512)].rearrange("p (a t d) -> p a t d", a=2, t=2),
                                ALU.add).then_inc(r3_ok, 1)

            def moments3(b, c):
                i = 2 * b + c
                moments(i, r3, r3_ok, st3, st3_ok, mv3, mv3_ok)

            G_STEPS = 11

            def gate_link(i, n, ins):
                ins.then_inc(gate_step, 1)
                dve.wait_ge(gate_step, G_STEPS * i + n)

            def gate(b, c):
                i = 2 * b + c
                by_tile = [P, SUP, E]
                dve.wait_ge(rs3_ok, i + 1)
                V.scalar_tensor_tensor(out=nm3[:, :], in0=mv3[:, :, 0], scalar=-1.0, in1=rs3[:, :],
                                       op0=ALU.mult, op1=ALU.mult).then_inc(nm3_ok, 1)
                V.tensor_tensor(l1[:, :, :].rearrange("p (a t) e -> p a t e", a=2), attended(c, D, ME),
                                rs3[:, :].rearrange("p (a t) -> p a t", a=2).unsqueeze(3).to_broadcast([P, 2, 2, E]), ALU.mult)
                dve.wait_ge(nm3_ok, i + 1)
                gate_link(i, 1, V.tensor_tensor(l2[:, :, :], wgsum[:, :].unsqueeze(1).to_broadcast(by_tile),
                                                nm3[:, :].unsqueeze(2).to_broadcast(by_tile), ALU.mult))
                gate_link(i, 2, V.tensor_tensor(l1[:, :, :], l1[:, :, :], l2[:, :, :], ALU.add))
                gate_link(i, 3, V.tensor_reduce(gmax[:, :], l1[:, :, :], axis=AX, op=ALU.max))
                V.tensor_tensor(gl[:, :, :], l1[:, :, :], gmax[:, :].unsqueeze(2).to_broadcast(by_tile), ALU.subtract).then_inc(gl_ok, 1)
                gate_link(i, 4, V.tensor_tensor(eqv[:, :, :], l1[:, :, :], gmax[:, :].unsqueeze(2).to_broadcast(by_tile), ALU.is_ge))
                gate_link(i, 5, V.tensor_tensor(eqv[:, :, :], eqv[:, :, :], rev8[:, :].unsqueeze(1).to_broadcast(by_tile), ALU.mult))
                gate_link(i, 6, V.tensor_reduce(vmax[:, :], eqv[:, :, :], axis=AX, op=ALU.max))
                V.tensor_tensor(oh[:, c, :, :], eqv[:, :, :], vmax[:, :].unsqueeze(2).to_broadcast(by_tile), ALU.is_equal).then_inc(oh_ok, 1)

            def route(b, c):
                i = 2 * b + c
                pos = bank(4 + c)[:, 0:SUP * E].rearrange("p (t e) -> p t e", t=SUP)
                dve.wait_ge(oh_ok, i + 1)
                gate_link(i, 7, V.tensor_reduce(ohs[:, :], oh[:, c, :, :].rearrange("p t e -> p e t"), axis=AX, op=ALU.add))
                dve.wait_ge(pos_ps, i + 1)
                V.tensor_tensor(carry[:, :], carry[:, :], ohs[:, :], ALU.add).then_inc(carry_ok, 1)
                gate_link(i, 8, V.tensor_tensor(sl1[:, :, :], pos, lim8[:, :].unsqueeze(1).to_broadcast([P, SUP, E]), ALU.is_gt))
                gate_link(i, 9, V.scalar_tensor_tensor(out=sl2[:, :, :], in0=sl1[:, :, :], scalar=DROP, in1=pos,
                                                       op0=ALU.mult, op1=ALU.add))
                V.tensor_tensor(sl1[:, :, :], sl2[:, :, :], oh[:, c, :, :], ALU.mult).then_inc(sl_ok, 1)
                dve.wait_ge(ge_ok, i + 1)
                gate_link(i, 10, V.tensor_reduce(gs[:, :], ge[:, :, :], axis=AX, op=ALU.add))
                wait_free(dve, scat[c], 16 * SUP * b)
                V.reciprocal(rows[:, c, :, D], gs[:, :])
                gate_link(i, 11, V.tensor_copy(rows[:, c, :, D + 1].bitcast(I32), tokid[:, bass.ds(SUP * i, SUP)]))
                wait_free(dve, slot_ok, i)
                dve.wait_ge(sl_ok, i + 1)
                V.tensor_reduce(slf[:, :], sl1[:, :, :], axis=AX, op=ALU.add).then_inc(slf_ok, 1)

            def body(b, c, nxt):
                if nxt is not None:
                    add3(*nxt)
                    moments3(*nxt)
                route(b, c)
                if nxt is not None:
                    gate(*nxt)

            dve.wait_ge(wg_sb, 1)
            for c in range(2):
                dve.wait_ge(x2_kept[c], 16 * B)
            add3(0, 0)
            moments3(0, 0)
            gate(0, 0)
            body(0, 0, (0, 1))
            body(0, 1, (1, 0))
            body(1, 0, (1, 1))
            with dve.Fori(1, B - 1) as b:
                body(b, 1, (b + 1, 0))
                body(b + 1, 0, (b + 1, 1))
            body(B - 1, 1, None)

            def expert(k, c):
                e = 2 * k + c
                dve.wait_ge(lds[c], 16 * (k + 1))
                wait_free(dve, put[c], 16 * CT * k)
                V.tensor_copy(xr[:, c, :, :], xs[:, c, :, :]).then_inc(xr_ok, 1)
                dve.wait_ge(xr_ok, e + 1)
                dve.wait_ge(ey_ps, e + 1)
                wait_free(dve, y4_ok, e)
                for j in range(CT):
                    last = V.scalar_tensor_tensor(out=r4[:, j, :], in0=pair(6)[:, j * D:(j + 1) * D],
                                                  scalar=xr[:, c, j, D:D + 1], in1=xr[:, c, j, 0:D],
                                                  op0=ALU.mult, op1=ALU.add)
                last.then_inc(r4_ok, 1)
                dve.wait_ge(r4_ok, e + 1)
                for j in range(CT):
                    last = V.bn_stats(st4[:, j, :], r4[:, j, :])
                last.then_inc(st4_ok, 1)
                dve.wait_ge(k_const, 1)
                dve.wait_ge(st4_ok, e + 1)
                for j in range(CT):
                    last = V.bn_aggr(mv4[:, j, :], st4[:, j, :])
                last.then_inc(mv4_ok, 1)
                dve.wait_ge(mv4_ok, e + 1)
                V.tensor_scalar(neg4[:, :], mv4[:, :, 0], -1.0, None, ALU.mult).then_inc(neg4_ok, 1)

            expert(0, 0)
            expert(0, 1)
            expert(1, 0)
            with dve.Fori(1, E // 2 - 1) as k:
                expert(k, 1)
                expert(k + 1, 0)
            expert(E // 2 - 1, 1)

        @block_.tensor
        def _(pe):
            T = nc.tensor
            pe.wait_ge(k_pool, 1)
            pe.wait_ge(ld_win, 32)
            for n in range(3):
                T.transpose(bank(0)[:, n * D:(n + 1) * D], win[:, n, :], ident[:, :])
            T.transpose(bank(0)[:, 3 * D:3 * D + H], windt[:, :], ident[0:H, 0:H])
            pe.wait_ge(k_sel, 1)
            pe.wait_ge(ld_small, 64)
            T.matmul(bank(0)[:, 400:401], selA[:, :, :, :].rearrange("p b a h -> p (b a h)"), ab[:, 0:1], start=True, stop=True)
            T.matmul(bank(0)[:, 401:402], selB[:, :, :, :].rearrange("p b a h -> p (b a h)"), ab[:, 1:2], start=True, stop=True).then_inc(win_ps, 1)

            def x_in(n):
                pe.wait_ge(ld_x[n // 2], 16)
                wait_free(pe, xT_sb[n % 2], n // 2)
                for j in range(SUP):
                    last = T.transpose(bank(1 + n % 2)[:, j * P:(j + 1) * P], xt[:, n * SUP + j, :], ident[:, :])
                last.then_inc(xT_ps, 1)

            def dt_in(n):
                pe.wait_ge(xT_sb[n % 2], n // 2 + 1)
                T.matmul(PS[32 * (n // 2):32 * (n // 2) + 32, 6 + n % 2, :], wdtT[:, :], xT[:, n * 512:(n + 1) * 512],
                         start=True, stop=True).then_inc(dt_ps, 1)

            x_in(0)
            x_in(1)
            pe.wait_ge(win_sb, 3)
            pe.wait_ge(xT_sb[0], 1)
            pe.wait_ge(xT_sb[1], 1)
            for n in range(6):
                if n == 2:
                    pe.wait_ge(wabs_ok, 1)
                    T.matmul(bank(0)[:, 0:2], ones[:, :], wabs[:, :], start=True, stop=True).then_inc(wsum_ps, 1)
                wait_free(pe, proj_sb, n - 2)
                T.matmul(bank(3 + n % 3), winT[:, (n // 2) * D:(n // 2 + 1) * D], xT[:, (n % 2) * 512:(n % 2 + 1) * 512],
                         start=True, stop=True).then_inc(proj_ps, 1)
                x_in(2 + n)
                dt_in(n)
            dt_in(6)
            dt_in(7)
            pe.wait_ge(proj_sb, 6)
            pe.wait_ge(ld_w, 80)
            T.transpose(bank(5)[:, 0:D], wout[:, :], ident[:, :])
            T.transpose(bank(5)[:, D:2 * D], wv[:, :], ident[:, :])
            T.transpose(bank(5)[:, 2 * D:2 * D + E * FB], eb1n[:, :], ident[0:E * FB, 0:E * FB])
            pe.wait_ge(ld_l1, 64)
            T.transpose(bank(5)[:, 3 * D:4 * D], wo, ident[:, :]).then_inc(wT_ps, 1)

            def chunk_in(t):
                pe.wait_ge(conv_ok, 3)
                if t == 0:
                    pe.wait_ge(cut_ok, 2)
                if t == 1:
                    pe.wait_ge(xT_sb[0], NS // 2)
                wait_free(pe, tr_sb, t - 1)
                for n in range(3):
                    last = T.transpose(bank(t % 2)[:, n * D:(n + 1) * D], conv[:, n, t * P:(t + 1) * P], ident[:, :])
                if t >= 2:
                    pe.wait_ge(r_ok, 1)
                    last = T.transpose(bank(t % 2)[:, 3 * D:4 * D], s1[:, (t - 2) * P:(t - 1) * P], ident[:, :])
                last.then_inc(tr_ps, 1)

            def yr_transpose(b, c):
                i = 2 * b + c
                pe.wait_ge(yr_ok, i + 1)
                wait_free(pe, yrT_sb, i)
                for j in range(SUP):
                    last = T.transpose(bank(0)[:, j * P:(j + 1) * P], yr[:, c, j, :], ident[:, :])
                last.then_inc(yrT_ps, 1)

            def attn_out(b, c):
                i = 2 * b + c
                pe.wait_ge(yrT_sb, i + 1)
                wait_free(pe, r1_ok, i)
                for j in range(SUP):
                    last = T.matmul(bank(1)[:, j * P:(j + 1) * P], yrT[:, j * P:(j + 1) * P], woutT[:, :], start=True, stop=True)
                last.then_inc(ao_ps, 1)

            pe.wait_ge(exp_ok, 1)
            for t in range(TPB):
                last = T.transpose(bank(3)[:, t * 2 * H:(t + 1) * 2 * H], expn[0:2 * H, t * P:(t + 1) * P], ident[0:2 * H, 0:2 * H])
            last.then_inc(e_ps, 1)
            chunk_in(0)
            chunk_in(1)
            pe.wait_ge(k_const, 1)
            pe.wait_ge(q_ok, 2)
            for a in range(2):
                for k in range(FB):
                    src = q16[:, a, k * P:(k + 1) * P]
                    last = T.transpose(bank(4).bitcast(F16)[:, (a * FB + k) * P:(a * FB + k + 1) * P], src, ident16[:, :])
            last.then_inc(q_ps, 1)
            pe.wait_ge(wT_sb, 4)
            T.matmul(bank(5)[:, 0:E], woT[:, :], wgs[:, :], start=True, stop=True)
            T.matmul(bank(5)[:, E:2 * E], ones[:, :], wgs[:, :], start=True, stop=True).then_inc(wg_ps, 1)
            pe.wait_ge(dt_pos, 1)
            pe.wait_ge(e_sb, 1)
            pe.wait_ge(q_sb, 1)
            pe.wait_ge(wg_sb, 1)
            for t in range(TPB):
                c = t % 2
                if 0 < t < TPB - 2:
                    chunk_in(t + 2)
                pe.wait_ge(z_ok, t + 1)
                wait_free(pe, cz_ok, t - 1)
                for a in range(2):
                    last = T.matmul(bank(2 + 2 * c + a), upper[:, :], zz[:, c, a * 512:(a + 1) * 512], start=True, stop=True)
                last.then_inc(cum_ps, 1)
                if t == 0:
                    chunk_in(2)
                if t < TPB - 1:
                    pe.wait_ge(xp_ok, t + 1)
                    wait_free(pe, st_ok, t)
                    last = T.matmul(bank(7)[:, 0:D], bcx[:, t % 3, D:2 * D], xp[:, c, :], start=True, stop=t == 0)
                    if t > 0:
                        last = T.matmul(bank(7)[:, 0:D], ident[:, :], st[:, (t - 1) % 2, :], start=False, stop=True)
                    last.then_inc(st_ps, 1)
                if t > 0:
                    pe.wait_ge(st_ok, t)
                    wait_free(pe, ys_ok, t - 1)
                    T.matmul(bank(6)[:, 0:D], conv[:, 0, t * P:(t + 1) * P], st[:, (t - 1) % 2, :], start=True, stop=True).then_inc(off_ps, 1)
            pe.wait_ge(tr_sb, TPB)
            yr_transpose(0, 0)
            attn_out(0, 0)
            pe.wait_ge(ys_ok, TPB - 1)
            for t in (TPB - 2, TPB - 1):
                last = T.transpose(bank(6)[:, (t - TPB + 2) * P:(t - TPB + 3) * P], s1[:, t * P:(t + 1) * P], ident[:, :])
            last.then_inc(r_ps, 1)

            def x1_transpose(b, c):
                i = 2 * b + c
                pe.wait_ge(x1_ok, i + 1)
                wait_free(pe, x1l_ok, i)
                for j in range(SUP):
                    last = T.transpose(bank(2)[:, j * P:(j + 1) * P], x1[:, c, j * P:(j + 1) * P], ident[:, :])
                last.then_inc(x1T_ps, 1)

            def hidden(b, c, f):
                i = 2 * b + c
                if f == 0:
                    pe.wait_ge(x1l_ok, i + 1)
                wait_free(pe, hl_ok, FB * i + f - 1)
                T.matmul(bank(3 + f % 2), qT[:, 0, f, :], x1h[:, c, :], start=True, stop=False)
                T.matmul(bank(3 + f % 2), qT[:, 0, f, :], x1l[:, c, :], start=False, stop=False)
                T.matmul(bank(3 + f % 2), b1s[:, f * P:(f + 1) * P], ones16[:, :], start=False, stop=True).then_inc(h_ps, 1)

            def feed_out(b, c, f):
                i = 2 * b + c
                if f == 0:
                    wait_free(pe, r2_ok, i)
                    T.matmul(bank(5), ones16[:, 0:P], b2s[:, :].unsqueeze(1).to_broadcast([P, SUP, D]), start=True, stop=False)
                pe.wait_ge(hl_ok, FB * i + f + 1)
                for j in range(SUP):
                    o = bank(5)[:, j * P:(j + 1) * P]
                    T.matmul(o, hh[:, c, f, j * P:(j + 1) * P], qT[:, 1, f, :], start=False, stop=False)
                    last = T.matmul(o, hl[:, c, f, j * P:(j + 1) * P], qT[:, 1, f, :], start=False,
                                    stop=f == FB - 1 and j == SUP - 1)
                if f == FB - 1:
                    last.then_inc(ff_ps, 1)

            def x2_products(b, c, after=None):
                i = 2 * b + c
                pe.wait_ge(x2_ok, i + 1)
                if after is not None:
                    pe.wait_ge(x2T_sb, after)
                for j in range(SUP):
                    T.matmul(bank(7)[:, 0:D], x2s[:, c, j * P:(j + 1) * P], x2s[:, c, j * P:(j + 1) * P],
                             start=c == 0 and j == 0, stop=c == 1 and j == SUP - 1)
                for j in range(SUP):
                    last = T.transpose(bank(6)[:, j * P:(j + 1) * P], x2s[:, c, j * P:(j + 1) * P], ident[:, :])
                last.then_inc(x2T_ps, 1)

            def body(b, c, prev=None, nxt=None, then=None, before=None):
                hidden(b, c, 0)
                hidden(b, c, 1)
                if before is not None:
                    x2_products(*before)
                hidden(b, c, 2)
                if nxt is not None:
                    x1_transpose(*nxt)
                if then is not None:
                    yr_transpose(*then)
                feed_out(b, c, 0)
                hidden(b, c, 3)
                if then is not None:
                    attn_out(*then)
                for f in range(1, FB):
                    feed_out(b, c, f)

            pe.wait_ge(r_sb, 1)
            pe.wait_ge(bias_ok, 1)
            pe.wait_ge(k_ones, 3)
            yr_transpose(0, 1)
            attn_out(0, 1)
            x1_transpose(0, 0)
            body(0, 0, nxt=(0, 1), then=(1, 0))
            body(0, 1, (0, 0), (1, 0), (1, 1))
            with pe.Fori(1, B - 1) as b:
                body(b, 0, (b - 1, 1), (b, 1), (b + 1, 0), (b - 1, 0))
                body(b, 1, (b, 0), (b + 1, 0), (b + 1, 1), (b - 1, 1))
            body(B - 1, 0, (B - 2, 1), (B - 1, 1), before=(B - 2, 0))
            body(B - 1, 1, (B - 1, 0), before=(B - 2, 1))
            x2_products(B - 1, 0)
            x2_products(B - 1, 1, NS - 1)

            pe.wait_ge(gram_sb, B)
            pe.wait_ge(ld_l1, 64)
            for b in range(B):
                last = T.matmul(bank(1)[:, b * D:(b + 1) * D], gram[:, b, :], wqk[:, :], start=True, stop=True)
            last.then_inc(m1_ps, 1)
            pe.wait_ge(m1_sb, 1)
            T.matmul(bank(2), wqk[:, :], gq[:, :], start=True, stop=True).then_inc(m2_ps, 1)
            pe.wait_ge(dq_ok, 1)
            T.matmul(bank(3)[:, 0:B * HD], block[:, :], dq[:, :, :].rearrange("p b d -> p (b d)"), start=True, stop=True).then_inc(m3_ps, 1)
            pe.wait_ge(ad_ok, 1)
            pe.wait_ge(wg_sb, 1)
            for b in range(B):
                last = T.matmul(bank(4 + b // 2)[:, b % 2 * ME:(b % 2 + 1) * ME], ad[:, b, :], wog[:, :], start=True, stop=True)
            last.then_inc(m4_ps, 1)
            pe.wait_ge(m4_sb, 1)
            for a in range(2):
                T.matmul(bank(1 + a)[:, 0:2 * ME], wvT[:, :], p1[:, a * 2 * ME:(a + 1) * 2 * ME], start=True, stop=False)
                for n in range(2):
                    last = T.matmul(bank(1 + a)[:, n * ME + D:(n + 1) * ME], ident[:, :], wgs[:, :], start=False, stop=n == 1)
            last.then_inc(m5_ps, 1)

            def attn2_out(b, c):
                i = 2 * b + c
                pe.wait_ge(staged[c], 16 * (b + 1))
                wait_free(pe, oh_ok, i - 1)
                for j in range(SUP):
                    last = T.matmul(bank(2 * c + j // 2)[:, j % 2 * ME:(j % 2 + 1) * ME], x2Ts[:, c, j * P:(j + 1) * P],
                                    mix[:, bass.ds(b * ME, ME)], start=True, stop=True)
                last.then_inc(o3_ps, 1)

            def places(b, c):
                i = 2 * b + c
                pe.wait_ge(oh_ok, i + 1)
                pe.wait_ge(carry_ok, i + 1)
                wait_free(pe, slf_ok, i - 1)
                flat = oh[:, c, :, :].rearrange("p t e -> p (t e)")
                T.matmul(bank(4 + c)[:, 0:SUP * E], upper16[:, :], flat, start=True, stop=False)
                for n in range(1, SUP):
                    T.matmul(bank(4 + c)[:, n * E:SUP * E], ones16[:, 0:P], flat[:, 0:(SUP - n) * E], start=False, stop=False)
                for add, stop in ((base16, False), (carry, True)):
                    last = T.matmul(bank(4 + c)[:, 0:SUP * E].rearrange("p (t e) -> p t e", t=SUP), ones16[:, 0:P],
                                    add[:, :].unsqueeze(1).to_broadcast([P, SUP, E]), start=False, stop=stop)
                last.then_inc(pos_ps, 1)

            def body(b, c, nxt):
                places(b, c)
                if nxt is not None:
                    attn2_out(*nxt)

            pe.wait_ge(mix_ok, 1)
            attn2_out(0, 0)
            attn2_out(0, 1)
            body(0, 0, (1, 0))
            body(0, 1, (1, 1))
            with pe.Fori(1, B - 1) as b:
                body(b, 0, (b + 1, 0))
                body(b, 1, (b + 1, 1))
            body(B - 1, 0, None)
            body(B - 1, 1, None)

            def expert_in(k, c):
                e = 2 * k + c
                pe.wait_ge(lds[c], 16 * (k + 1))
                wait_free(pe, xeT_sb, e)
                for j in range(CT):
                    last = T.transpose(pair(0)[:, j * P:(j + 1) * P], xs[:, c, j, 0:D], ident[:, :])
                last.then_inc(xeT_ps, 1)

            def expert_hidden(k, c, f):
                e = 2 * k + c
                if f == 0:
                    pe.wait_ge(xeT_sb, e + 1)
                    pe.wait_ge(ldw[c], 32 * (k + 1))
                wait_free(pe, eh_ok, FB * e + f - 1)
                for a in range(2):
                    last = T.matmul(PS[:, 2 + 2 * (f % 2) + a, 0:CAP // 2], w1s[:, c, f * P:(f + 1) * P],
                                    xeT[:, c, a * (CAP // 2):(a + 1) * (CAP // 2)], start=True, stop=True)
                last.then_inc(eh_ps, 1)

            def expert_out(k, c):
                e = 2 * k + c
                pe.wait_ge(eh_ok, FB * (e + 1))
                wait_free(pe, r4_ok, e)
                for j in range(CT):
                    o = pair(6)[:, j * D:(j + 1) * D]
                    T.matmul(o, ones16[:, 0:P], eb2s[:, bass.ds(e * D, D)], start=True, stop=False)
                    for f in range(FB):
                        last = T.matmul(o, eh[:, f, j * P:(j + 1) * P], w2s[:, c, f, :], start=False, stop=f == FB - 1)
                last.then_inc(ey_ps, 1)

            def expert(k, c, nxt):
                for f in range(FB):
                    expert_hidden(k, c, f)
                if nxt is not None:
                    expert_in(*nxt)
                expert_out(k, c)

            pe.wait_ge(slot_ok, NS)
            expert_in(0, 0)
            expert(0, 0, (0, 1))
            with pe.Fori(0, E // 2 - 1) as k:
                expert(k, 1, (k + 1, 0))
                expert(k + 1, 0, (k + 1, 1))
            expert(E // 2 - 1, 1, None)


_INS = ['L0_attn_x', 'L0_attn_W_in', 'L0_attn_conv_w', 'L0_attn_conv_b', 'L0_attn_A_param', 'L0_attn_dt_bias',
        'L0_attn_W_out', 'L0_ffn_W1', 'L0_ffn_b1', 'L0_ffn_W2', 'L0_ffn_b2', 'L1_attn_Wqk', 'L1_attn_Wv',
        'L1_attn_Wo', 'L1_attn_tau', 'L1_ffn_wg', 'L1_ffn_w1', 'L1_ffn_b1', 'L1_ffn_w2', 'L1_ffn_b2']


def kernel(**inputs):
    import numpy as np
    import concourse.bacc as bacc
    from concourse.bass_utils import run_bass_kernel_spmd

    nc = bacc.Bacc("TRN2", target_bir_lowering=False, num_devices=1)
    arrays, args = {}, []
    for name in _INS:
        a = np.ascontiguousarray(inputs[name])
        arrays[f"in_{name}"] = a
        args.append(nc.dram_tensor(f"in_{name}", a.shape, mybir.dt.from_np(a.dtype), kind="ExternalInput").ap())
    args.append(nc.dram_tensor("out", (B, S, D), F32, kind="ExternalOutput").ap())
    build_program(nc, *args)
    return run_bass_kernel_spmd(nc, [arrays], core_ids=[0]).results[0]["out"]
```

```python
from contextlib import ExitStack

import concourse.bass as bass
from concourse import mybir

F32 = mybir.dt.float32
F16 = mybir.dt.float16
I32 = mybir.dt.int32
U32 = mybir.dt.uint32
ACT = mybir.ActivationFunctionType
ALU = mybir.AluOpType
AX = mybir.AxisListType.X

P = 128
B, S, D = 4, 1024, 128
H, HD = 16, 8
TAPS = 4
F = 512
FB = F // P
E = 8
TOK = B * S
CAP = int(1.25 * TOK / E)
CT = CAP // P
NT = TOK // P
TPB = S // P
SUP = 4
NS = NT // SUP
ME = D + E
ROW = D + 2
EPS = 1e-5
DROP = 8192.0


def build_program(nc, x, W_in, conv_w, conv_b, A_param, dt_bias, W_out, W1, b1, W2, b2,
                  Wqk, Wv, Wo, tau, wg, w1, eb1, w2, eb2, out):
    ctx = ExitStack()
    with ctx:
        def sb(name, shape, dt=F32):
            return ctx.enter_context(nc.sbuf_tensor(name, shape, dt))

        def sem(name):
            return ctx.enter_context(nc.semaphore(name))

        def wait_free(eng, semaphore, count):
            if not isinstance(count, int) or count > 0:
                eng.wait_ge(semaphore, count)

        def tiles_done(c, j):
            return E - 2 + CT * c + j + 1

        PS = ctx.enter_context(nc.psum_tensor("PS", [P, 8, 512], F32))

        def bank(n):
            return PS[:, n, :]

        def part(tensor, first, *dims):
            size, names = 1, "abcd"[:len(dims)]
            for d in dims:
                size *= d
            flat = tensor[:, first:first + size]
            if len(dims) == 1:
                return flat
            return flat.rearrange(f"p ({' '.join(names)}) -> p {' '.join(names)}", **dict(zip(names, dims)))

        def pair(n):
            return PS[:, n:n + 2, :].rearrange("p a f -> p (a f)")

        slots = nc.dram_tensor("slots", (E * CAP, ROW), F32, kind="Internal").ap()

        ones = sb("ones", [P, P])
        ident = sb("ident", [P, P])
        upper = sb("upper", [P, P])
        block = sb("block", [P, P])
        ones16 = sb("ones16", [P, 512], F16)
        ident16 = sb("ident16", [P, P], F16)
        upper16 = sb("upper16", [P, P], F16)
        diag8 = sb("diag8", [P, HD])
        selA = sb("selA", [H, B, 2, H])
        selB = sb("selB", [H, B, 2, H])
        tokid = sb("tokid", [P, NT], I32)
        rev8 = sb("rev8", [P, E])
        base8 = sb("base8", [P, E])
        lim8 = sb("lim8", [P, E])
        base16 = sb("base16", [P, E], F16)
        epsT = sb("epsT", [P, SUP])
        mhalf = sb("mhalf", [P, SUP])
        empty = sb("empty", [P, ROW])

        xt = sb("xt", [P, NT, D])
        win = sb("win", [P, 3, D])
        windt = sb("windt", [H, D])
        convw = sb("convw", [P, 3, TAPS])
        convb = sb("convb", [P, 3])
        ab = sb("ab", [H, 2])
        wout = sb("wout", [P, D])
        wn = sb("wn", [P, 2, F])
        w1n = part(wn[:, 0, :], 0, FB, D)
        w2n = wn[:, 1, :]
        wqk = sb("wqk", [P, D])
        wv = sb("wv", [P, D])
        wog = sb("wog", [P, ME])
        wo = wog[:, 0:D]
        tauc = sb("tauc", [P, 1])
        wgs = sb("wgs", [P, E])
        eb1n = sb("eb1n", [E * FB, P])
        b1r = sb("b1r", [1, F])
        b2r = sb("b2r", [1, D])
        eb2r = sb("eb2r", [1, E * D])

        winT = sb("winT", [P, 3 * D])
        wdtT = sb("wdtT", [P, 2 * H])
        acol = sb("acol", [P, 2])
        nega = sb("nega", [P, 1])
        woutT = sb("woutT", [P, D])
        wvT = sb("wvT", [P, D])
        woT = sb("woT", [P, D])
        wgsum = sb("wgsum", [P, E])
        eb1T = sb("eb1T", [P, E * FB])
        wabs = sb("wabs", [P, 2])
        cut = sb("cut", [P, 2])
        ncut = sb("ncut", [P, 2])
        q16 = sb("q16", [P, 2, F], F16)
        qT = sb("qT", [P, 2, FB, P], F16)
        b1s = sb("b1s", [P, F], F16)
        b2s = sb("b2s", [P, D], F16)
        eb2s = sb("eb2s", [P, E * D], F16)
        tau32 = sb("tau32", [P, 1])

        def last_out(c, j):
            return pair(6)[:, j * D:(j + 1) * D] if c == 0 else bank((0, 1, 6, 7, 2)[j])[:, 0:D]

        xT = sb("xT", [P, TOK])
        first = sb("first", [P, 3 * (TAPS - 1 + S) + 3 * S])
        craw = part(first, 0, 3, TAPS - 1 + S)
        conv = part(first, 3 * (TAPS - 1 + S), 3, S)
        work = sb("work", [P, 5, S])
        s1, s2, s3, s4, s5 = (work[:, n, :] for n in range(5))
        qpos = part(s5, 0, F)
        qneg = part(s5, F, F)
        cum = sb("cum", [P, S])
        onesS = sb("onesS", [P, S])
        expn = sb("expn", [P, S])
        rT = sb("rT", [P, TPB, P])
        eT = sb("eT", [P, TPB, 2 * H])
        bcx = sb("bcx", [P, 3, 3 * D])
        xp = sb("xp", [P, 2, D])
        zz = sb("zz", [P, 2, 1024])
        cz = sb("cz", [P, 2, 1024])
        taps = [zz[:, 0, :], zz[:, 1, :], cz[:, 0, :]]
        yi = sb("yi", [P, 2, D])
        ys = sb("ys", [P, 4, D])
        st = sb("st", [P, 2, D])
        y0 = sb("y0", [P, TPB, D])

        ld_x = [sem(f"ld_x{b}") for b in range(B)]
        ld_win = sem("ld_win")
        ld_small = sem("ld_small")
        ld_w = sem("ld_w")
        ld_l1 = sem("ld_l1")
        ld_bias = sem("ld_bias")
        k_ones = sem("k_ones")
        k_pool = sem("k_pool")
        k_sel = sem("k_sel")
        k_const = sem("k_const")
        k_empty = sem("k_empty")
        slots_init = sem("slots_init")
        slf_ok = sem("slf_ok")
        slp_ok = sem("slp_ok")
        win_ps = sem("win_ps")
        win_sb = sem("win_sb")
        acol_ps = sem("acol_ps")
        nega_ok = sem("nega_ok")
        pad_ok = sem("pad_ok")
        xT_ps = sem("xT_ps")
        xT_sb = [sem("xT_sb0"), sem("xT_sb1")]
        proj_ps = sem("proj_ps")
        proj_sb = sem("proj_sb")
        dt_ps = sem("dt_ps")
        dt_abs = sem("dt_abs")
        dt_ln = sem("dt_ln")
        dve1 = sem("dve1")
        act1 = sem("act1")
        dt_pos = sem("dt_pos")
        cum_ok = sem("cum_ok")
        exp_ok = sem("exp_ok")
        cs_ok = sem("cs_ok")
        lncs_ok = sem("lncs_ok")
        lr_ok = sem("lr_ok")
        r_ok = sem("r_ok")
        e_ps = sem("e_ps")
        e_sb = sem("e_sb")
        r_ps = sem("r_ps")
        r_sb = sem("r_sb")
        tap_ok = sem("tap_ok")
        tap_sum = sem("tap_sum")
        conv_ok = sem("conv_ok")
        wabs_ok = sem("wabs_ok")
        wsum_ps = sem("wsum_ps")
        q_ok = sem("q_ok")
        cut_ok = sem("cut_ok")
        cmp_ok = sem("cmp_ok")
        q_ps = sem("q_ps")
        q_sb = sem("q_sb")
        wT_ps = sem("wT_ps")
        wT_sb = sem("wT_sb")
        wg_ps = sem("wg_ps")
        wg_sb = sem("wg_sb")
        bias_ok = sem("bias_ok")
        tr_ps = sem("tr_ps")
        tr_sb = sem("tr_sb")
        xp_ok = sem("xp_ok")
        z_ok = sem("z_ok")
        cum_ps = sem("cum_ps")
        cz_ok = sem("cz_ok")
        off_ps = sem("off_ps")
        st_ps = sem("st_ps")
        st_ok = sem("st_ok")
        yi_ok = sem("yi_ok")
        ys_ok = sem("ys_ok")
        y0_ok = sem("y0_ok")

        yr = sb("yr", [P, 2, SUP, D])
        yrT = sb("yrT", [P, 512])
        r1 = sb("r1", [P, 512])
        st1 = sb("st1", [P, SUP, 6])
        mv1 = sb("mv1", [P, SUP, 2])
        neg1 = sb("neg1", [P, SUP])
        ve1 = sb("ve1", [P, SUP])
        neg1_ok = sem("neg1_ok")
        rs1 = sb("rs1", [P, SUP])
        nm1 = sb("nm1", [P, SUP])
        x1 = sb("x1", [P, 2, 512])
        x1h = sb("x1h", [P, 2, 512], F16)
        x1l = sb("x1l", [P, 2, 512], F16)
        hh = sb("hh", [P, 2, FB, 512], F16)
        hl = sb("hl", [P, 2, FB, 512], F16)
        r2 = sb("r2", [P, 512])
        st2 = sb("st2", [P, SUP, 6])
        mv2 = sb("mv2", [P, SUP, 2])
        neg2 = sb("neg2", [P, SUP])
        ve2 = sb("ve2", [P, SUP])
        neg2_ok = sem("neg2_ok")
        rs2 = sb("rs2", [P, SUP])
        nm2 = sb("nm2", [P, SUP])
        x2s = sb("x2s", [P, 2, 512])
        x2k = xt[:, :, :].rearrange("p t d -> p (t d)")
        x2T = xT
        gram = sb("gram", [P, B, D])
        yr_ok = sem("yr_ok")
        yrT_ps = sem("yrT_ps")
        yrT_sb = sem("yrT_sb")
        ao_ps = sem("ao_ps")
        r1_ok = sem("r1_ok")
        st1_ok = sem("st1_ok")
        mv1_ok = sem("mv1_ok")
        ln1_step = sem("ln1_step")
        x1_ok = sem("x1_ok")
        x1T_ps = sem("x1T_ps")
        x1h_ok = sem("x1h_ok")
        x1l_ok = sem("x1l_ok")
        h_ps = sem("h_ps")
        hh_ok = sem("hh_ok")
        hl_ok = sem("hl_ok")
        ff_ps = sem("ff_ps")
        r2_ok = sem("r2_ok")
        st2_ok = sem("st2_ok")
        mv2_ok = sem("mv2_ok")
        ln2_step = sem("ln2_step")
        x2_ok = sem("x2_ok")
        x2_kept = [sem("x2_kept0"), sem("x2_kept1")]
        x2T_ps = sem("x2T_ps")
        x2T_sb = sem("x2T_sb")
        gram_sb = sem("gram_sb")

        gq = part(expn, 0, 512)
        dm = sb("dm", [P, B, D])
        dc = sb("dc", [P, B, HD])
        dq = sb("dq", [P, B, HD])
        qc = sb("qc", [P, B])
        lg = sb("lg", [P, B, HD])
        mx = sb("mx", [P, B])
        ea = sb("ea", [P, B, HD])
        ad = sb("ad", [P, B, D])
        p1 = sb("p1", [P, B * ME])
        mix = sb("mix", [P, B * ME])
        m1_ps = sem("m1_ps")
        m1_sb = sem("m1_sb")
        m2_ps = sem("m2_ps")
        mixs = sem("mixs")
        dq_ok = sem("dq_ok")
        m3_ps = sem("m3_ps")
        lg_ok = sem("lg_ok")
        ea_ok = sem("ea_ok")
        ad_ok = sem("ad_ok")
        m4_ps = sem("m4_ps")
        m4_sb = sem("m4_sb")
        m5_ps = sem("m5_ps")
        mix_ok = sem("mix_ok")

        x2Ts = part(onesS, 0, 2, 512)
        r3 = part(y0[:, :, :].rearrange("p t d -> p (t d)"), 0, 2, 512)
        st3 = sb("st3", [P, SUP, 6])
        mv3 = sb("mv3", [P, SUP, 2])
        rs3 = sb("rs3", [P, SUP])
        nm3 = sb("nm3", [P, SUP])
        lv3 = sb("lv3", [P, SUP])
        sq3 = sb("sq3", [P, SUP])
        lq3 = sb("lq3", [P, SUP])
        s43 = sb("s43", [P, 2, SUP])
        onep = sb("onep", [P, 1])
        work1 = work[:, :, :].rearrange("p a f -> p (a f)")
        rows = part(work1, 0, NS * SUP, ROW)
        x4 = part(cz[:, 0, :], 0, 2, 512)
        gmax = sb("gmax", [P, SUP])
        l1 = sb("l1", [P, SUP, E])
        l2 = sb("l2", [P, SUP, E])
        gl = sb("gl", [P, SUP, E])
        ge = sb("ge", [P, SUP, E])
        gs = sb("gs", [P, SUP])
        eqv = sb("eqv", [P, SUP, E])
        vmax = sb("vmax", [P, SUP])
        oh = sb("oh", [P, 2, SUP, E], F16)
        ohs = sb("ohs", [P, E])
        carry = sb("carry", [P, E], F16)
        sl1 = sb("sl1", [P, SUP, E])
        sl2 = sb("sl2", [P, SUP, E])
        slf = sb("slf", [P, SUP])
        slp = sb("slp", [P, SUP])
        slot = sb("slot", [P, 2, SUP], U32)
        staged = [sem("staged0"), sem("staged1")]
        o3_ps = sem("o3_ps")
        r3_ok = sem("r3_ok")
        st3_ok = sem("st3_ok")
        mv3_ok = sem("mv3_ok")
        lv3_ok = sem("lv3_ok")
        rs3_ok = sem("rs3_ok")
        nm3_ok = sem("nm3_ok")
        x3_ok = sem("x3_ok")
        gate_step = sem("gate_step")
        route_step = sem("route_step")
        gl_ok = sem("gl_ok")
        ge_ok = sem("ge_ok")
        oh_ok = sem("oh_ok")
        pos_ps = sem("pos_ps")
        slot_ok = sem("slot_ok")
        s4_step = sem("s4_step")
        x4_ok = sem("x4_ok")
        stored = [sem("stored0"), sem("stored1")]
        scat = [sem("scat0"), sem("scat1")]
        carry_ok = sem("carry_ok")

        xs = part(first, 0, 2, CT, ROW)
        xr = part(first, 2 * CT * ROW, 2, CT, ROW)
        w1s = part(cum, 0, 2, F)
        w2s = part(wn[:, :, :].rearrange("p a f -> p (a f)"), 0, 2, FB, D)
        xeT = part(xT, 0, 2, CAP)
        eh = part(work1, 0, FB, CAP)
        xr_ok = sem("xr_ok")
        r4 = part(work1, FB * CAP, CT, D)
        st4 = sb("st4", [P, CT, 6])
        mv4 = sb("mv4", [P, CT, 2])
        neg4 = sb("neg4", [P, CT])
        lv4 = sb("lv4", [P, CT])
        rs4 = sb("rs4", [P, CT])
        nm4 = sb("nm4", [P, CT])
        y4 = part(work1, (FB + 1) * CAP, 2, CT, D)
        ldw = [sem("ldw0"), sem("ldw1")]
        lds = [sem("lds0"), sem("lds1")]
        xeT_ps = sem("xeT_ps")
        xeT_sb = sem("xeT_sb")
        eh_ps = sem("eh_ps")
        eh_ok = sem("eh_ok")
        ey_ps = sem("ey_ps")
        r4_ok = sem("r4_ok")
        st4_ok = sem("st4_ok")
        mv4_ok = sem("mv4_ok")
        rs4_ok = sem("rs4_ok")
        neg4_ok = sem("neg4_ok")
        lv4_ok = sem("lv4_ok")
        ln4_step = sem("ln4_step")
        y4_ok = sem("y4_ok")
        put = [sem("put0"), sem("put1")]

        block_ = ctx.enter_context(nc.Block())

        @block_.sync
        def _(sp):
            sp.dma_start(win[:, :, :], W_in[0:3 * D, :].rearrange("(g p) d -> p g d", p=P)).then_inc(ld_win, 16)
            sp.dma_start(windt[:, :], W_in[3 * D:3 * D + H, :]).then_inc(ld_win, 16)
            for b in range(B):
                sp.dma_start(xt[:, b * TPB:(b + 1) * TPB, :],
                             x[b].rearrange("(t p) d -> p t d", p=P)).then_inc(ld_x[b], 16)
            sp.dma_start(w1n[:, :, :], W1.rearrange("(k p) d -> p k d", p=P)).then_inc(ld_w, 16)
            sp.dma_start(w2n[:, :], W2).then_inc(ld_w, 16)
            sp.dma_start(wout[:, :], W_out).then_inc(ld_w, 16)
            sp.dma_start(wv[:, :], Wv).then_inc(ld_w, 16)
            sp.dma_start(eb1n[:, :], eb1.rearrange("e (k p) -> (e k) p", p=P)).then_inc(ld_w, 16)
            sp.dma_start(b1r[:, :], b1.rearrange("(o f) -> o f", o=1)).then_inc(ld_bias, 16)
            sp.dma_start(b2r[:, :], b2.rearrange("(o f) -> o f", o=1)).then_inc(ld_bias, 16)
            sp.dma_start(eb2r[:, :], eb2.rearrange("(o e) d -> o (e d)", o=1)).then_inc(ld_bias, 16)
            sp.dma_start(wqk[:, :], Wqk).then_inc(ld_l1, 16)
            sp.dma_start(wo, Wo).then_inc(ld_l1, 16)
            sp.dma_start(tauc[:, :], tau.rearrange("h a b -> h (a b)").unsqueeze(1).to_broadcast([H, HD, 1])).then_inc(ld_l1, 16)
            sp.dma_start(wgs[:, :], wg).then_inc(ld_l1, 16)
            sp.wait_ge(k_empty, 2)
            sp.dma_start(slots.rearrange("(p t) r -> p t r", p=P),
                         empty[:, :].unsqueeze(1).to_broadcast([P, E * CT, ROW])).then_inc(slots_init, 16)

            def keep_x2(b, c):
                sp.wait_ge(x2_ok, 2 * b + c + 1)
                sp.dma_start(x2k[:, bass.ds(b * 1024 + c * 512, 512)], x2s[:, c, :]).then_inc(x2_kept[c], 16)

            with sp.Fori(0, B - 1) as b:
                keep_x2(b, 0)
                keep_x2(b, 1)

            def load_weights(k, c):
                sp.dma_start(w1s[:, c, :], w1[bass.ds(2 * k + c, 1)].rearrange("e d f -> d (e f)")).then_inc(ldw[c], 16)
                sp.dma_start(w2s[:, c, :, :], w2[bass.ds(2 * k + c, 1)].rearrange("e (k p) d -> p (e k) d", p=P)).then_inc(ldw[c], 16)

            def stage_x2T(b, c):
                sp.dma_start(x2Ts[:, c, :], x2T[:, bass.ds(b * 1024 + c * 512, 512)]).then_inc(staged[c], 16)

            def store_x4(b, c):
                sp.wait_ge(x4_ok, 2 * b + c + 1)
                sp.dma_start(out[bass.ds(b, 1), c * 512:(c + 1) * 512, :].rearrange("b (t p) d -> p (b t) d", p=P),
                             x4[:, c, :].rearrange("p (t d) -> p t d", t=SUP)).then_inc(stored[c], 16)

            load_weights(0, 0)
            load_weights(0, 1)
            stage_x2T(0, 0)
            stage_x2T(0, 1)
            keep_x2(B - 1, 0)
            keep_x2(B - 1, 1)
            sp.wait_ge(x2T_sb, NS)
            for c in range(2):
                sp.wait_ge(o3_ps, c + 1)
                stage_x2T(1, c)
            with sp.Fori(1, B - 1) as b:
                sp.wait_ge(o3_ps, 2 * b + 1)
                stage_x2T(b + 1, 0)
                store_x4(b - 1, 0)
                sp.wait_ge(o3_ps, 2 * b + 2)
                stage_x2T(b + 1, 1)
                store_x4(b - 1, 1)
            store_x4(B - 2, 0)
            store_x4(B - 2, 1)
            store_x4(B - 1, 0)
            store_x4(B - 1, 1)

            def load_slots(k, c):
                sp.dma_start(xs[:, c, :, :],
                             slots[bass.ds((2 * k + c) * CAP, CAP), :].rearrange("(t p) r -> p t r", p=P)).then_inc(lds[c], 16)

            for c in range(2):
                sp.wait_ge(scat[c], 16 * SUP * B)
            load_slots(0, 0)
            load_slots(0, 1)
            with sp.Fori(0, E // 2 - 1) as k:
                for c in range(2):
                    sp.wait_ge(xeT_ps, 2 * k + c + 1)
                    sp.wait_ge(xr_ok, 2 * k + c + 1)
                    load_slots(k + 1, c)
                for c in range(2):
                    sp.wait_ge(ey_ps, 2 * k + c + 1)
                    load_weights(k + 1, c)
            for c in range(2):
                sp.wait_ge(put[c], 16 * CT * (E // 2))
                sp.wait_ge(stored[c], 16 * B)

        @block_.gpsimd
        def _(pool):
            pool.memset(ones[:, :], 1.0).then_inc(k_ones, 1)
            pool.wait_ge(k_ones, 1)
            pool.affine_select(out=ident[:, :], in_=ones[:, :], compare_op=ALU.is_equal, fill=0.0, base=0,
                               pattern=[[-1, P]], channel_multiplier=1).then_inc(k_pool, 1)
            pool.affine_select(out=upper[:, :], in_=ones[:, :], compare_op=ALU.is_ge, fill=0.0, base=0,
                               pattern=[[1, P]], channel_multiplier=-1).then_inc(k_pool, 1)
            pool.affine_select(out=block[:, :], in_=ones[:, :], compare_op=ALU.is_ge, fill=0.0, base=0,
                               pattern=[[-HD, H], [0, HD]], channel_multiplier=1).then_inc(k_pool, 1)
            pool.wait_ge(k_pool, 3)
            pool.affine_select(out=block[:, :], in_=block[:, :], compare_op=ALU.is_ge, fill=0.0, base=HD - 1,
                               pattern=[[HD, H], [0, HD]], channel_multiplier=-1).then_inc(k_pool, 1)
            pool.iota(tokid[:, :], pattern=[[P, NT]], base=0, channel_multiplier=1).then_inc(k_pool, 1)
            pool.iota(rev8[:, :], pattern=[[-1, E]], base=E, channel_multiplier=0,
                      allow_small_or_imprecise_dtypes=True).then_inc(k_pool, 1)
            pool.iota(base8[:, :], pattern=[[CAP, E]], base=0, channel_multiplier=0,
                      allow_small_or_imprecise_dtypes=True).then_inc(k_pool, 1)
            pool.memset(ones16[:, :], 1.0).then_inc(k_ones, 1)
            pool.memset(onesS[:, :], 1.0).then_inc(k_ones, 1)
            pool.wait_ge(ld_w, 80)
            pool.wait_ge(cut_ok, 2)
            for n, src in enumerate((w1n[:, :, :].rearrange("p k d -> p (k d)"), w2n[:, :])):
                pool.tensor_scalar(qneg[:, :], src, ncut[:, n:n + 1], None, ALU.is_lt).then_inc(cmp_ok, 1)
                pool.tensor_scalar(qpos[:, :], src, cut[:, n:n + 1], None, ALU.is_gt).then_inc(cmp_ok, 1)
                pool.wait_ge(cmp_ok, 2 * n + 2)
                pool.tensor_tensor(q16[:, n, :], qpos[:, :], qneg[:, :], ALU.subtract).then_inc(q_ok, 1)
                pool.wait_ge(q_ok, n + 1)
            pool.wait_ge(tap_ok, 1)
            pool.tensor_tensor(conv[:, 2, :], conv[:, 2, :], taps[0], ALU.add).then_inc(tap_sum, 1)

            def scale_out(t):
                if t == 0:
                    pool.wait_ge(yi_ok, 1)
                else:
                    pool.wait_ge(ys_ok, t)
                pool.tensor_tensor(y0[:, t, :].rearrange("p (h d) -> p h d", h=H),
                                   ys[:, t % 4, :].rearrange("p (h d) -> p h d", h=H),
                                   eT[:, t, H:2 * H].unsqueeze(2).to_broadcast([P, H, HD]), ALU.mult).then_inc(y0_ok, 1)

            def norm_out(b, c):
                if isinstance(b, int) and b == 0:
                    pool.wait_ge(y0_ok, SUP * (c + 1))
                    if c == 0:
                        pool.wait_ge(tr_sb, TPB - 2)
                    else:
                        pool.wait_ge(r_sb, 1)
                wait_free(pool, yrT_ps, 2 * b + c - 1)
                pool.tensor_tensor(yr[:, c, :, :].rearrange("p t (h d) -> p t h d", h=H),
                                   y0[:, SUP * c:SUP * (c + 1), :].rearrange("p t (h d) -> p t h d", h=H),
                                   rT[:, SUP * c:SUP * (c + 1), bass.ds(b * 2 * H, H)].unsqueeze(3).to_broadcast([P, SUP, H, HD]),
                                   ALU.mult).then_inc(yr_ok, 1)

            for t in range(TPB):
                c = t % 2
                pool.wait_ge(tr_sb, t + 1)
                if t == 0:
                    pool.wait_ge(e_sb, 1)
                wait_free(pool, st_ps, t - 1)
                pool.tensor_tensor(xp[:, c, :].rearrange("p (h d) -> p h d", h=H),
                                   bcx[:, t % 3, 2 * D:].rearrange("p (h d) -> p h d", h=H),
                                   eT[:, t, 0:H].unsqueeze(2).to_broadcast([P, H, HD]), ALU.mult).then_inc(xp_ok, 1)
                pool.wait_ge(xp_ok, t + 1)
                wait_free(pool, cum_ps, t - 1)
                pool.tensor_tensor(zz[:, c, :].rearrange("p (h d n) -> p h d n", h=H, d=HD),
                                   bcx[:, t % 3, D:2 * D].rearrange("p (h n) -> p h n", h=H).unsqueeze(2).to_broadcast([P, H, HD, HD]),
                                   xp[:, c, :].rearrange("p (h d) -> p h d", h=H).unsqueeze(3).to_broadcast([P, H, HD, HD]),
                                   ALU.mult).then_inc(z_ok, 1)

                if t > 1:
                    scale_out(t - 2)
            norm_out(0, 0)
            scale_out(TPB - 2)
            scale_out(TPB - 1)

            def rstd(i, mv, neg, neg_ok, ve, ln_step, rs, nm, free):
                pool.wait_ge(neg_ok, i + 1)
                wait_free(pool, free, i)
                pool.tensor_tensor(ve[:, :], mv[:, :, 1], epsT[:, :], ALU.add).then_inc(ln_step, 1)
                pool.wait_ge(ln_step, 3 * i + 1)
                pool.tensor_tensor(rs[:, :], ve[:, :], mhalf[:, :], ALU.pow).then_inc(ln_step, 1)
                pool.wait_ge(ln_step, 3 * i + 2)
                pool.tensor_tensor(nm[:, :], neg[:, :], rs[:, :], ALU.mult).then_inc(ln_step, 1)

            def rstd1(b, c):
                rstd(2 * b + c, mv1, neg1, neg1_ok, ve1, ln1_step, rs1, nm1, x1_ok)

            def rstd2(b, c):
                rstd(2 * b + c, mv2, neg2, neg2_ok, ve2, ln2_step, rs2, nm2, x2_ok)

            def body(prev=None, then=None):
                if then is not None:
                    norm_out(*then)
                if prev is not None:
                    rstd2(*prev)
                if then is not None:
                    rstd1(*then)

            norm_out(0, 1)
            rstd1(0, 0)
            rstd1(0, 1)
            body(then=(1, 0))
            body((0, 0), (1, 1))
            with pool.Fori(1, B - 1) as b:
                body((b - 1, 1), (b + 1, 0))
                body((b, 0), (b + 1, 1))
            body(prev=(B - 2, 1))
            body(prev=(B - 1, 0))
            rstd2(B - 1, 1)

            def scatter(b, c):
                i = 2 * b + c
                wait_free(pool, scat[c], 16 * SUP * b)
                pool.wait_ge(slf_ok, i + 1)
                pool.tensor_tensor(slp[:, :], slf[:, :], ones[:, 0:SUP], ALU.subtract).then_inc(slp_ok, 1)
                pool.wait_ge(k_ones, 3)
                pool.wait_ge(slp_ok, i + 1)
                pool.tensor_copy(slot[:, c, :], slp[:, :]).then_inc(slot_ok, 1)
                pool.wait_ge(slots_init, 16)
                pool.wait_ge(slot_ok, i + 1)
                pool.wait_ge(x3_ok, i + 1)
                for j in range(SUP):
                    pool.indirect_dma_start(out=slots, out_offset=bass.IndirectOffsetOnAxis(ap=slot[:, c, j:j + 1], axis=0),
                                            in_=rows[:, SUP * i + j, :], in_offset=None,
                                            bounds_check=E * CAP - 1, oob_is_err=False).then_inc(scat[c], 16)

            for b in range(B):
                scatter(b, 0)
                scatter(b, 1)

            def scaled_mean(k, c):
                e = 2 * k + c
                pool.wait_ge(neg4_ok, e + 1)
                pool.wait_ge(rs4_ok, e + 1)
                pool.tensor_tensor(nm4[:, :], neg4[:, :], rs4[:, :], ALU.mult).then_inc(ln4_step, 1)

            def put_rows(k, c, each=False):
                for n in range(2):
                    pool.wait_ge(stored[n], 16 * B)
                if not each:
                    pool.wait_ge(y4_ok, 2 * k + c + 1)
                for j in range(CT):
                    if each:
                        pool.wait_ge(y4_ok, tiles_done(c, j))
                    pool.indirect_dma_start(out=out.rearrange("b s d -> (b s) d"),
                                            out_offset=bass.IndirectOffsetOnAxis(ap=xr[:, c, j, D + 1:D + 2].bitcast(U32), axis=0),
                                            in_=y4[:, c, j, :], in_offset=None,
                                            bounds_check=TOK - 1, oob_is_err=False).then_inc(put[c], 16)

            with pool.Fori(0, E // 2 - 1) as k:
                scaled_mean(k, 0)
                put_rows(k, 0)
                scaled_mean(k, 1)
                put_rows(k, 1)
            put_rows(E // 2 - 1, 0, each=True)
            put_rows(E // 2 - 1, 1, each=True)

        @block_.scalar
        def _(act):
            act.dma_start(convw[:, :, :], conv_w.rearrange("(g p) k -> p g k", p=P)).then_inc(ld_small, 16)
            act.dma_start(convb[:, :], conv_b.rearrange("(g p) -> p g", p=P), allow_slow_non_contiguous=True).then_inc(ld_small, 16)
            act.dma_start(ab[:, 0:1], A_param.rearrange("(h o) -> h o", o=1)).then_inc(ld_small, 16)
            act.dma_start(ab[:, 1:2], dt_bias.rearrange("(h o) -> h o", o=1)).then_inc(ld_small, 16)
            nc.scalar.preload_act_table_set("natural_log_exp_and_others")
            act.wait_ge(win_ps, 1)
            nc.scalar.copy(winT[:, :], bank(0)[:, 0:3 * D]).then_inc(win_sb, 1)
            nc.scalar.copy(wdtT[:, :].rearrange("p (a h) -> p a h", a=2),
                           bank(0)[:, 3 * D:3 * D + H].unsqueeze(1).to_broadcast([P, 2, H])).then_inc(win_sb, 1)
            def x_out(n):
                act.wait_ge(xT_ps, n + 1)
                nc.scalar.copy(xT[:, n * 512:(n + 1) * 512], bank(1)).then_inc(xT_sb[0], 1)

            x_out(0)
            act.wait_ge(acol_ps, 1)
            nc.scalar.copy(acol[:, :], bank(0)[:, 400:402]).then_inc(win_sb, 1)
            for n in range(6):
                act.wait_ge(proj_ps, n + 1)
                if n == 0:
                    act.wait_ge(ld_small, 64)
                if n == 3:
                    act.wait_ge(wsum_ps, 1)
                    for half, sign in ((cut, 0.5), (ncut, -0.5)):
                        nc.scalar.activation(half[:, :], bank(0)[:, 0:2], ACT.Copy,
                                             scale=sign / (F * D), bias=sign * EPS).then_inc(cut_ok, 1)
                nc.scalar.activation(conv[:, n // 2, 512 * (n % 2):512 * (n % 2) + 512], bank(3 + n % 3), ACT.Identity,
                                     scale=convw[:, n // 2, TAPS - 1:TAPS], bias=convb[:, n // 2:n // 2 + 1])
                nc.scalar.copy(craw[:, n // 2, TAPS - 1 + 512 * (n % 2):TAPS - 1 + 512 * (n % 2) + 512],
                               bank(3 + n % 3)).then_inc(proj_sb, 1)
                if n % 2 == 0:
                    x_out(2 + n)
            act.wait_ge(dt_ps, NS)
            act.wait_ge(win_sb, 3)
            nc.scalar.activation(s1[:, :], pair(6), ACT.Abs, bias=acol[:, 1:2]).then_inc(dt_abs, 1)
            act.wait_ge(dt_abs, 1)
            nc.scalar.activation(s2[:, :], s1[:, :], ACT.Exp, scale=-1.0).then_inc(act1, 1)
            act.wait_ge(act1, 1)
            nc.scalar.activation(s3[:, :], s2[:, :], ACT.Ln, bias=1.0).then_inc(dt_ln, 1)
            for k, tap in enumerate(taps):
                nc.scalar.activation(tap, craw[:, 2, k:k + S], ACT.Copy, scale=convw[:, 2, k:k + 1]).then_inc(tap_ok, 1)
            act.wait_ge(cum_ok, 1)
            act.wait_ge(nega_ok, 1)
            nc.scalar.activation(expn[:, :], cum[:, :], ACT.Exp, scale=nega[:, 0:1]).then_inc(exp_ok, 1)
            act.wait_ge(e_ps, 1)
            nc.scalar.copy(eT[:, :, :], bank(3)[:, 0:TPB * 2 * H].rearrange("p (t k) -> p t k", t=TPB)).then_inc(e_sb, 1)

            act.wait_ge(wT_ps, 1)
            nc.scalar.copy(woutT[:, :], bank(5)[:, 0:D]).then_inc(wT_sb, 1)
            nc.scalar.copy(wvT[:, :], bank(5)[:, D:2 * D]).then_inc(wT_sb, 1)
            nc.scalar.copy(eb1T[:, :], bank(5)[:, 2 * D:2 * D + E * FB]).then_inc(wT_sb, 1)
            nc.scalar.copy(woT[:, :], bank(5)[:, 3 * D:4 * D]).then_inc(wT_sb, 1)
            def chunk_out(t):
                act.wait_ge(tr_ps, t + 1)
                wait_free(act, st_ps, t - 2)
                wait_free(act, z_ok, t - 2)
                wait_free(act, cz_ok, t - 2)
                last = nc.scalar.copy(bcx[:, t % 3, :], bank(t % 2)[:, 0:3 * D])
                if t >= 2:
                    last = nc.scalar.copy(rT[:, t - 2, :], bank(t % 2)[:, 3 * D:4 * D])
                last.then_inc(tr_sb, 1)

            chunk_out(0)
            act.wait_ge(cs_ok, 1)
            nc.scalar.activation(s4[:, :], s5[:, :], ACT.Ln).then_inc(lncs_ok, 1)
            chunk_out(1)
            act.wait_ge(q_ps, 1)
            nc.scalar.copy(qT[:, :, :, :].rearrange("p a k f -> p (a k f)"), bank(4).bitcast(F16)).then_inc(q_sb, 1)
            act.wait_ge(wg_ps, 1)
            nc.scalar.copy(wog[:, D:ME], bank(5)[:, 0:E])
            nc.scalar.copy(wgsum[:, :], bank(5)[:, E:2 * E]).then_inc(wg_sb, 1)
            act.wait_ge(lr_ok, 1)
            nc.scalar.activation(s1[:, :], s2[:, :], ACT.Exp).then_inc(r_ok, 1)
            for t in range(2, TPB):
                chunk_out(t)
            def yrT_out(b, c):
                i = 2 * b + c
                act.wait_ge(yrT_ps, i + 1)
                wait_free(act, ao_ps, i)
                nc.scalar.copy(yrT[:, :], bank(0)).then_inc(yrT_sb, 1)

            yrT_out(0, 0)
            act.wait_ge(r_ps, 1)
            nc.scalar.copy(rT[:, TPB - 2:TPB, :].rearrange("p t k -> p (t k)"), bank(6)[:, 0:2 * P]).then_inc(r_sb, 1)

            def x1_norm(b, c):
                i = 2 * b + c
                act.wait_ge(ln1_step, 3 * i + 3)
                wait_free(act, r2_ok, i - 1)
                for j in range(SUP):
                    last = nc.scalar.activation(x1[:, c, j * P:(j + 1) * P], r1[:, j * P:(j + 1) * P], ACT.Identity,
                                                scale=rs1[:, j:j + 1], bias=nm1[:, j:j + 1])
                last.then_inc(x1_ok, 1)

            def x1_high(b, c):
                i = 2 * b + c
                act.wait_ge(x1T_ps, i + 1)
                wait_free(act, h_ps, FB * (i - 1))
                nc.scalar.copy(x1h[:, c, :], bank(2)).then_inc(x1h_ok, 1)

            def hidden_high(b, c, f):
                i = 2 * b + c
                act.wait_ge(h_ps, FB * i + f + 1)
                if f == 0:
                    wait_free(act, ff_ps, i - 1)
                nc.scalar.activation(hh[:, c, f, :], bank(3 + f % 2), ACT.Relu).then_inc(hh_ok, 1)

            def x2_norm(b, c):
                i = 2 * b + c
                act.wait_ge(ln2_step, 3 * i + 3)
                for j in range(SUP):
                    last = nc.scalar.activation(x2s[:, c, j * P:(j + 1) * P], r2[:, j * P:(j + 1) * P], ACT.Identity,
                                                scale=rs2[:, j:j + 1], bias=nm2[:, j:j + 1])
                last.then_inc(x2_ok, 1)

            def x2T_out(b, c):
                i = 2 * b + c
                act.wait_ge(x2T_ps, i + 1)
                nc.scalar.copy(x2T[:, bass.ds(b * 1024 + c * 512, 512)], bank(6)).then_inc(x2T_sb, 1)
                if c == 1:
                    nc.scalar.copy(gram[:, bass.ds(b, 1), :], bank(7)[:, 0:D].unsqueeze(1)).then_inc(gram_sb, 1)

            def body(b, c, prev=None, nxt=None, then=None, before=None, between=None):
                hidden_high(b, c, 0)
                hidden_high(b, c, 1)
                if nxt is not None:
                    x1_norm(*nxt)
                if before is not None:
                    x2T_out(*before)
                    act.wait_ge(x2_kept[c], 16 * (before[0] + 1))
                hidden_high(b, c, 2)
                hidden_high(b, c, 3)
                if between is not None:
                    between(0)
                if then is not None:
                    yrT_out(*then)
                if nxt is not None:
                    x1_high(*nxt)
                if prev is not None:
                    x2_norm(*prev)

            yrT_out(0, 1)
            x1_norm(0, 0)
            x1_high(0, 0)
            body(0, 0, nxt=(0, 1), then=(1, 0))
            body(0, 1, (0, 0), (1, 0), (1, 1))
            with act.Fori(1, B - 1) as b:
                body(b, 0, (b - 1, 1), (b, 1), (b + 1, 0), (b - 1, 0))
                body(b, 1, (b, 0), (b + 1, 0), (b + 1, 1), (b - 1, 1))
            def mix_gram(g):
                act.wait_ge(m1_ps, g + 1)
                nc.scalar.copy(gq[:, 2 * g * D:2 * (g + 1) * D], bank(6 * g)[:, 0:2 * D]).then_inc(m1_sb, 1)

            def mix_exp(g):
                act.wait_ge(lg_ok, g + 1)
                nc.scalar.activation(ea[:, 2 * g:2 * g + 2, :], lg[:, 2 * g:2 * g + 2, :], ACT.Exp).then_inc(ea_ok, 1)

            def mix_out(g):
                act.wait_ge(m4_ps, g + 1)
                nc.scalar.copy(p1[:, 2 * g * ME:2 * (g + 1) * ME], bank(6 * g + 1)[:, 0:2 * ME]).then_inc(m4_sb, 1)

            def mix_values(g):
                act.wait_ge(m5_ps, g + 1)
                nc.scalar.copy(mix[:, 2 * g * ME:2 * (g + 1) * ME], bank(6 * g)[:, 0:2 * ME]).then_inc(mix_ok, 1)

            mix_gram(0)
            body(B - 1, 0, (B - 2, 1), (B - 1, 1), before=(B - 2, 0))
            body(B - 1, 1, (B - 1, 0), before=(B - 2, 1), between=mix_exp)
            mix_out(0)
            x2T_out(B - 1, 0)
            mix_values(0)
            x2_norm(B - 1, 1)

            def x3_rstd(b, c):
                i = 2 * b + c
                act.wait_ge(mv3_ok, i + 1)
                nc.scalar.activation(lv3[:, :], mv3[:, :, 1], ACT.Ln, bias=epsT[:, 0:1]).then_inc(lv3_ok, 1)
                wait_free(act, oh_ok, i)
                act.wait_ge(lv3_ok, i + 1)
                nc.scalar.activation(rs3[:, :], lv3[:, :], ACT.Exp, scale=-0.5).then_inc(rs3_ok, 1)
                nc.scalar.activation(sq3[:, :], lv3[:, :], ACT.Exp, scale=-1.0).then_inc(s4_step, 1)
                act.wait_ge(s4_step, 3 * i + 1)
                nc.scalar.activation(lq3[:, :], sq3[:, :], ACT.Ln, scale=-EPS, bias=onep[:, 0:1]).then_inc(s4_step, 1)
                act.wait_ge(s4_step, 3 * i + 2)
                nc.scalar.activation(s43[:, c, :], lq3[:, :], ACT.Exp, scale=-0.5).then_inc(s4_step, 1)

            def x3_norm(b, c):
                i = 2 * b + c
                act.wait_ge(carry_ok, 1)
                act.wait_ge(nm3_ok, i + 1)
                for j in range(SUP):
                    last = nc.scalar.activation(work1[:, bass.ds((SUP * i + j) * ROW, D)], r3[:, c, j * P:(j + 1) * P],
                                                ACT.Identity, scale=rs3[:, j:j + 1], bias=nm3[:, j:j + 1])
                last.then_inc(x3_ok, 1)

            def x4_norm(b, c):
                i = 2 * b + c
                act.wait_ge(s4_step, 3 * i + 3)
                act.wait_ge(x3_ok, i + 1)
                wait_free(act, stored[c], 16 * b)
                for j in range(SUP):
                    last = nc.scalar.activation(x4[:, c, j * P:(j + 1) * P],
                                                work1[:, bass.ds(2 * SUP * ROW * b + (SUP * c + j) * ROW, D)],
                                                ACT.Copy, scale=s43[:, c, j:j + 1])
                last.then_inc(x4_ok, 1)

            def gate_exp(b, c):
                i = 2 * b + c
                act.wait_ge(gl_ok, i + 1)
                nc.scalar.activation(ge[:, :, :], gl[:, :, :], ACT.Exp).then_inc(ge_ok, 1)

            def body(b, c, nxt):
                if nxt is not None:
                    x3_rstd(*nxt)
                    x3_norm(*nxt)
                    gate_exp(*nxt)
                x4_norm(b, c)

            act.wait_ge(carry_ok, 1)
            x3_rstd(0, 0)
            x2T_out(B - 1, 1)
            mix_gram(1)
            x3_norm(0, 0)
            gate_exp(0, 0)
            body(0, 0, (0, 1))
            mix_exp(1)
            mix_out(1)
            body(0, 1, (1, 0))
            mix_values(1)
            body(1, 0, (1, 1))
            with act.Fori(1, B - 1) as b:
                body(b, 1, (b + 1, 0))
                body(b + 1, 0, (b + 1, 1))
            body(B - 1, 1, None)

            def xeT_out(k, c):
                e = 2 * k + c
                act.wait_ge(xeT_ps, e + 1)
                wait_free(act, eh_ps, FB * (e - 1))
                nc.scalar.copy(xeT[:, c, :], pair(0)[:, 0:CAP]).then_inc(xeT_sb, 1)

            def expert_hidden(k, c, f):
                e = 2 * k + c
                act.wait_ge(eh_ps, FB * e + f + 1)
                if f == 0:
                    wait_free(act, ey_ps, e)
                n = 2 + 2 * (f % 2)
                nc.scalar.activation(eh[:, f, :].rearrange("p (a n) -> p a n", a=2), PS[:, n:n + 2, 0:CAP // 2], ACT.Relu,
                                     bias=eb1T[:, bass.ds(FB * e + f, 1)]).then_inc(eh_ok, 1)

            def y4_norm(k, c):
                e = 2 * k + c
                act.wait_ge(mv4_ok, e + 1)
                nc.scalar.activation(lv4[:, :], mv4[:, :, 1], ACT.Ln, bias=epsT[:, 0:1]).then_inc(lv4_ok, 1)
                act.wait_ge(lv4_ok, e + 1)
                nc.scalar.activation(rs4[:, :], lv4[:, :], ACT.Exp, scale=-0.5).then_inc(rs4_ok, 1)
                act.wait_ge(ln4_step, e + 1)
                act.wait_ge(rs4_ok, e + 1)
                wait_free(act, put[c], 16 * CT * k)
                for j in range(CT):
                    last = nc.scalar.activation(y4[:, c, j, :], r4[:, j, :], ACT.Identity,
                                                scale=rs4[:, j:j + 1], bias=nm4[:, j:j + 1])
                last.then_inc(y4_ok, 1)

            def tile_rstd(c, j):
                act.wait_ge(mv4_ok, tiles_done(c, j))
                nc.scalar.activation(lv4[:, j:j + 1], mv4[:, j, 1:2], ACT.Ln, bias=epsT[:, 0:1]).then_inc(lv4_ok, 1)
                act.wait_ge(lv4_ok, tiles_done(c, j))
                nc.scalar.activation(rs4[:, j:j + 1], lv4[:, j:j + 1], ACT.Exp, scale=-0.5).then_inc(rs4_ok, 1)

            def expert(k, c, nxt, prev):
                for f in range(FB):
                    if f == FB // 2 and prev is not None:
                        y4_norm(*prev)
                    expert_hidden(k, c, f)
                if nxt is not None:
                    xeT_out(*nxt)

            xeT_out(0, 0)
            expert(0, 0, (0, 1), None)
            expert(0, 1, (1, 0), (0, 0))
            expert(1, 0, (1, 1), (0, 1))
            with act.Fori(1, E // 2 - 1) as k:
                expert(k, 1, (k + 1, 0), (k, 0))
                expert(k + 1, 0, (k + 1, 1), (k, 1))
            for f in range(FB - 1):
                expert_hidden(E // 2 - 1, 1, f)
                tile_rstd(0, f)
            tile_rstd(0, FB - 1)
            expert_hidden(E // 2 - 1, 1, FB - 1)
            for j in range(FB, CT):
                tile_rstd(0, j)
            for j in range(CT):
                tile_rstd(1, j)

        @block_.vector
        def _(dve):
            V = nc.vector
            step = [0]

            def link(ins):
                step[0] += 1
                ins.then_inc(dve1, 1)
                dve.wait_ge(dve1, step[0])

            V.memset(craw[:, :, 0:TAPS - 1], 0.0).then_inc(pad_ok, 1)
            V.memset(selA[:, :, :, :], 0.0)
            V.memset(empty[:, :], 0.0).then_inc(k_empty, 1)
            dve.wait_ge(k_empty, 1)
            V.memset(empty[:, D + 1:D + 2].bitcast(I32), TOK).then_inc(k_empty, 1)
            dve.wait_ge(k_pool, 1)
            for a in range(2):
                V.tensor_scalar(selA[:, :, a, :], ident[0:H, 0:H].unsqueeze(1).to_broadcast([H, B, H]),
                                1.0 - 2.0 * a, None, ALU.mult)
                last = V.tensor_copy(selB[:, :, a, :], ident[0:H, 0:H].unsqueeze(1).to_broadcast([H, B, H]))
            last.then_inc(k_sel, 1)
            V.memset(epsT[:, :], EPS)
            V.memset(mhalf[:, :], -0.5)
            V.memset(base16[:, :], 0.0)
            V.memset(b1s[:, :], 0.0)
            V.memset(b2s[:, :], 0.0)
            link(V.memset(eb2s[:, :], 0.0))
            dve.wait_ge(k_pool, 7)
            V.tensor_scalar(lim8[:, :], base8[:, :], float(CAP), None, ALU.add)
            V.tensor_copy(base16[0:1, :], base8[0:1, :])
            V.tensor_reduce(diag8[:, :], ident[:, :].rearrange("p (h d) -> p d h", h=H), axis=AX, op=ALU.add)
            V.tensor_copy(ident16[:, :], ident[:, :])
            V.tensor_copy(upper16[:, :], upper[:, :]).then_inc(k_const, 1)
            def x_out(n):
                dve.wait_ge(xT_ps, n + 1)
                V.tensor_copy(xT[:, n * 512:(n + 1) * 512], bank(2)).then_inc(xT_sb[1], 1)

            x_out(1)
            dve.wait_ge(ld_w, 80)
            V.tensor_reduce(wabs[:, 0:1], w1n[:, :, :].rearrange("p k d -> p (k d)"), axis=AX, op=ALU.add,
                            apply_absolute_value=True)
            V.tensor_reduce(wabs[:, 1:2], w2n[:, :], axis=AX, op=ALU.add,
                            apply_absolute_value=True).then_inc(wabs_ok, 1)
            dve.wait_ge(win_sb, 3)
            V.tensor_scalar(nega[:, :], acol[:, 0:1], -1.0, None, ALU.mult).then_inc(nega_ok, 1)
            dve.wait_ge(ld_small, 64)
            dve.wait_ge(pad_ok, 1)

            def convolve(n, k):
                if k == 0:
                    dve.wait_ge(proj_sb, 2 * n + 2)
                ins = V.scalar_tensor_tensor(out=conv[:, n, :], in0=craw[:, n, k:k + S],
                                             scalar=convw[:, n, k:k + 1], in1=conv[:, n, :],
                                             op0=ALU.mult, op1=ALU.add)
                if k < TAPS - 2:
                    link(ins)
                else:
                    ins.then_inc(conv_ok, 1)

            x_out(3)
            convolve(0, 0)
            convolve(0, 1)
            x_out(5)
            convolve(0, 2)
            x_out(7)
            for k in range(TAPS - 1):
                convolve(1, k)
            dve.wait_ge(dt_abs, 1)
            V.tensor_scalar(s4[:, :], pair(6), acol[:, 1:2], 0.0, ALU.add, ALU.max).then_inc(dt_pos, 1)
            dve.wait_ge(dt_ln, 1)
            dve.wait_ge(dt_pos, 1)
            link(V.tensor_tensor(s3[:, :], s3[:, :], s4[:, :], ALU.add))
            dve.wait_ge(k_ones, 3)
            V.tensor_tensor_scan(cum[:, :], onesS[:, :], s3[:, :], 0.0, ALU.mult, ALU.add).then_inc(cum_ok, 1)
            dve.wait_ge(tap_ok, 3)
            link(V.tensor_tensor(taps[1], taps[1], taps[2], ALU.add))
            dve.wait_ge(tap_sum, 1)
            V.tensor_tensor(conv[:, 2, :], conv[:, 2, :], taps[1], ALU.add).then_inc(conv_ok, 1)
            dve.wait_ge(exp_ok, 1)
            V.tensor_tensor_scan(s5[:, :], onesS[:, :], expn[:, :], 0.0, ALU.mult, ALU.add).then_inc(cs_ok, 1)
            dve.wait_ge(lncs_ok, 1)
            V.scalar_tensor_tensor(out=s2[:, :], in0=cum[:, :], scalar=nega[:, 0:1], in1=s4[:, :],
                                   op0=ALU.mult, op1=ALU.subtract).then_inc(lr_ok, 1)
            dve.wait_ge(ld_bias, 48)
            for src, dst in ((b1r, b1s), (b2r, b2s), (eb2r, eb2s)):
                link(V.tensor_copy(dst[0:1, :], src[0:1, :]))
                last = V.tensor_tensor(dst[32:33, :], src[0:1, :], dst[0:1, :], ALU.subtract)
            last.then_inc(bias_ok, 1)

            def add_state(t):
                dve.wait_ge(off_ps, t)
                dve.wait_ge(yi_ok, t + 1)
                wait_free(dve, y0_ok, t - 3)
                V.tensor_tensor(ys[:, t % 4, :], bank(6)[:, 0:D], yi[:, t % 2, :], ALU.add).then_inc(ys_ok, 1)

            for t in range(TPB):
                c = t % 2
                wait_free(dve, yi_ok, t - 1)
                dve.wait_ge(cum_ps, t + 1)
                V.tensor_tensor(cz[:, c, :].rearrange("p (h d n) -> p h d n", h=H, d=HD),
                                pair(2 + 2 * c).rearrange("p (h d n) -> p h d n", h=H, d=HD),
                                bcx[:, t % 3, 0:D].rearrange("p (h n) -> p h n", h=H).unsqueeze(2).to_broadcast([P, H, HD, HD]),
                                ALU.mult).then_inc(cz_ok, 1)
                if t < TPB - 1:
                    dve.wait_ge(st_ps, t + 1)
                    wait_free(dve, off_ps, t - 1)
                    V.tensor_tensor(st[:, c, :], bank(7)[:, 0:D], block[:, :], ALU.mult).then_inc(st_ok, 1)
                dve.wait_ge(cz_ok, t + 1)
                wait_free(dve, ys_ok, t - 2)
                if t == 0:
                    V.tensor_reduce(ys[:, 0, :], cz[:, c, :].rearrange("p (k n) -> p k n", n=HD),
                                    axis=AX, op=ALU.add).then_inc(yi_ok, 1)
                else:
                    V.tensor_reduce(yi[:, t % 2, :], cz[:, c, :].rearrange("p (k n) -> p k n", n=HD),
                                    axis=AX, op=ALU.add).then_inc(yi_ok, 1)
                    add_state(t)
            def moments(i, r, r_ok, st, st_ok, mv, mv_ok):
                dve.wait_ge(r_ok, i + 1)
                for j in range(SUP):
                    last = V.bn_stats(st[:, j, :], r[:, j * P:(j + 1) * P])
                last.then_inc(st_ok, 1)
                dve.wait_ge(k_const, 1)
                dve.wait_ge(st_ok, i + 1)
                for j in range(SUP):
                    last = V.bn_aggr(mv[:, j, :], st[:, j, :])
                last.then_inc(mv_ok, 1)

            def add1(b, c):
                i = 2 * b + c
                dve.wait_ge(ao_ps, i + 1)
                wait_free(dve, x1_ok, i)
                V.tensor_tensor(r1[:, :], bank(1), xt[:, :, :].rearrange("p t d -> p (t d)")[:, bass.ds(b * 1024 + c * 512, 512)],
                                ALU.add).then_inc(r1_ok, 1)

            def moments1(b, c):
                i = 2 * b + c
                moments(i, r1, r1_ok, st1, st1_ok, mv1, mv1_ok)
                dve.wait_ge(mv1_ok, i + 1)
                V.tensor_scalar(neg1[:, :], mv1[:, :, 0], -1.0, None, ALU.mult).then_inc(neg1_ok, 1)

            def x1_low(b, c):
                i = 2 * b + c
                dve.wait_ge(x1h_ok, i + 1)
                V.tensor_tensor(x1l[:, c, :], bank(2), x1h[:, c, :], ALU.subtract).then_inc(x1l_ok, 1)

            def hidden_low(b, c, f):
                i = 2 * b + c
                dve.wait_ge(hh_ok, FB * i + f + 1)
                V.scalar_tensor_tensor(out=hl[:, c, f, :], in0=bank(3 + f % 2), scalar=0.0, in1=hh[:, c, f, :],
                                       op0=ALU.max, op1=ALU.subtract).then_inc(hl_ok, 1)

            def add2(b, c):
                i = 2 * b + c
                dve.wait_ge(ff_ps, i + 1)
                wait_free(dve, x2_ok, i)
                V.tensor_tensor(r2[:, :], bank(5), x1[:, c, :], ALU.add).then_inc(r2_ok, 1)

            def moments2(b, c):
                i = 2 * b + c
                moments(i, r2, r2_ok, st2, st2_ok, mv2, mv2_ok)
                dve.wait_ge(mv2_ok, i + 1)
                V.tensor_scalar(neg2[:, :], mv2[:, :, 0], -1.0, None, ALU.mult).then_inc(neg2_ok, 1)

            def body(b, c, prev=None, nxt=None, then=None, between=None):
                if prev is not None:
                    add2(*prev)
                hidden_low(b, c, 0)
                hidden_low(b, c, 1)
                if prev is not None:
                    moments2(*prev)
                hidden_low(b, c, 2)
                hidden_low(b, c, 3)
                if between is not None:
                    between(0)
                if nxt is not None:
                    x1_low(*nxt)
                if then is not None:
                    add1(*then)
                    moments1(*then)

            add1(0, 0)
            moments1(0, 0)
            add1(0, 1)
            x1_low(0, 0)
            moments1(0, 1)
            body(0, 0, nxt=(0, 1), then=(1, 0))
            body(0, 1, (0, 0), (1, 0), (1, 1))
            with dve.Fori(1, B - 1) as b:
                body(b, 0, (b - 1, 1), (b, 1), (b + 1, 0))
                body(b, 1, (b, 0), (b + 1, 0), (b + 1, 1))
            dve.wait_ge(ld_l1, 64)
            V.tensor_scalar(tau32[:, :], tauc[:, :], float(S) ** -0.5, None, ALU.mult)
            step = [0]

            def link2(ins):
                step[0] += 1
                ins.then_inc(mixs, 1)
                dve.wait_ge(mixs, step[0])

            def two(g, tensor):
                return tensor[:, 2 * g:2 * g + 2]

            def mix_dots(g):
                dve.wait_ge(m2_ps, g + 1)
                link2(V.tensor_tensor(two(g, dm), bank(6 * g + 1)[:, 0:2 * D].rearrange("p (b f) -> p b f", b=2),
                                      block[:, :].unsqueeze(1).to_broadcast([P, 2, D]), ALU.mult))
                link2(V.tensor_reduce(two(g, dc), two(g, dm).rearrange("p b (h d) -> p b d h", h=H), axis=AX, op=ALU.add))
                V.tensor_tensor(two(g, dq), two(g, dc), diag8[:, :].unsqueeze(1).to_broadcast([P, 2, HD]),
                                ALU.mult).then_inc(dq_ok, 1)
                dve.wait_ge(dq_ok, g + 1)
                link2(V.tensor_reduce(two(g, qc), two(g, dq), axis=AX, op=ALU.add))

            def mix_logits(g):
                dve.wait_ge(m3_ps, g + 1)
                link2(V.scalar_tensor_tensor(out=two(g, lg), in0=two(g, dc), scalar=2.0,
                                             in1=bank(6 * g)[:, 0:2 * HD].rearrange("p (b d) -> p b d", b=2),
                                             op0=ALU.mult, op1=ALU.subtract))
                link2(V.tensor_tensor(two(g, lg), two(g, lg), two(g, qc).unsqueeze(2).to_broadcast([P, 2, HD]), ALU.subtract))
                link2(V.tensor_scalar(two(g, lg), two(g, lg), tau32[:, 0:1], None, ALU.mult))
                link2(V.tensor_reduce(two(g, mx), two(g, lg), axis=AX, op=ALU.max))
                V.tensor_tensor(two(g, lg), two(g, lg), two(g, mx).unsqueeze(2).to_broadcast([P, 2, HD]),
                                ALU.subtract).then_inc(lg_ok, 1)

            def mix_weights(g):
                dve.wait_ge(ea_ok, g + 1)
                link2(V.tensor_reduce(two(g, mx), two(g, ea), axis=AX, op=ALU.add))
                link2(V.reciprocal(two(g, mx), two(g, mx)))
                link2(V.tensor_tensor(two(g, ea), two(g, ea), two(g, mx).unsqueeze(2).to_broadcast([P, 2, HD]), ALU.mult))
                V.tensor_tensor(two(g, ad).rearrange("p b (h d) -> p b h d", h=H),
                                two(g, ea).unsqueeze(2).to_broadcast([P, 2, H, HD]),
                                block[:, :].rearrange("p (h d) -> p h d", h=H).unsqueeze(1).to_broadcast([P, 2, H, HD]),
                                ALU.mult).then_inc(ad_ok, 1)

            body(B - 1, 0, (B - 2, 1), (B - 1, 1))
            mix_dots(0)
            body(B - 1, 1, (B - 1, 0), between=mix_logits)
            mix_weights(0)
            add2(B - 1, 1)
            moments2(B - 1, 1)

            V.memset(carry[:, :], 0.0)
            V.memset(onep[:, :], 1.0 + EPS).then_inc(carry_ok, 1)

            def attended(c, first, last):
                return PS[:, 2 * c:2 * c + 2, 0:2 * ME].rearrange("p a (t k) -> p a t k", k=ME)[:, :, :, first:last]

            def add3(b, c):
                i = 2 * b + c
                dve.wait_ge(o3_ps, i + 1)
                wait_free(dve, x3_ok, i - 1)
                V.tensor_tensor(r3[:, c, :].rearrange("p (a t d) -> p a t d", a=2, t=2), attended(c, 0, D),
                                x2k[:, bass.ds(b * 1024 + c * 512, 512)].rearrange("p (a t d) -> p a t d", a=2, t=2),
                                ALU.add).then_inc(r3_ok, 1)

            def moments3(b, c):
                i = 2 * b + c
                moments(i, r3[:, c, :], r3_ok, st3, st3_ok, mv3, mv3_ok)

            by_tile = [P, SUP, E]
            GATE_STEPS, ROUTE_STEPS = 6, 7

            def gate_and_route(nxt, cur):
                if nxt is not None:
                    nb, n_c = nxt
                    n = 2 * nb + n_c
                if cur is not None:
                    b, c = cur
                    i = 2 * b + c
                    pos = bank(4 + c)[:, 0:SUP * E].rearrange("p (t e) -> p t e", t=SUP)
                    dve.wait_ge(oh_ok, i + 1)
                    V.tensor_reduce(ohs[:, :], oh[:, c, :, :].rearrange("p t e -> p e t"),
                                    axis=AX, op=ALU.add).then_inc(route_step, 1)
                    dve.wait_ge(pos_ps, i + 1)
                    V.tensor_tensor(sl1[:, :, :], pos, lim8[:, :].unsqueeze(1).to_broadcast(by_tile),
                                    ALU.is_gt).then_inc(route_step, 1)
                    dve.wait_ge(route_step, ROUTE_STEPS * i + 1)
                    V.tensor_tensor(carry[:, :], carry[:, :], ohs[:, :], ALU.add).then_inc(carry_ok, 1)
                    dve.wait_ge(route_step, ROUTE_STEPS * i + 2)
                    V.scalar_tensor_tensor(out=sl2[:, :, :], in0=sl1[:, :, :], scalar=DROP, in1=pos,
                                           op0=ALU.mult, op1=ALU.add).then_inc(route_step, 1)
                    dve.wait_ge(ge_ok, i + 1)
                    V.tensor_reduce(gs[:, :], ge[:, :, :], axis=AX, op=ALU.add).then_inc(route_step, 1)
                if nxt is not None:
                    dve.wait_ge(rs3_ok, n + 1)
                    V.scalar_tensor_tensor(out=nm3[:, :], in0=mv3[:, :, 0], scalar=-1.0, in1=rs3[:, :],
                                           op0=ALU.mult, op1=ALU.mult).then_inc(nm3_ok, 1)
                    V.tensor_tensor(l1[:, :, :].rearrange("p (a t) e -> p a t e", a=2), attended(n_c, D, ME),
                                    rs3[:, :].rearrange("p (a t) -> p a t", a=2).unsqueeze(3).to_broadcast([P, 2, 2, E]), ALU.mult)
                if cur is not None:
                    dve.wait_ge(route_step, ROUTE_STEPS * i + 3)
                    V.tensor_tensor(sl1[:, :, :], sl2[:, :, :], oh[:, c, :, :], ALU.mult).then_inc(route_step, 1)
                if nxt is not None:
                    dve.wait_ge(nm3_ok, n + 1)
                    V.tensor_tensor(l2[:, :, :], wgsum[:, :].unsqueeze(1).to_broadcast(by_tile),
                                    nm3[:, :].unsqueeze(2).to_broadcast(by_tile), ALU.mult).then_inc(gate_step, 1)
                if cur is not None:
                    dve.wait_ge(route_step, ROUTE_STEPS * i + 4)
                    V.reciprocal(rows[:, bass.ds(SUP * i, SUP), D], gs[:, :]).then_inc(route_step, 1)
                if nxt is not None:
                    dve.wait_ge(gate_step, GATE_STEPS * n + 1)
                    V.tensor_tensor(l1[:, :, :], l1[:, :, :], l2[:, :, :], ALU.add).then_inc(gate_step, 1)
                if cur is not None:
                    V.tensor_copy(rows[:, bass.ds(SUP * i, SUP), D + 1].bitcast(I32), tokid[:, bass.ds(SUP * i, SUP)]).then_inc(route_step, 1)
                if nxt is not None:
                    dve.wait_ge(gate_step, GATE_STEPS * n + 2)
                    V.tensor_reduce(gmax[:, :], l1[:, :, :], axis=AX, op=ALU.max).then_inc(gate_step, 1)
                if cur is not None:
                    wait_free(dve, slot_ok, i)
                    dve.wait_ge(route_step, ROUTE_STEPS * (i + 1))
                    V.tensor_reduce(slf[:, :], sl1[:, :, :], axis=AX, op=ALU.add).then_inc(slf_ok, 1)
                if nxt is not None:
                    dve.wait_ge(gate_step, GATE_STEPS * n + 3)
                    V.tensor_tensor(eqv[:, :, :], l1[:, :, :], gmax[:, :].unsqueeze(2).to_broadcast(by_tile),
                                    ALU.is_ge).then_inc(gate_step, 1)
                    V.tensor_tensor(gl[:, :, :], l1[:, :, :], gmax[:, :].unsqueeze(2).to_broadcast(by_tile),
                                    ALU.subtract).then_inc(gl_ok, 1)
                    dve.wait_ge(gate_step, GATE_STEPS * n + 4)
                    V.tensor_tensor(eqv[:, :, :], eqv[:, :, :], rev8[:, :].unsqueeze(1).to_broadcast(by_tile),
                                    ALU.mult).then_inc(gate_step, 1)
                    dve.wait_ge(gate_step, GATE_STEPS * n + 5)
                    V.tensor_reduce(vmax[:, :], eqv[:, :, :], axis=AX, op=ALU.max).then_inc(gate_step, 1)
                    dve.wait_ge(gate_step, GATE_STEPS * n + 6)
                    V.tensor_tensor(oh[:, n_c, :, :], eqv[:, :, :], vmax[:, :].unsqueeze(2).to_broadcast(by_tile),
                                    ALU.is_equal).then_inc(oh_ok, 1)

            def body(b, c, nxt):
                if nxt is not None:
                    add3(*nxt)
                    moments3(*nxt)
                gate_and_route(nxt, (b, c))

            dve.wait_ge(wg_sb, 1)
            add3(0, 0)
            moments3(0, 0)
            gate_and_route((0, 0), None)
            add3(0, 1)
            moments3(0, 1)
            mix_dots(1)
            gate_and_route((0, 1), (0, 0))
            mix_logits(1)
            mix_weights(1)
            body(0, 1, (1, 0))
            for c in range(2):
                dve.wait_ge(x2_kept[c], 16 * B)
            body(1, 0, (1, 1))
            with dve.Fori(1, B - 1) as b:
                body(b, 1, (b + 1, 0))
                body(b + 1, 0, (b + 1, 1))
            body(B - 1, 1, None)

            def keep_slots(k, c):
                dve.wait_ge(lds[c], 16 * (k + 1))
                wait_free(dve, put[c], 16 * CT * k)
                V.tensor_copy(xr[:, c, :, :], xs[:, c, :, :]).then_inc(xr_ok, 1)
                dve.wait_ge(xr_ok, 2 * k + c + 1)

            def expert(k, c):
                e = 2 * k + c
                keep_slots(k, c)
                dve.wait_ge(ey_ps, e + 1)
                wait_free(dve, y4_ok, e)
                for j in range(CT):
                    last = V.scalar_tensor_tensor(out=r4[:, j, :], in0=pair(6)[:, j * D:(j + 1) * D],
                                                  scalar=xr[:, c, j, D:D + 1], in1=xr[:, c, j, 0:D],
                                                  op0=ALU.mult, op1=ALU.add)
                last.then_inc(r4_ok, 1)
                dve.wait_ge(r4_ok, e + 1)
                for j in range(CT):
                    last = V.bn_stats(st4[:, j, :], r4[:, j, :])
                last.then_inc(st4_ok, 1)
                dve.wait_ge(k_const, 1)
                dve.wait_ge(st4_ok, e + 1)
                for j in range(CT):
                    last = V.bn_aggr(mv4[:, j, :], st4[:, j, :])
                last.then_inc(mv4_ok, 1)
                dve.wait_ge(mv4_ok, e + 1)
                V.tensor_scalar(neg4[:, :], mv4[:, :, 0], -1.0, None, ALU.mult).then_inc(neg4_ok, 1)

            def tile_norm(c, j):
                dve.wait_ge(rs4_ok, tiles_done(c, j))
                V.tensor_scalar(y4[:, c, j, :], r4[:, j, :], mv4[:, j, 0:1], rs4[:, j:j + 1],
                                ALU.subtract, ALU.mult).then_inc(y4_ok, 1)

            def expert_by_tile(c):
                if c == 0:
                    keep_slots(E // 2 - 1, 0)
                    dve.wait_ge(y4_ok, E - 2)
                for j in range(CT):
                    dve.wait_ge(ey_ps, E - 1 if c == 0 else E + j)
                    V.scalar_tensor_tensor(out=r4[:, j, :], in0=last_out(c, j),
                                           scalar=xr[:, c, j, D:D + 1], in1=xr[:, c, j, 0:D],
                                           op0=ALU.mult, op1=ALU.add).then_inc(r4_ok, 1)
                    dve.wait_ge(r4_ok, tiles_done(c, j))
                    V.bn_stats(st4[:, j, :], r4[:, j, :]).then_inc(st4_ok, 1)
                    dve.wait_ge(st4_ok, tiles_done(c, j))
                    V.bn_aggr(mv4[:, j, :], st4[:, j, :]).then_inc(mv4_ok, 1)
                    if j > 0:
                        tile_norm(c, j - 1)
                if c == 0:
                    keep_slots(E // 2 - 1, 1)
                tile_norm(c, CT - 1)

            expert(0, 0)
            expert(0, 1)
            with dve.Fori(1, E // 2 - 1) as k:
                expert(k, 0)
                expert(k, 1)
            expert_by_tile(0)
            expert_by_tile(1)

        @block_.tensor
        def _(pe):
            T = nc.tensor
            pe.wait_ge(k_pool, 1)
            pe.wait_ge(ld_win, 32)
            for n in range(3):
                T.transpose(bank(0)[:, n * D:(n + 1) * D], win[:, n, :], ident[:, :])
            last = T.transpose(bank(0)[:, 3 * D:3 * D + H], windt[:, :], ident[0:H, 0:H])
            last.then_inc(win_ps, 1)

            def x_in(n):
                pe.wait_ge(ld_x[n // 2], 16)
                wait_free(pe, xT_sb[n % 2], n // 2)
                for j in range(SUP):
                    last = T.transpose(bank(1 + n % 2)[:, j * P:(j + 1) * P], xt[:, n * SUP + j, :], ident[:, :])
                last.then_inc(xT_ps, 1)

            x_in(0)
            x_in(1)
            pe.wait_ge(k_sel, 1)
            pe.wait_ge(ld_small, 64)
            pe.wait_ge(win_sb, 2)
            T.matmul(bank(0)[:, 400:401], selA[:, :, :, :].rearrange("p b a h -> p (b a h)"), ab[:, 0:1], start=True, stop=True)
            T.matmul(bank(0)[:, 401:402], selB[:, :, :, :].rearrange("p b a h -> p (b a h)"), ab[:, 1:2], start=True, stop=True).then_inc(acol_ps, 1)

            def dt_in(n):
                pe.wait_ge(xT_sb[n % 2], n // 2 + 1)
                T.matmul(PS[32 * (n // 2):32 * (n // 2) + 32, 6 + n % 2, :], wdtT[:, :], xT[:, n * 512:(n + 1) * 512],
                         start=True, stop=True).then_inc(dt_ps, 1)

            pe.wait_ge(xT_sb[0], 1)
            pe.wait_ge(xT_sb[1], 1)
            for n in range(6):
                if n == 2:
                    pe.wait_ge(wabs_ok, 1)
                    pe.wait_ge(win_sb, 3)
                    T.matmul(bank(0)[:, 0:2], ones[:, :], wabs[:, :], start=True, stop=True).then_inc(wsum_ps, 1)
                wait_free(pe, proj_sb, n - 2)
                T.matmul(bank(3 + n % 3), winT[:, (n // 2) * D:(n // 2 + 1) * D], xT[:, (n % 2) * 512:(n % 2 + 1) * 512],
                         start=True, stop=True).then_inc(proj_ps, 1)
                x_in(2 + n)
                dt_in(n)
            dt_in(6)
            dt_in(7)
            pe.wait_ge(proj_sb, 6)
            pe.wait_ge(ld_w, 80)
            T.transpose(bank(5)[:, 0:D], wout[:, :], ident[:, :])
            T.transpose(bank(5)[:, D:2 * D], wv[:, :], ident[:, :])
            T.transpose(bank(5)[:, 2 * D:2 * D + E * FB], eb1n[:, :], ident[0:E * FB, 0:E * FB])
            pe.wait_ge(ld_l1, 64)
            T.transpose(bank(5)[:, 3 * D:4 * D], wo, ident[:, :]).then_inc(wT_ps, 1)

            def chunk_in(t):
                pe.wait_ge(conv_ok, 3)
                if t == 0:
                    pe.wait_ge(cut_ok, 2)
                if t == 1:
                    pe.wait_ge(xT_sb[0], NS // 2)
                wait_free(pe, tr_sb, t - 1)
                for n in range(3):
                    last = T.transpose(bank(t % 2)[:, n * D:(n + 1) * D], conv[:, n, t * P:(t + 1) * P], ident[:, :])
                if t >= 2:
                    pe.wait_ge(r_ok, 1)
                    last = T.transpose(bank(t % 2)[:, 3 * D:4 * D], s1[:, (t - 2) * P:(t - 1) * P], ident[:, :])
                last.then_inc(tr_ps, 1)

            def yr_transpose(b, c):
                i = 2 * b + c
                pe.wait_ge(yr_ok, i + 1)
                wait_free(pe, yrT_sb, i)
                for j in range(SUP):
                    last = T.transpose(bank(0)[:, j * P:(j + 1) * P], yr[:, c, j, :], ident[:, :])
                last.then_inc(yrT_ps, 1)

            def attn_out(b, c):
                i = 2 * b + c
                pe.wait_ge(yrT_sb, i + 1)
                wait_free(pe, r1_ok, i)
                for j in range(SUP):
                    last = T.matmul(bank(1)[:, j * P:(j + 1) * P], yrT[:, j * P:(j + 1) * P], woutT[:, :], start=True, stop=True)
                last.then_inc(ao_ps, 1)

            pe.wait_ge(exp_ok, 1)
            for t in range(TPB):
                last = T.transpose(bank(3)[:, t * 2 * H:(t + 1) * 2 * H], expn[0:2 * H, t * P:(t + 1) * P], ident[0:2 * H, 0:2 * H])
            last.then_inc(e_ps, 1)
            chunk_in(0)
            chunk_in(1)
            pe.wait_ge(k_const, 1)
            pe.wait_ge(q_ok, 2)
            for a in range(2):
                for k in range(FB):
                    src = q16[:, a, k * P:(k + 1) * P]
                    last = T.transpose(bank(4).bitcast(F16)[:, (a * FB + k) * P:(a * FB + k + 1) * P], src, ident16[:, :])
            last.then_inc(q_ps, 1)
            pe.wait_ge(wT_sb, 4)
            T.matmul(bank(5)[:, 0:E], woT[:, :], wgs[:, :], start=True, stop=True)
            T.matmul(bank(5)[:, E:2 * E], ones[:, :], wgs[:, :], start=True, stop=True).then_inc(wg_ps, 1)
            pe.wait_ge(dt_pos, 1)
            pe.wait_ge(e_sb, 1)
            pe.wait_ge(q_sb, 1)
            pe.wait_ge(wg_sb, 1)
            for t in range(TPB):
                c = t % 2
                if 0 < t < TPB - 2:
                    chunk_in(t + 2)
                pe.wait_ge(z_ok, t + 1)
                wait_free(pe, cz_ok, t - 1)
                for a in range(2):
                    last = T.matmul(bank(2 + 2 * c + a), upper[:, :], zz[:, c, a * 512:(a + 1) * 512], start=True, stop=True)
                last.then_inc(cum_ps, 1)
                if t == 0:
                    chunk_in(2)
                if t < TPB - 1:
                    pe.wait_ge(xp_ok, t + 1)
                    wait_free(pe, st_ok, t)
                    last = T.matmul(bank(7)[:, 0:D], bcx[:, t % 3, D:2 * D], xp[:, c, :], start=True, stop=t == 0)
                    if t > 0:
                        last = T.matmul(bank(7)[:, 0:D], ident[:, :], st[:, (t - 1) % 2, :], start=False, stop=True)
                    last.then_inc(st_ps, 1)
                if t > 0:
                    pe.wait_ge(st_ok, t)
                    wait_free(pe, ys_ok, t - 1)
                    T.matmul(bank(6)[:, 0:D], conv[:, 0, t * P:(t + 1) * P], st[:, (t - 1) % 2, :], start=True, stop=True).then_inc(off_ps, 1)
            pe.wait_ge(tr_sb, TPB)
            yr_transpose(0, 0)
            attn_out(0, 0)
            pe.wait_ge(ys_ok, TPB - 1)
            for t in (TPB - 2, TPB - 1):
                last = T.transpose(bank(6)[:, (t - TPB + 2) * P:(t - TPB + 3) * P], s1[:, t * P:(t + 1) * P], ident[:, :])
            last.then_inc(r_ps, 1)

            def x1_transpose(b, c):
                i = 2 * b + c
                pe.wait_ge(x1_ok, i + 1)
                wait_free(pe, x1l_ok, i)
                for j in range(SUP):
                    last = T.transpose(bank(2)[:, j * P:(j + 1) * P], x1[:, c, j * P:(j + 1) * P], ident[:, :])
                last.then_inc(x1T_ps, 1)

            def hidden(b, c, f):
                i = 2 * b + c
                if f == 0:
                    pe.wait_ge(x1l_ok, i + 1)
                wait_free(pe, hl_ok, FB * i + f - 1)
                T.matmul(bank(3 + f % 2), qT[:, 0, f, :], x1h[:, c, :], start=True, stop=False)
                T.matmul(bank(3 + f % 2), qT[:, 0, f, :], x1l[:, c, :], start=False, stop=False)
                T.matmul(bank(3 + f % 2), b1s[:, f * P:(f + 1) * P], ones16[:, :], start=False, stop=True).then_inc(h_ps, 1)

            def feed_out(b, c, f):
                i = 2 * b + c
                if f == 0:
                    wait_free(pe, r2_ok, i)
                    T.matmul(bank(5), ones16[:, 0:P], b2s[:, :].unsqueeze(1).to_broadcast([P, SUP, D]), start=True, stop=False)
                pe.wait_ge(hl_ok, FB * i + f + 1)
                for j in range(SUP):
                    o = bank(5)[:, j * P:(j + 1) * P]
                    T.matmul(o, hh[:, c, f, j * P:(j + 1) * P], qT[:, 1, f, :], start=False, stop=False)
                    last = T.matmul(o, hl[:, c, f, j * P:(j + 1) * P], qT[:, 1, f, :], start=False,
                                    stop=f == FB - 1 and j == SUP - 1)
                if f == FB - 1:
                    last.then_inc(ff_ps, 1)

            def x2_products(b, c, after=None):
                i = 2 * b + c
                pe.wait_ge(x2_ok, i + 1)
                if after is not None:
                    pe.wait_ge(x2T_sb, after)
                for j in range(SUP):
                    T.matmul(bank(7)[:, 0:D], x2s[:, c, j * P:(j + 1) * P], x2s[:, c, j * P:(j + 1) * P],
                             start=c == 0 and j == 0, stop=c == 1 and j == SUP - 1)
                for j in range(SUP):
                    last = T.transpose(bank(6)[:, j * P:(j + 1) * P], x2s[:, c, j * P:(j + 1) * P], ident[:, :])
                last.then_inc(x2T_ps, 1)

            def body(b, c, prev=None, nxt=None, then=None, before=None, between=None):
                hidden(b, c, 0)
                hidden(b, c, 1)
                if before is not None:
                    x2_products(*before)
                hidden(b, c, 2)
                hidden(b, c, 3)
                if between is not None:
                    between(0)
                if then is not None:
                    yr_transpose(*then)
                if nxt is not None:
                    x1_transpose(*nxt)
                feed_out(b, c, 0)
                feed_out(b, c, 1)
                if then is not None:
                    attn_out(*then)
                feed_out(b, c, 2)
                feed_out(b, c, 3)

            pe.wait_ge(r_sb, 1)
            pe.wait_ge(bias_ok, 1)
            pe.wait_ge(k_ones, 3)
            yr_transpose(0, 1)
            attn_out(0, 1)
            x1_transpose(0, 0)
            body(0, 0, nxt=(0, 1), then=(1, 0))
            body(0, 1, (0, 0), (1, 0), (1, 1))
            with pe.Fori(1, B - 1) as b:
                body(b, 0, (b - 1, 1), (b, 1), (b + 1, 0), (b - 1, 0))
                body(b, 1, (b, 0), (b + 1, 0), (b + 1, 1), (b - 1, 1))
            def mix_gram(g):
                pe.wait_ge(gram_sb, 2 * g + 2)
                pe.wait_ge(ld_l1, 64)
                for n in range(2):
                    last = T.matmul(bank(6 * g)[:, n * D:(n + 1) * D], gram[:, 2 * g + n, :], wqk[:, :], start=True, stop=True)
                last.then_inc(m1_ps, 1)

            def mix_dots(g):
                pe.wait_ge(m1_sb, g + 1)
                T.matmul(bank(6 * g + 1)[:, 0:2 * D], wqk[:, :], gq[:, 2 * g * D:2 * (g + 1) * D], start=True, stop=True).then_inc(m2_ps, 1)

            def mix_squares(g):
                pe.wait_ge(dq_ok, g + 1)
                T.matmul(bank(6 * g)[:, 0:2 * HD], block[:, :], dq[:, 2 * g:2 * g + 2, :].rearrange("p b d -> p (b d)"),
                         start=True, stop=True).then_inc(m3_ps, 1)

            def mix_out(g):
                pe.wait_ge(ad_ok, g + 1)
                pe.wait_ge(wg_sb, 1)
                for n in range(2):
                    last = T.matmul(bank(6 * g + 1)[:, n * ME:(n + 1) * ME], ad[:, 2 * g + n, :], wog[:, :], start=True, stop=True)
                last.then_inc(m4_ps, 1)

            def mix_values(g):
                pe.wait_ge(m4_sb, g + 1)
                T.matmul(bank(6 * g)[:, 0:2 * ME], wvT[:, :], p1[:, 2 * g * ME:2 * (g + 1) * ME], start=True, stop=False)
                for n in range(2):
                    last = T.matmul(bank(6 * g)[:, n * ME + D:(n + 1) * ME], ident[:, :], wgs[:, :], start=False, stop=n == 1)
                last.then_inc(m5_ps, 1)

            mix_gram(0)
            body(B - 1, 0, (B - 2, 1), (B - 1, 1), before=(B - 2, 0), between=mix_dots)
            mix_squares(0)
            body(B - 1, 1, (B - 1, 0), before=(B - 2, 1))
            mix_out(0)
            x2_products(B - 1, 0)
            mix_values(0)

            def attn2_out(b, c):
                i = 2 * b + c
                pe.wait_ge(staged[c], 16 * (b + 1))
                wait_free(pe, oh_ok, i - 1)
                for j in range(SUP):
                    last = T.matmul(bank(2 * c + j // 2)[:, j % 2 * ME:(j % 2 + 1) * ME], x2Ts[:, c, j * P:(j + 1) * P],
                                    mix[:, bass.ds(b * ME, ME)], start=True, stop=True)
                last.then_inc(o3_ps, 1)

            def places(b, c):
                i = 2 * b + c
                pe.wait_ge(oh_ok, i + 1)
                pe.wait_ge(carry_ok, i + 1)
                wait_free(pe, slf_ok, i - 1)
                flat = oh[:, c, :, :].rearrange("p t e -> p (t e)")
                T.matmul(bank(4 + c)[:, 0:SUP * E], upper16[:, :], flat, start=True, stop=False)
                for n in range(1, SUP):
                    T.matmul(bank(4 + c)[:, n * E:SUP * E], ones16[:, 0:P], flat[:, 0:(SUP - n) * E], start=False, stop=False)
                for add, stop in ((base16, False), (carry, True)):
                    last = T.matmul(bank(4 + c)[:, 0:SUP * E].rearrange("p (t e) -> p t e", t=SUP), ones16[:, 0:P],
                                    add[:, :].unsqueeze(1).to_broadcast([P, SUP, E]), start=False, stop=stop)
                last.then_inc(pos_ps, 1)

            def body(b, c, nxt):
                places(b, c)
                if nxt is not None:
                    attn2_out(*nxt)

            pe.wait_ge(mix_ok, 1)
            attn2_out(0, 0)
            x2_products(B - 1, 1, NS - 1)
            attn2_out(0, 1)
            mix_gram(1)
            mix_dots(1)
            mix_squares(1)
            body(0, 0, (1, 0))
            mix_out(1)
            body(0, 1, (1, 1))
            mix_values(1)
            pe.wait_ge(mix_ok, 2)
            with pe.Fori(1, B - 1) as b:
                body(b, 0, (b + 1, 0))
                body(b, 1, (b + 1, 1))
            body(B - 1, 0, None)
            body(B - 1, 1, None)

            def expert_in(k, c):
                e = 2 * k + c
                pe.wait_ge(lds[c], 16 * (k + 1))
                wait_free(pe, xeT_sb, e)
                for j in range(CT):
                    last = T.transpose(pair(0)[:, j * P:(j + 1) * P], xs[:, c, j, 0:D], ident[:, :])
                last.then_inc(xeT_ps, 1)

            def expert_hidden(k, c, f):
                e = 2 * k + c
                if f == 0:
                    pe.wait_ge(xeT_sb, e + 1)
                    pe.wait_ge(ldw[c], 32 * (k + 1))
                wait_free(pe, eh_ok, FB * e + f - 1)
                for a in range(2):
                    last = T.matmul(PS[:, 2 + 2 * (f % 2) + a, 0:CAP // 2], w1s[:, c, f * P:(f + 1) * P],
                                    xeT[:, c, a * (CAP // 2):(a + 1) * (CAP // 2)], start=True, stop=True)
                last.then_inc(eh_ps, 1)

            def expert_out(k, c, f):
                e = 2 * k + c
                if f == 0:
                    wait_free(pe, r4_ok, e)
                    bias = eb2s[:, bass.ds(e * D, D)]
                    T.matmul(bank(6).rearrange("p (t d) -> p t d", d=D), ones16[:, 0:P],
                             bias.unsqueeze(1).to_broadcast([P, 4, D]), start=True, stop=False)
                    T.matmul(bank(7)[:, 0:D], ones16[:, 0:P], bias, start=True, stop=False)
                pe.wait_ge(eh_ok, FB * e + f + 1)
                for j in range(CT):
                    last = T.matmul(pair(6)[:, j * D:(j + 1) * D], eh[:, f, j * P:(j + 1) * P], w2s[:, c, f, :],
                                    start=False, stop=f == FB - 1 and j in (3, CT - 1))
                if f == FB - 1:
                    last.then_inc(ey_ps, 1)

            def expert(k, c, nxt):
                for f in range(FB - 1):
                    expert_hidden(k, c, f)
                expert_out(k, c, 0)
                expert_hidden(k, c, FB - 1)
                if nxt is not None:
                    expert_in(*nxt)
                for f in range(1, FB):
                    expert_out(k, c, f)

            pe.wait_ge(slot_ok, NS)
            expert_in(0, 0)
            expert(0, 0, (0, 1))
            with pe.Fori(0, E // 2 - 1) as k:
                expert(k, 1, (k + 1, 0))
                expert(k + 1, 0, (k + 1, 1))
            k = E // 2 - 1
            for f in range(FB - 1):
                expert_hidden(k, 1, f)

            def tile_out(j, blocks):
                for f in blocks:
                    if f == 0:
                        T.matmul(last_out(1, j), ones16[:, 0:P], eb2s[:, (E - 1) * D:E * D], start=True, stop=False)
                    pe.wait_ge(eh_ok, FB * (E - 1) + f + 1)
                    last = T.matmul(last_out(1, j), eh[:, f, j * P:(j + 1) * P], w2s[:, 1, f, :],
                                    start=False, stop=f == FB - 1)
                if blocks[-1] == FB - 1:
                    last.then_inc(ey_ps, 1)

            tile_out(0, range(FB - 2))
            expert_hidden(k, 1, FB - 1)
            tile_out(1, range(FB - 2))
            for blocks in ((FB - 2,), (FB - 1,)):
                for j in range(2):
                    tile_out(j, blocks)
            pe.wait_ge(r4_ok, tiles_done(0, CT - 1))
            for j in range(2, CT):
                tile_out(j, range(FB))


_INS = ['L0_attn_x', 'L0_attn_W_in', 'L0_attn_conv_w', 'L0_attn_conv_b', 'L0_attn_A_param', 'L0_attn_dt_bias',
        'L0_attn_W_out', 'L0_ffn_W1', 'L0_ffn_b1', 'L0_ffn_W2', 'L0_ffn_b2', 'L1_attn_Wqk', 'L1_attn_Wv',
        'L1_attn_Wo', 'L1_attn_tau', 'L1_ffn_wg', 'L1_ffn_w1', 'L1_ffn_b1', 'L1_ffn_w2', 'L1_ffn_b2']


def kernel(**inputs):
    import numpy as np
    import concourse.bacc as bacc
    from concourse.bass_utils import run_bass_kernel_spmd

    nc = bacc.Bacc("TRN2", target_bir_lowering=False, num_devices=1)
    arrays, args = {}, []
    for name in _INS:
        a = np.ascontiguousarray(inputs[name])
        arrays[f"in_{name}"] = a
        args.append(nc.dram_tensor(f"in_{name}", a.shape, mybir.dt.from_np(a.dtype), kind="ExternalInput").ap())
    args.append(nc.dram_tensor("out", (B, S, D), F32, kind="ExternalOutput").ap())
    build_program(nc, *args)
    return run_bass_kernel_spmd(nc, [arrays], core_ids=[0]).results[0]["out"]
```
